# Optimizing a Trainium2 kernel written in Bass

```python
import numpy as np
import jax
import jax.numpy as jnp

def _softmax(x, axis=-1):
    return jax.nn.softmax(x, axis=axis)

def _gelu(x):
    return jax.nn.gelu(x, approximate=True)

def _silu(x):
    return jax.nn.silu(x)

def _sigmoid(x):
    return jax.nn.sigmoid(x)

def _layernorm(x, axis=-1, eps=1e-05):
    m = jnp.mean(x, axis=axis, keepdims=True)
    v = jnp.var(x, axis=axis, keepdims=True)
    return (x - m) / jnp.sqrt(v + eps)

def _scatter_add(tgt, idx, src, axis=0):
    return tgt.at[idx].add(src)

def _segment_sum(src, seg, n):
    return jax.ops.segment_sum(src, seg, n)
kernel_name = 'mk_gnn_resnorm_d4_gnn_r32_81849a'

def setup_inputs(seed: int=0):
    np.random.seed(seed)
    _w = jnp.asarray

    def _rec_inputs():
        import jax
        import jax.numpy as jnp
        _gk = jax.random.key(seed)
        x = -0.000202 + 1 * jax.random.normal(jax.random.fold_in(_gk, 1), (50000, 160), jnp.float32)
        src = jax.random.randint(jax.random.fold_in(_gk, 2), (50000,), 0, 50000, jnp.int32)
        dst = jax.random.randint(jax.random.fold_in(_gk, 3), (50000,), 0, 50000, jnp.int32)
        _o = jnp.argsort(dst, stable=True)
        src = src[_o]
        dst = dst[_o]
        edge_attr_16 = 6.40344e-05 + 1.00026 * jax.random.normal(jax.random.fold_in(_gk, 12), (50000, 16), jnp.float32)
        edge_attr_4 = 0.0012443 + 1.0001 * jax.random.normal(jax.random.fold_in(_gk, 13), (50000, 4), jnp.float32)
        edge_attr_64 = 0.000127647 + 1.00004 * jax.random.normal(jax.random.fold_in(_gk, 14), (50000, 64), jnp.float32)
        node_vec1 = jax.random.uniform(jax.random.fold_in(_gk, 16), (50000, 1), jnp.float32, 0.0, 1)
        return (x, src, dst, edge_attr_16, edge_attr_4, edge_attr_64, node_vec1)
    x, src, dst, edge_attr_16, edge_attr_4, edge_attr_64, node_vec1 = _rec_inputs()

    def _L0_gnn_setup():
        import jax, jax.numpy as jnp
        import numpy as np
        N, E = (1250, 20000)
        S_IN, V_IN = (64, 32)
        S_MID, V_MID = (96, 128)
        S_OUT, V_OUT = (96, 32)
        R = 64
        FC_HID = 64
        W_NUMEL = 64 + 64 + 32 + 32 + 32
        NUM_NEIGHBORS = 16.0

        def _inv(d):
            return 1.0 / jnp.sqrt(jnp.float32(d))

        def _forward(node_features, node_attr, edge_attr, edge_scalars, lin1_ws, lin1_wv, fc_w1, fc_w2, sc_ws, sc_wv, lin2_ws, lin2_wv, edge_src, edge_dst):
            n = node_features.shape[0]
            s = node_features[:, :S_IN]
            v = node_features[:, S_IN:].reshape(n, V_IN, 3)
            a = node_attr
            sc_s = s @ sc_ws * a * _inv(S_IN)
            sc_v = jnp.einsum('nci,cd->ndi', v, sc_wv) * a[:, :, None] * _inv(V_IN)
            h_s = s @ lin1_ws * a * _inv(S_IN)
            h_v = jnp.einsum('nci,cd->ndi', v, lin1_wv) * a[:, :, None] * _inv(V_IN)
            hid = jax.nn.silu(edge_scalars @ fc_w1 * _inv(R))
            w = hid @ fc_w2 * _inv(FC_HID)
            w1, w2, w3, w4, w5 = jnp.split(w, [64, 128, 160, 192], axis=-1)
            es = h_s[edge_src]
            ev = h_v[edge_src]
            e0 = edge_attr[:, :1]
            e1 = edge_attr[:, 1:4]
            m_s1 = w1 * es * e0
            m_s2 = w4 * jnp.einsum('eci,ei->ec', ev, e1) * _inv(3)
            m_v1 = (w2 * es)[:, :, None] * e1[:, None, :]
            m_v2 = w3[:, :, None] * ev * e0[:, :, None]
            m_v3 = w5[:, :, None] * jnp.cross(ev, e1[:, None, :]) * _inv(2)
            mid_s = jnp.concatenate([m_s1, m_s2], axis=-1)
            mid_v = jnp.concatenate([m_v1, m_v2, m_v3], axis=1)
            inv_nn = 1.0 / jnp.sqrt(jnp.float32(NUM_NEIGHBORS))
            agg_s = jax.ops.segment_sum(mid_s, edge_dst, num_segments=n) * inv_nn
            agg_v = jax.ops.segment_sum(mid_v, edge_dst, num_segments=n) * inv_nn
            o_s = agg_s @ lin2_ws * a * _inv(S_MID)
            o_v = jnp.einsum('nci,cd->ndi', agg_v, lin2_wv) * a[:, :, None] * _inv(V_MID)
            pre_s = sc_s + o_s
            pre_v = sc_v + o_v
            scalars = jax.nn.silu(pre_s[:, :64])
            gates = jax.nn.sigmoid(pre_s[:, 64:96])
            gated = gates[:, :, None] * pre_v
            return jnp.concatenate([scalars, gated.reshape(n, 3 * V_OUT)], axis=-1)
        key = jax.random.key(seed)
        ks = jax.random.split(key, 13)
        return {'node_features': jax.random.normal(ks[0], (N, S_IN + 3 * V_IN), jnp.float32), 'node_attr': jnp.ones((N, 1), jnp.float32), 'edge_src': jax.random.randint(ks[1], (E,), 0, N), 'edge_dst': jax.random.randint(ks[2], (E,), 0, N), 'edge_attr': jax.random.normal(ks[3], (E, 4), jnp.float32), 'edge_scalars': jax.random.normal(ks[4], (E, R), jnp.float32), 'lin1_ws': jax.random.normal(ks[5], (S_IN, S_IN), jnp.float32), 'lin1_wv': jax.random.normal(ks[6], (V_IN, V_IN), jnp.float32), 'fc_w1': jax.random.normal(ks[7], (R, FC_HID), jnp.float32), 'fc_w2': jax.random.normal(ks[8], (FC_HID, W_NUMEL), jnp.float32), 'sc_ws': jax.random.normal(ks[9], (S_IN, S_OUT), jnp.float32), 'sc_wv': jax.random.normal(ks[10], (V_IN, V_OUT), jnp.float32), 'lin2_ws': jax.random.normal(ks[11], (S_MID, S_OUT), jnp.float32), 'lin2_wv': jax.random.normal(ks[12], (V_MID, V_OUT), jnp.float32)}
    _L0_gnn_all = _L0_gnn_setup()
    _L0_gnn_in = {k: v for k, v in _L0_gnn_all.items() if k in ('lin1_ws', 'lin1_wv', 'fc_w1', 'fc_w2', 'sc_ws', 'sc_wv', 'lin2_ws', 'lin2_wv')}
    del _L0_gnn_all

    def _L1_gnn_setup():
        import jax, jax.numpy as jnp
        import numpy as np
        N_NODES = 3125
        N_EDGES = 25000
        MUL_S = 64
        MUL_V = 32
        DIM = MUL_S + 3 * MUL_V
        EDGE_SCALAR_DIM = 16
        ISQ3 = 1.0 / np.sqrt(3.0)
        ISQ2 = 1.0 / np.sqrt(2.0)

        def _forward(x, edge_index, edge_feat, edge_scalars, W_ss, W_sv, W_vs, W_vv, W_rad, b_rad, L_s, L_v):
            src, dst = (edge_index[0], edge_index[1])
            n = x.shape[0]
            xs = x[:, :MUL_S]
            xv = x[:, MUL_S:].reshape(n, MUL_V, 3)
            xs_e = xs[src]
            xv_e = xv[src]
            es = edge_feat[:, 0]
            ev = edge_feat[:, 1:4]
            out_s = (jnp.einsum('eu,uo->eo', xs_e * es[:, None], W_ss) / np.sqrt(MUL_S) + jnp.einsum('eud,ed,uo->eo', xv_e, ev, W_vv) * ISQ3 / np.sqrt(MUL_V)) * ISQ2
            out_v = (jnp.einsum('eu,ed,uv->evd', xs_e, ev, W_sv) * ISQ3 / np.sqrt(MUL_S) + jnp.einsum('eud,e,uv->evd', xv_e, es, W_vs) * ISQ3 / np.sqrt(MUL_V)) * ISQ2
            messages = jnp.concatenate([out_s, out_v.reshape(-1, 3 * MUL_V)], axis=1)
            scale = jax.nn.sigmoid(edge_scalars @ W_rad.T + b_rad)
            messages = messages * scale
            agg = jax.ops.segment_sum(messages, dst, num_segments=n)
            h = x + agg
            hs = h[:, :MUL_S]
            hv = h[:, MUL_S:].reshape(n, MUL_V, 3)
            ys = hs @ L_s / np.sqrt(MUL_S)
            yv = jnp.einsum('nud,uv->nvd', hv, L_v) / np.sqrt(MUL_V)
            return jnp.concatenate([ys, yv.reshape(n, 3 * MUL_V)], axis=1)
        key = jax.random.key(seed)
        ks = jax.random.split(key, 12)
        x = jax.random.normal(ks[0], (N_NODES, DIM), dtype=jnp.float32)
        edge_index = jax.random.randint(ks[1], (2, N_EDGES), 0, N_NODES, dtype=jnp.int64)
        edge_feat = jax.random.normal(ks[2], (N_EDGES, 4), dtype=jnp.float32)
        edge_scalars = jax.random.normal(ks[3], (N_EDGES, EDGE_SCALAR_DIM), dtype=jnp.float32)
        W_ss = jax.random.normal(ks[4], (MUL_S, MUL_S), dtype=jnp.float32)
        W_sv = jax.random.normal(ks[5], (MUL_S, MUL_V), dtype=jnp.float32)
        W_vs = jax.random.normal(ks[6], (MUL_V, MUL_V), dtype=jnp.float32)
        W_vv = jax.random.normal(ks[7], (MUL_V, MUL_S), dtype=jnp.float32)
        W_rad = jax.random.normal(ks[8], (DIM, EDGE_SCALAR_DIM), dtype=jnp.float32) / np.sqrt(EDGE_SCALAR_DIM)
        b_rad = jax.random.normal(ks[9], (DIM,), dtype=jnp.float32) * 0.1
        L_s = jax.random.normal(ks[10], (MUL_S, MUL_S), dtype=jnp.float32)
        L_v = jax.random.normal(ks[11], (MUL_V, MUL_V), dtype=jnp.float32)
        return {'x': x, 'edge_index': edge_index, 'edge_feat': edge_feat, 'edge_scalars': edge_scalars, 'W_ss': W_ss, 'W_sv': W_sv, 'W_vs': W_vs, 'W_vv': W_vv, 'W_rad': W_rad, 'b_rad': b_rad, 'L_s': L_s, 'L_v': L_v}
    _L1_gnn_all = _L1_gnn_setup()
    _L1_gnn_in = {k: v for k, v in _L1_gnn_all.items() if k in ('W_ss', 'W_sv', 'W_vs', 'W_vv', 'W_rad', 'b_rad', 'L_s', 'L_v')}
    del _L1_gnn_all

    def _L2_gnn_setup():
        import jax, jax.numpy as jnp
        import numpy as np
        N = 625
        E = 10000
        MUL0 = 64
        MUL1 = 32
        FC_IN = 16
        FC_H = 64
        WNUM = 192
        key = jax.random.key(seed)
        ks = jax.random.split(key, 16)
        return {'x': jax.random.normal(ks[0], (N, MUL0 + 3 * MUL1), jnp.float32), 'node_attr': jnp.ones((N, 1), jnp.float32), 'edge_scalars': jax.random.normal(ks[1], (E, FC_IN), jnp.float32), 'edge_attr_sh': jax.random.normal(ks[2], (E, 4), jnp.float32), 'edge_src': jax.random.randint(ks[3], (E,), 0, N), 'edge_dst': jax.random.randint(ks[4], (E,), 0, N), 'Wfc1': jax.random.normal(ks[5], (FC_IN, FC_H), jnp.float32), 'Wfc2': jax.random.normal(ks[6], (FC_H, WNUM), jnp.float32), 'Wsc0': jax.random.normal(ks[7], (MUL0, MUL0), jnp.float32), 'Wsc1': jax.random.normal(ks[8], (MUL1, MUL1), jnp.float32), 'Wl1_0': jax.random.normal(ks[9], (MUL0, MUL0), jnp.float32), 'Wl1_1': jax.random.normal(ks[10], (MUL1, MUL1), jnp.float32), 'Wl2_s': jax.random.normal(ks[11], (MUL0 + MUL1, MUL0), jnp.float32), 'Wl2_v': jax.random.normal(ks[12], (MUL0 + MUL1, MUL1), jnp.float32), 'Wa': 0.1 * jax.random.normal(ks[13], (MUL0 + MUL1, 1), jnp.float32)}
    _L2_gnn_all = _L2_gnn_setup()
    _L2_gnn_in = {k: v for k, v in _L2_gnn_all.items() if k in ('Wfc1', 'Wfc2', 'Wsc0', 'Wsc1', 'Wl1_0', 'Wl1_1', 'Wl2_s', 'Wl2_v', 'Wa')}
    del _L2_gnn_all

    def _L3_gnn_setup():
        import jax, jax.numpy as jnp
        import numpy as np
        N, E = (625, 10000)
        CS, CV = (64, 32)
        AS_, AV, H = (16, 8, 4)
        NB = 16
        SQRT3 = 1.7320508075688772
        SQRT2 = 1.4142135623730951
        EPS = 1e-05

        def _cg_tp(s, v, y0, y1, w_ss, w_sv, w_vs, w_vv0, w_vv1):
            out_s = jnp.concatenate([w_ss * s * y0[:, None], w_vv0 * (jnp.einsum('eci,ei->ec', v, y1) / SQRT3)], axis=-1)
            out_v = jnp.concatenate([(w_sv * s)[:, :, None] * y1[:, None, :], (w_vs * jnp.ones_like(v[..., 0]))[..., None] * v * y0[:, None, None], (w_vv1 * jnp.ones_like(v[..., 0]))[..., None] * (jnp.cross(v, y1[:, None, :]) / SQRT2)], axis=1)
            return (out_s, out_v)

        def _equiv_layernorm(s, v, gamma_s, beta_s, gamma_v):
            mu = jnp.mean(s, axis=-1, keepdims=True)
            var = jnp.var(s, axis=-1, keepdims=True)
            s_n = (s - mu) * jax.lax.rsqrt(var + EPS) * gamma_s + beta_s
            rms = jnp.sqrt(jnp.mean(jnp.sum(v * v, axis=-1), axis=-1, keepdims=True) + EPS)
            v_n = v / rms[..., None] * gamma_v[None, :, None]
            return (s_n, v_n)
        key = jax.random.key(seed)
        ks = jax.random.split(key, 26)

        def rn(k, shape, fan):
            return jax.random.normal(k, shape, jnp.float32) / np.sqrt(fan)
        D1S, D1V = (CS + CV, CS + 2 * CV)
        WN = 2 * CS + 3 * CV
        inp = {'node': jax.random.normal(ks[0], (N, CS + 3 * CV), jnp.float32), 'edge_index': jax.random.randint(ks[1], (2, E), 0, N, jnp.int64 if jax.config.jax_enable_x64 else jnp.int32), 'rbf': jax.random.uniform(ks[2], (E, NB), jnp.float32), 'rsh': jax.random.normal(ks[3], (E, 4), jnp.float32), 'gamma_s': jnp.ones((CS,), jnp.float32), 'beta_s': jnp.zeros((CS,), jnp.float32), 'gamma_v': jnp.ones((CV,), jnp.float32), 'Ws_src': rn(ks[4], (CS, CS), CS), 'Wv_src': rn(ks[5], (CV, CV), CV), 'Ws_dst': rn(ks[6], (CS, CS), CS), 'Wv_dst': rn(ks[7], (CV, CV), CV), 'W_rbf': rn(ks[8], (NB, WN), NB), 'W_alpha': rn(ks[9], (D1S, H * AS_), D1S), 'alpha_dot': rn(ks[10], (1, H, AS_), AS_), 'Ws_val': rn(ks[11], (D1S, CS), D1S), 'Wv_val': rn(ks[12], (D1V, CV), D1V), 'Wg': rn(ks[13], (CS, CV), CS), 'w2_ss': rn(ks[14], (CS,), 1), 'w2_sv': rn(ks[15], (CS,), 1), 'w2_vs': rn(ks[16], (CV,), 1), 'w2_vv0': rn(ks[17], (CV,), 1), 'w2_vv1': rn(ks[18], (CV,), 1), 'Ws_vlin': rn(ks[19], (D1S, H * AS_), D1S), 'Wv_vlin': rn(ks[20], (D1V, H * AV), D1V), 'Wps': rn(ks[21], (H * AS_, CS), H * AS_), 'Wpv': rn(ks[22], (H * AV, CV), H * AV)}
        return inp
    _L3_gnn_all = _L3_gnn_setup()
    _L3_gnn_in = {k: v for k, v in _L3_gnn_all.items() if k in ('gamma_s', 'beta_s', 'gamma_v', 'Ws_src', 'Wv_src', 'Ws_dst', 'Wv_dst', 'W_rbf', 'W_alpha', 'alpha_dot', 'Ws_val', 'Wv_val', 'Wg', 'w2_ss', 'w2_sv', 'w2_vs', 'w2_vv0', 'w2_vv1', 'Ws_vlin', 'Wv_vlin', 'Wps', 'Wpv')}
    del _L3_gnn_all
    return {'x': x, 'src': src, 'dst': dst, 'edge_attr_16': edge_attr_16, 'edge_attr_4': edge_attr_4, 'edge_attr_64': edge_attr_64, 'node_vec1': node_vec1, 'L0_gnn_lin1_ws': _L0_gnn_in['lin1_ws'], 'L0_gnn_lin1_wv': _L0_gnn_in['lin1_wv'], 'L0_gnn_fc_w1': _L0_gnn_in['fc_w1'], 'L0_gnn_fc_w2': _L0_gnn_in['fc_w2'], 'L0_gnn_sc_ws': _L0_gnn_in['sc_ws'], 'L0_gnn_sc_wv': _L0_gnn_in['sc_wv'], 'L0_gnn_lin2_ws': _L0_gnn_in['lin2_ws'], 'L0_gnn_lin2_wv': _L0_gnn_in['lin2_wv'], 'L1_gnn_W_ss': _L1_gnn_in['W_ss'], 'L1_gnn_W_sv': _L1_gnn_in['W_sv'], 'L1_gnn_W_vs': _L1_gnn_in['W_vs'], 'L1_gnn_W_vv': _L1_gnn_in['W_vv'], 'L1_gnn_W_rad': _L1_gnn_in['W_rad'], 'L1_gnn_b_rad': _L1_gnn_in['b_rad'], 'L1_gnn_L_s': _L1_gnn_in['L_s'], 'L1_gnn_L_v': _L1_gnn_in['L_v'], 'L2_gnn_Wfc1': _L2_gnn_in['Wfc1'], 'L2_gnn_Wfc2': _L2_gnn_in['Wfc2'], 'L2_gnn_Wsc0': _L2_gnn_in['Wsc0'], 'L2_gnn_Wsc1': _L2_gnn_in['Wsc1'], 'L2_gnn_Wl1_0': _L2_gnn_in['Wl1_0'], 'L2_gnn_Wl1_1': _L2_gnn_in['Wl1_1'], 'L2_gnn_Wl2_s': _L2_gnn_in['Wl2_s'], 'L2_gnn_Wl2_v': _L2_gnn_in['Wl2_v'], 'L2_gnn_Wa': _L2_gnn_in['Wa'], 'L3_gnn_gamma_s': _L3_gnn_in['gamma_s'], 'L3_gnn_beta_s': _L3_gnn_in['beta_s'], 'L3_gnn_gamma_v': _L3_gnn_in['gamma_v'], 'L3_gnn_Ws_src': _L3_gnn_in['Ws_src'], 'L3_gnn_Wv_src': _L3_gnn_in['Wv_src'], 'L3_gnn_Ws_dst': _L3_gnn_in['Ws_dst'], 'L3_gnn_Wv_dst': _L3_gnn_in['Wv_dst'], 'L3_gnn_W_rbf': _L3_gnn_in['W_rbf'], 'L3_gnn_W_alpha': _L3_gnn_in['W_alpha'], 'L3_gnn_alpha_dot': _L3_gnn_in['alpha_dot'], 'L3_gnn_Ws_val': _L3_gnn_in['Ws_val'], 'L3_gnn_Wv_val': _L3_gnn_in['Wv_val'], 'L3_gnn_Wg': _L3_gnn_in['Wg'], 'L3_gnn_w2_ss': _L3_gnn_in['w2_ss'], 'L3_gnn_w2_sv': _L3_gnn_in['w2_sv'], 'L3_gnn_w2_vs': _L3_gnn_in['w2_vs'], 'L3_gnn_w2_vv0': _L3_gnn_in['w2_vv0'], 'L3_gnn_w2_vv1': _L3_gnn_in['w2_vv1'], 'L3_gnn_Ws_vlin': _L3_gnn_in['Ws_vlin'], 'L3_gnn_Wv_vlin': _L3_gnn_in['Wv_vlin'], 'L3_gnn_Wps': _L3_gnn_in['Wps'], 'L3_gnn_Wpv': _L3_gnn_in['Wpv']}

def reference(x, src, dst, edge_attr_16, edge_attr_4, edge_attr_64, node_vec1, L0_gnn_lin1_ws, L0_gnn_lin1_wv, L0_gnn_fc_w1, L0_gnn_fc_w2, L0_gnn_sc_ws, L0_gnn_sc_wv, L0_gnn_lin2_ws, L0_gnn_lin2_wv, L1_gnn_W_ss, L1_gnn_W_sv, L1_gnn_W_vs, L1_gnn_W_vv, L1_gnn_W_rad, L1_gnn_b_rad, L1_gnn_L_s, L1_gnn_L_v, L2_gnn_Wfc1, L2_gnn_Wfc2, L2_gnn_Wsc0, L2_gnn_Wsc1, L2_gnn_Wl1_0, L2_gnn_Wl1_1, L2_gnn_Wl2_s, L2_gnn_Wl2_v, L2_gnn_Wa, L3_gnn_gamma_s, L3_gnn_beta_s, L3_gnn_gamma_v, L3_gnn_Ws_src, L3_gnn_Wv_src, L3_gnn_Ws_dst, L3_gnn_Wv_dst, L3_gnn_W_rbf, L3_gnn_W_alpha, L3_gnn_alpha_dot, L3_gnn_Ws_val, L3_gnn_Wv_val, L3_gnn_Wg, L3_gnn_w2_ss, L3_gnn_w2_sv, L3_gnn_w2_vs, L3_gnn_w2_vv0, L3_gnn_w2_vv1, L3_gnn_Ws_vlin, L3_gnn_Wv_vlin, L3_gnn_Wps, L3_gnn_Wpv):
    import jax
    import jax.numpy as jnp

    def _L0_gnn_ref(node_features, node_attr, edge_src, edge_dst, edge_attr, edge_scalars, lin1_ws, lin1_wv, fc_w1, fc_w2, sc_ws, sc_wv, lin2_ws, lin2_wv):
        import jax, jax.numpy as jnp
        import numpy as np
        N, E = (1250, 20000)
        S_IN, V_IN = (64, 32)
        S_MID, V_MID = (96, 128)
        S_OUT, V_OUT = (96, 32)
        R = 64
        FC_HID = 64
        W_NUMEL = 64 + 64 + 32 + 32 + 32
        NUM_NEIGHBORS = 16.0

        def _inv(d):
            return 1.0 / jnp.sqrt(jnp.float32(d))

        def _forward(node_features, node_attr, edge_attr, edge_scalars, lin1_ws, lin1_wv, fc_w1, fc_w2, sc_ws, sc_wv, lin2_ws, lin2_wv, edge_src, edge_dst):
            n = node_features.shape[0]
            s = node_features[:, :S_IN]
            v = node_features[:, S_IN:].reshape(n, V_IN, 3)
            a = node_attr
            sc_s = s @ sc_ws * a * _inv(S_IN)
            sc_v = jnp.einsum('nci,cd->ndi', v, sc_wv) * a[:, :, None] * _inv(V_IN)
            h_s = s @ lin1_ws * a * _inv(S_IN)
            h_v = jnp.einsum('nci,cd->ndi', v, lin1_wv) * a[:, :, None] * _inv(V_IN)
            hid = jax.nn.silu(edge_scalars @ fc_w1 * _inv(R))
            w = hid @ fc_w2 * _inv(FC_HID)
            w1, w2, w3, w4, w5 = jnp.split(w, [64, 128, 160, 192], axis=-1)
            es = h_s[edge_src]
            ev = h_v[edge_src]
            e0 = edge_attr[:, :1]
            e1 = edge_attr[:, 1:4]
            m_s1 = w1 * es * e0
            m_s2 = w4 * jnp.einsum('eci,ei->ec', ev, e1) * _inv(3)
            m_v1 = (w2 * es)[:, :, None] * e1[:, None, :]
            m_v2 = w3[:, :, None] * ev * e0[:, :, None]
            m_v3 = w5[:, :, None] * jnp.cross(ev, e1[:, None, :]) * _inv(2)
            mid_s = jnp.concatenate([m_s1, m_s2], axis=-1)
            mid_v = jnp.concatenate([m_v1, m_v2, m_v3], axis=1)
            inv_nn = 1.0 / jnp.sqrt(jnp.float32(NUM_NEIGHBORS))
            agg_s = jax.ops.segment_sum(mid_s, edge_dst, num_segments=n) * inv_nn
            agg_v = jax.ops.segment_sum(mid_v, edge_dst, num_segments=n) * inv_nn
            o_s = agg_s @ lin2_ws * a * _inv(S_MID)
            o_v = jnp.einsum('nci,cd->ndi', agg_v, lin2_wv) * a[:, :, None] * _inv(V_MID)
            pre_s = sc_s + o_s
            pre_v = sc_v + o_v
            scalars = jax.nn.silu(pre_s[:, :64])
            gates = jax.nn.sigmoid(pre_s[:, 64:96])
            gated = gates[:, :, None] * pre_v
            return jnp.concatenate([scalars, gated.reshape(n, 3 * V_OUT)], axis=-1)
        return _forward(node_features, node_attr, edge_attr, edge_scalars, lin1_ws, lin1_wv, fc_w1, fc_w2, sc_ws, sc_wv, lin2_ws, lin2_wv, edge_src, edge_dst)

    def _L1_gnn_ref(x, edge_index, edge_feat, edge_scalars, W_ss, W_sv, W_vs, W_vv, W_rad, b_rad, L_s, L_v):
        import jax, jax.numpy as jnp
        import numpy as np
        N_NODES = 3125
        N_EDGES = 25000
        MUL_S = 64
        MUL_V = 32
        DIM = MUL_S + 3 * MUL_V
        EDGE_SCALAR_DIM = 16
        ISQ3 = 1.0 / np.sqrt(3.0)
        ISQ2 = 1.0 / np.sqrt(2.0)

        def _forward(x, edge_index, edge_feat, edge_scalars, W_ss, W_sv, W_vs, W_vv, W_rad, b_rad, L_s, L_v):
            src, dst = (edge_index[0], edge_index[1])
            n = x.shape[0]
            xs = x[:, :MUL_S]
            xv = x[:, MUL_S:].reshape(n, MUL_V, 3)
            xs_e = xs[src]
            xv_e = xv[src]
            es = edge_feat[:, 0]
            ev = edge_feat[:, 1:4]
            out_s = (jnp.einsum('eu,uo->eo', xs_e * es[:, None], W_ss) / np.sqrt(MUL_S) + jnp.einsum('eud,ed,uo->eo', xv_e, ev, W_vv) * ISQ3 / np.sqrt(MUL_V)) * ISQ2
            out_v = (jnp.einsum('eu,ed,uv->evd', xs_e, ev, W_sv) * ISQ3 / np.sqrt(MUL_S) + jnp.einsum('eud,e,uv->evd', xv_e, es, W_vs) * ISQ3 / np.sqrt(MUL_V)) * ISQ2
            messages = jnp.concatenate([out_s, out_v.reshape(-1, 3 * MUL_V)], axis=1)
            scale = jax.nn.sigmoid(edge_scalars @ W_rad.T + b_rad)
            messages = messages * scale
            agg = jax.ops.segment_sum(messages, dst, num_segments=n)
            h = x + agg
            hs = h[:, :MUL_S]
            hv = h[:, MUL_S:].reshape(n, MUL_V, 3)
            ys = hs @ L_s / np.sqrt(MUL_S)
            yv = jnp.einsum('nud,uv->nvd', hv, L_v) / np.sqrt(MUL_V)
            return jnp.concatenate([ys, yv.reshape(n, 3 * MUL_V)], axis=1)
        return _forward(x, edge_index, edge_feat, edge_scalars, W_ss, W_sv, W_vs, W_vv, W_rad, b_rad, L_s, L_v)

    def _L2_gnn_ref(x, node_attr, edge_scalars, edge_attr_sh, edge_src, edge_dst, Wfc1, Wfc2, Wsc0, Wsc1, Wl1_0, Wl1_1, Wl2_s, Wl2_v, Wa):
        import jax, jax.numpy as jnp
        import numpy as np
        N = 625
        E = 10000
        MUL0 = 64
        MUL1 = 32
        FC_IN = 16
        FC_H = 64
        WNUM = 192
        n = x.shape[0]
        x0 = x[:, :MUL0]
        x1 = x[:, MUL0:].reshape(n, MUL1, 3)
        a = node_attr
        h = jax.nn.silu(edge_scalars @ (Wfc1 / jnp.sqrt(jnp.float32(FC_IN))))
        w = h @ (Wfc2 / jnp.sqrt(jnp.float32(FC_H)))
        w0 = w[:, :64]
        w1 = w[:, 64:128]
        w2 = w[:, 128:160]
        w3 = w[:, 160:192]
        inv8 = 1.0 / jnp.sqrt(jnp.float32(MUL0))
        inv32 = 1.0 / jnp.sqrt(jnp.float32(MUL1))
        sc = jnp.concatenate([x0 @ Wsc0 * a * inv8, (jnp.einsum('num,uv->nvm', x1, Wsc1) * a[..., None] * inv32).reshape(n, 3 * MUL1)], axis=1)
        f0 = x0 @ Wl1_0 * a * inv8
        f1 = jnp.einsum('num,uv->nvm', x1, Wl1_1) * a[..., None] * inv32
        e0 = f0[edge_src]
        e1 = f1[edge_src]
        sh0 = edge_attr_sh[:, :1]
        sh1 = edge_attr_sh[:, 1:4]
        mid0 = w0 * e0 * sh0
        mid1 = w3 * jnp.einsum('eum,em->eu', e1, sh1) / jnp.sqrt(3.0)
        mid2 = w1[:, :, None] * e0[:, :, None] * sh1[:, None, :]
        mid3 = w2[:, :, None] * e1 * sh0[:, :, None]
        cnt = jnp.clip(jax.ops.segment_sum(jnp.ones(edge_dst.shape, x.dtype), edge_dst, num_segments=n), 1.0)

        def smean(v):
            s = jax.ops.segment_sum(v, edge_dst, num_segments=n)
            return s / cnt.reshape((n,) + (1,) * (v.ndim - 1))
        n0, n1 = (smean(mid0), smean(mid1))
        n2, n3 = (smean(mid2), smean(mid3))
        scal = jnp.concatenate([n0, n1], axis=1)
        vec = jnp.concatenate([n2, n3], axis=1)
        inv96 = 1.0 / jnp.sqrt(jnp.float32(MUL0 + MUL1))
        alpha = scal @ Wa * a * inv96
        out_s = scal @ Wl2_s * a * inv96
        out_v = jnp.einsum('num,uv->nvm', vec, Wl2_v) * a[..., None] * inv96
        conv = jnp.concatenate([out_s, out_v.reshape(n, 3 * MUL1)], axis=1)
        return sc + alpha * conv

    def _L3_gnn_ref(node, rbf, rsh, gamma_s, beta_s, gamma_v, Ws_src, Wv_src, Ws_dst, Wv_dst, W_rbf, W_alpha, alpha_dot, Ws_val, Wv_val, Wg, w2_ss, w2_sv, w2_vs, w2_vv0, w2_vv1, Ws_vlin, Wv_vlin, Wps, Wpv, edge_index):
        import jax, jax.numpy as jnp
        import numpy as np
        N, E = (625, 10000)
        CS, CV = (64, 32)
        AS_, AV, H = (16, 8, 4)
        NB = 16
        SQRT3 = 1.7320508075688772
        SQRT2 = 1.4142135623730951
        EPS = 1e-05

        def _cg_tp(s, v, y0, y1, w_ss, w_sv, w_vs, w_vv0, w_vv1):
            out_s = jnp.concatenate([w_ss * s * y0[:, None], w_vv0 * (jnp.einsum('eci,ei->ec', v, y1) / SQRT3)], axis=-1)
            out_v = jnp.concatenate([(w_sv * s)[:, :, None] * y1[:, None, :], (w_vs * jnp.ones_like(v[..., 0]))[..., None] * v * y0[:, None, None], (w_vv1 * jnp.ones_like(v[..., 0]))[..., None] * (jnp.cross(v, y1[:, None, :]) / SQRT2)], axis=1)
            return (out_s, out_v)

        def _equiv_layernorm(s, v, gamma_s, beta_s, gamma_v):
            mu = jnp.mean(s, axis=-1, keepdims=True)
            var = jnp.var(s, axis=-1, keepdims=True)
            s_n = (s - mu) * jax.lax.rsqrt(var + EPS) * gamma_s + beta_s
            rms = jnp.sqrt(jnp.mean(jnp.sum(v * v, axis=-1), axis=-1, keepdims=True) + EPS)
            v_n = v / rms[..., None] * gamma_v[None, :, None]
            return (s_n, v_n)
        n = node.shape[0]
        e = rsh.shape[0]
        s = node[:, :CS]
        v = node[:, CS:].reshape(n, CV, 3)
        s_n, v_n = _equiv_layernorm(s, v, gamma_s, beta_s, gamma_v)
        src, dst = (edge_index[0], edge_index[1])
        msg_s = (s_n @ Ws_src)[src] + (s_n @ Ws_dst)[dst]
        msg_v = jnp.einsum('ncx,cd->ndx', v_n, Wv_src)[src] + jnp.einsum('ncx,cd->ndx', v_n, Wv_dst)[dst]
        y0, y1 = (rsh[:, 0], rsh[:, 1:4])
        w1 = rbf @ W_rbf
        m1_s, m1_v = _cg_tp(msg_s, msg_v, y0, y1, w1[:, :CS], w1[:, CS:2 * CS], w1[:, 2 * CS:2 * CS + CV], w1[:, 2 * CS + CV:2 * CS + 2 * CV], w1[:, 2 * CS + 2 * CV:])
        a = (m1_s @ W_alpha).reshape(e, H, AS_)
        a = jnp.where(a > 0, a, 0.2 * a)
        a = jnp.sum(a * alpha_dot, axis=-1, keepdims=True)
        amax = jax.ops.segment_max(a, dst, num_segments=n)
        amax = jnp.where(jnp.isfinite(amax), amax, 0.0)
        ex = jnp.exp(a - amax[dst])
        den = jax.ops.segment_sum(ex, dst, num_segments=n)
        alpha = ex / (den[dst] + 1e-16)
        val_s = m1_s @ Ws_val
        val_v = jnp.einsum('ecx,cd->edx', m1_v, Wv_val)
        val_v = val_v * jax.nn.sigmoid(val_s @ Wg)[..., None]
        val_s = jax.nn.sigmoid(val_s)
        m2_s, m2_v = _cg_tp(val_s, val_v, y0, y1, w2_ss, w2_sv, w2_vs, w2_vv0, w2_vv1)
        hs = (m2_s @ Ws_vlin).reshape(e, H, AS_)
        hv = jnp.einsum('ecx,cd->edx', m2_v, Wv_vlin).reshape(e, H, AV, 3)
        h = jnp.concatenate([hs, hv.reshape(e, H, AV * 3)], axis=-1)
        agg = jax.ops.segment_sum(alpha * h, dst, num_segments=n)
        agg_s = agg[:, :, :AS_].reshape(n, H * AS_)
        agg_v = agg[:, :, AS_:].reshape(n, H * AV, 3)
        out = node + jnp.concatenate([agg_s @ Wps, jnp.einsum('ncx,cd->ndx', agg_v, Wpv).reshape(n, CV * 3)], axis=-1)
        return out
    edge_index = jnp.stack([src, dst])
    x = _layernorm(x + _L0_gnn_ref(x, node_vec1, src, dst, edge_attr_4, edge_attr_64, L0_gnn_lin1_ws, L0_gnn_lin1_wv, L0_gnn_fc_w1, L0_gnn_fc_w2, L0_gnn_sc_ws, L0_gnn_sc_wv, L0_gnn_lin2_ws, L0_gnn_lin2_wv), axis=-1)
    x = _layernorm(x + _L1_gnn_ref(x, edge_index, edge_attr_4, edge_attr_16, L1_gnn_W_ss, L1_gnn_W_sv, L1_gnn_W_vs, L1_gnn_W_vv, L1_gnn_W_rad, L1_gnn_b_rad, L1_gnn_L_s, L1_gnn_L_v), axis=-1)
    x = _layernorm(x + _L2_gnn_ref(x, node_vec1, edge_attr_16, edge_attr_4, src, dst, L2_gnn_Wfc1, L2_gnn_Wfc2, L2_gnn_Wsc0, L2_gnn_Wsc1, L2_gnn_Wl1_0, L2_gnn_Wl1_1, L2_gnn_Wl2_s, L2_gnn_Wl2_v, L2_gnn_Wa), axis=-1)
    x = _layernorm(x + _L3_gnn_ref(x, edge_attr_16, edge_attr_4, L3_gnn_gamma_s, L3_gnn_beta_s, L3_gnn_gamma_v, L3_gnn_Ws_src, L3_gnn_Wv_src, L3_gnn_Ws_dst, L3_gnn_Wv_dst, L3_gnn_W_rbf, L3_gnn_W_alpha, L3_gnn_alpha_dot, L3_gnn_Ws_val, L3_gnn_Wv_val, L3_gnn_Wg, L3_gnn_w2_ss, L3_gnn_w2_sv, L3_gnn_w2_vs, L3_gnn_w2_vv0, L3_gnn_w2_vv1, L3_gnn_Ws_vlin, L3_gnn_Wv_vlin, L3_gnn_Wps, L3_gnn_Wpv, edge_index), axis=-1)
    return x

_drawn_inputs = setup_inputs


def setup_inputs(seed=0):
    import zlib

    import numpy as np

    out = dict(_drawn_inputs(seed))
    spreads = {'L3_gnn_gamma_s': (1.0, 0.2), 'L3_gnn_beta_s': (0.0, 0.401), 'L3_gnn_gamma_v': (1.0, 0.6)}
    factors = {'L0_gnn_lin1_ws': 3.089,
     'L0_gnn_lin1_wv': 3.581,
     'L0_gnn_lin2_ws': 3.44,
     'L0_gnn_lin2_wv': 3.26,
     'L1_gnn_b_rad': 5.32,
     'L2_gnn_Wfc1': 8.0,
     'L2_gnn_Wfc2': 8.0,
     'L2_gnn_Wl1_0': 8.0,
     'L2_gnn_Wl1_1': 8.0,
     'L2_gnn_Wl2_s': 8.0,
     'L2_gnn_Wl2_v': 8.0,
     'L2_gnn_Wa': 8.0}
    for name, (base, spread) in spreads.items():
        noise = np.random.default_rng([zlib.crc32(name.encode()), seed]).standard_normal(out[name].shape)
        drawn = base * np.exp(spread * noise) if base else spread * noise
        out[name] = jnp.asarray(drawn.astype(out[name].dtype))
    for name, factor in factors.items():
        out[name] = (out[name] * factor).astype(out[name].dtype)
    return out
```

```python
from contextlib import ExitStack

import numpy as np

import concourse.bass as bass
from concourse import mybir

F32 = mybir.dt.float32
I32 = mybir.dt.int32
ALU = mybir.AluOpType
ACT = mybir.ActivationFunctionType
AXX = mybir.AxisListType.X

P = 128
SUB = 4
STEP = P * SUB
NS, NV = 64, 32
D = NS + 3 * NV
SCR = 1 << 20
AGG_W = 192
EPS = 1e-5
HEADS = 4
BIG = 3.0e38


class Signals(dict):

    def __init__(self, nc, ctx):
        self.nc, self.ctx, self.kept = nc, ctx, []

    def __missing__(self, name):
        self[name] = self.ctx.enter_context(self.nc.semaphore(name))
        return self[name]


def reach(eng, sem, count):
    if isinstance(count, int) and count <= 0:
        return
    eng.wait_ge(sem, count)


def reach_gate(eng, sem, count, gate):
    if isinstance(count, int) and count <= 0:
        return
    eng.wait_ge(sem, count)
    eng.sem_inc(gate, 1)


def dma_count(t, p, each):
    if isinstance(t, int):
        return each * (t // 2 + 1) if t >= 0 else 0
    return (t - p) * (each // 2) + each


def rolled(eng, steps, stages):
    deep = max(lag for _, lag in stages)
    head = (deep + 3) // 2 * 2

    def one(s, k):
        for f, lag in stages:
            t = s + k - lag
            if isinstance(t, int) and not 0 <= t < steps:
                continue
            f(t, (k - lag) % 2)

    for s in range(head):
        one(0, s)
    with eng.Fori(head, steps - 1, 2) as i:
        one(i, 0)
        one(i, 1)
    for s in range(deep):
        one(steps, s)


class Program:

    def __init__(self, nc, d, steps, output, lasting):
        self.nc, self.d, self.T, self.output, self.lasting = nc, d, steps, output, lasting


def finish_pass(nc, sig):
    nc.all_engine_barrier()
    for name, sem in sig.items():
        if name not in sig.kept:
            nc.gpsimd.sem_clear(sem)
    nc.all_engine_barrier()


def weight_tile(pr, ctx, sig, name, cols, parts):
    tile = ctx.enter_context(pr.nc.sbuf_tensor(name, [P, cols], F32))

    def zero(pool):
        pool.memset(tile[:, :], 0.0).then_inc(sig["weights_zeroed"], 1)

    def load(sp):
        sp.wait_ge(sig["weights_zeroed"], 1)
        for r, c, ap, _ in parts:
            sp.dma_start(tile[r:r + ap.shape[0], c:c + ap.shape[1]], ap).then_inc(sig["weights_loaded"], 16)

    def scale(dve):
        dve.wait_ge(sig["weights_loaded"], 16 * len(parts))
        for r, c, ap, factor in parts:
            part = tile[r:r + ap.shape[0], c:c + ap.shape[1]]
            dve.tensor_scalar(part, part, float(factor), None, ALU.mult).then_inc(sig["weights_ready"], 1)

    return tile, zero, load, scale, len(parts)


def block_diagonal(c, ap, factor):
    n = ap.shape[1]
    return [(NV * i, c + n * i, ap, factor) for i in range(3)]


def prepare(pr):
    nc, T, pr.name = pr.nc, pr.T, "p"
    with ExitStack() as ctx:
        sig = Signals(nc, ctx)
        sb = lambda name, shape, dt=F32: ctx.enter_context(nc.sbuf_tensor(name, shape, dt))
        zeros = sb("zeros", [P, T * SUB * AGG_W // 12])
        same = sb("same_as_previous", [P, T, SUB])
        xs = [sb(f"p_xs{p}", [NS, STEP]) for p in range(2)]
        xv = [sb(f"p_xv{p}", [3 * NV, STEP]) for p in range(2)]
        hs = [sb(f"p_h{p}", [P, SUB, D]) for p in range(2)]
        acc = [ctx.enter_context(nc.psum_tensor(f"p_acc{p}", [P, SUB, 256], F32)) for p in range(2)]
        w, w_zero, w_load, w_scale, w_n = weight_tile(pr, ctx, sig, "p_w", D, [
            (0, 0, pr.d["L0_gnn_lin1_ws"], NS ** -0.5)] + block_diagonal(NS, pr.d["L0_gnn_lin1_wv"], NV ** -0.5))
        block = ctx.enter_context(nc.Block())
        agg_flat = pr.agg.rearrange("(p r) c -> p (r c)", p=P)
        piece = T * SUB * AGG_W // 12

        @block.gpsimd
        def _(pool):
            w_zero(pool)
            pool.memset(zeros[:, :], 0.0).then_inc(sig["zeros_made"], 1)

        @block.sync
        def _(sp):
            w_load(sp)
            sp.dma_start(pr.ident[:, :], pr.d["identity"]).then_inc(sig["resident"], 16)
            sp.dma_start(pr.index[:, :], pr.d["edge_index"]).then_inc(sig["resident"], 16)
            sp.dma_start(pr.edge4[:, :], pr.d["edge_attr_4"]).then_inc(sig["resident"], 16)
            sp.dma_start(pr.attr[:, :], pr.d["node_attr"]).then_inc(sig["resident"], 16)
            sp.wait_ge(sig["zeros_made"], 1)
            for k in range(12):
                sp.dma_start(agg_flat[:, k * piece:(k + 1) * piece], zeros[:, :]).then_inc(sig["agg_zeroed"], 16)

            def load(t, p):
                reach(sp, sig["h_product"], t - 1)
                sp.dma_start(xs[p][:, :], pr.d["xT"][0:NS, bass.ds(t * STEP, STEP)]).then_inc(sig[f"x_loaded{p}"], 16)
                sp.dma_start(xv[p][:, :], pr.d["xT"][NS:D, bass.ds(t * STEP, STEP)]).then_inc(sig[f"x_loaded{p}"], 16)

            rolled(sp, T, [(load, 0)])
            sp.wait_ge(sig["agg_zeroed"], 12 * 16)
            sp.wait_ge(sig["resident"], 4 * 16)

        @block.tensor
        def _(pe):
            pe.wait_ge(sig["weights_ready"], w_n)

            def product(t, p):
                reach(pe, sig[f"x_loaded{p}"], dma_count(t, p, 32))
                reach_gate(pe, sig["h_out"], t - 1, sig["pe_gate"])
                for j in range(SUB):
                    cols = slice(j * P, (j + 1) * P)
                    pe.matmul(acc[p][:, j, 0:NS], xs[p][:, cols], w[0:NS, 0:NS], start=True, stop=True)
                    mm = pe.matmul(acc[p][:, j, NS:D], xv[p][:, cols], w[0:3 * NV, NS:D], start=True, stop=True)
                mm.then_inc(sig["h_product"], 1)

            rolled(pe, T, [(product, 0)])

        @block.vector
        def _(dve):
            w_scale(dve)
            dve.wait_ge(sig["resident"], 4 * 16)
            index = pr.index[:, :].rearrange("p (t k j) -> p t k j", k=3, j=SUB)
            dve.tensor_tensor(same[:, :, :], index[:, :, 1, :], index[:, :, 2, :], ALU.is_equal).then_inc(sig["same"], 1)
            dve.wait_ge(sig["same"], 1)
            dve.scalar_tensor_tensor(out=index[:, :, 1, :], in0=same[:, :, :], scalar=float(SCR), in1=index[:, :, 2, :],
                                     op0=ALU.mult, op1=ALU.add).then_inc(sig["same"], 1)
            dve.tensor_copy(pr.dst_f[:, :].rearrange("p (t j) -> p t j", j=SUB), index[:, :, 2, :]).then_inc(sig["same"], 1)
            dve.wait_ge(sig["same"], 3)

            def out(t, p):
                reach(dve, sig["h_product"], t + 1)
                reach(dve, sig[f"h_stored{p}"], dma_count(t - 2, p, 16))
                dve.tensor_tensor(hs[p][:, :, :], acc[p][:, :, 0:D],
                                  pr.attr[:, bass.ds(t * SUB, SUB)].unsqueeze(2).to_broadcast([P, SUB, D]),
                                  ALU.mult).then_inc(sig["h_out"], 1)

            rolled(dve, T, [(out, 0)])

        @block.scalar
        def _(act):
            def store(t, p):
                reach(act, sig["h_out"], t + 1)
                act.dma_start(pr.rows(pr.table_a, t), hs[p][:, :, :].rearrange("p j c -> p (j c)")).then_inc(
                    sig[f"h_stored{p}"], 16)

            rolled(act, T, [(store, 0)])
            for p in range(2):
                act.wait_ge(sig[f"h_stored{p}"], 16 * (T // 2))

    finish_pass(nc, sig)


class EdgeCommon:

    def __init__(self, pr, ctx, sig, tables, width, rows_read, row_width=D, banks=2):
        nc = pr.nc
        self.pr, self.sig, self.tables, self.width, self.rows_read = pr, sig, tables, width, rows_read
        for n in ("gathered0", "gathered1", "scattered0", "scattered1"):
            sig[n] = pr.lasting.enter_context(nc.semaphore(f"{pr.name}_{n}"))
            sig.kept.append(n)
        sb = lambda name, shape, dt=F32: ctx.enter_context(nc.sbuf_tensor(f"{pr.name}_{name}", shape, dt))
        self.gather_idx = [sb(f"e_gidx{p}", [P, 3 * SUB], I32) for p in range(2)]
        self.scatter_idx = [sb(f"e_sidx{p}", [P, SUB], I32) for p in range(2)]
        self.rows_in = [[sb(f"e_g{k}_{p}", [P, SUB, row_width]) for p in range(2)] for k in range(len(tables))]
        self.drow = [sb(f"e_drow{p}", [P, STEP + 2], I32) for p in range(2)]
        self.sel = [sb(f"e_sel{p}", [P, SUB, P]) for p in range(2)]
        self.cont = [sb(f"e_cont{p}", [1, SUB, P]) for p in range(2)]
        self.out = [sb(f"e_out{p}", [P, SUB, AGG_W]) for p in range(2)]
        self.o_ps = [ctx.enter_context(nc.psum_tensor(f"{pr.name}_e_sums{k}", [P, 512], F32)) for k in range(banks)] * (2 // banks)

    def load_dst(self, sp, t, p):
        sig = self.sig
        reach(sp, sig["sel_made"], t - 1)
        row = self.pr.d["dst_rows"][bass.ds(t, 1), :]
        sp.dma_start(self.drow[p][:, :], row.to_broadcast([P, STEP + 2])).then_inc(sig[f"dst_loaded{p}"], 16)

    def gather(self, pool, t, p):
        sig, pr = self.sig, self.pr
        reach_gate(pool, sig[self.rows_read], t - 1, sig["pool_gate"])
        pool.tensor_copy(self.gather_idx[p][:, :], pr.index[:, bass.ds(t * (3 * SUB), 3 * SUB)]).then_inc(
            sig["index_copied"], 1)
        reach_gate(pool, sig["index_copied"], t + 1, sig["pool_gate"])
        for j in reversed(range(SUB)):
            for k, (table, slot) in enumerate(self.tables):
                pool.indirect_dma_start(
                    out=self.rows_in[k][p][:, j, 0:D], out_offset=None, in_=table,
                    in_offset=bass.IndirectOffsetOnAxis(ap=self.gather_idx[p][:, slot * SUB + j:slot * SUB + j + 1], axis=0),
                ).then_inc(sig[f"gathered{p}"], 16)

    def gathered(self, eng, t, p):
        reach(eng, self.sig[f"gathered{p}"], dma_count(t, p, 16 * SUB * len(self.tables)))

    def scatter(self, pool, t, p):
        sig, pr = self.sig, self.pr
        reach_gate(pool, sig[f"scattered{p}"], dma_count(t - 2, p, 16 * SUB), sig["pool_gate"])
        pool.tensor_copy(self.scatter_idx[p][:, :], pr.index[:, bass.ds(t * (3 * SUB) + SUB, SUB)]).then_inc(
            sig["scatter_index_copied"], 1)
        reach_gate(pool, sig["scatter_index_copied"], t + 1, sig["pool_gate"])
        reach_gate(pool, sig["out_ready"], SUB * t + SUB, sig["pool_gate"])
        for j in range(SUB):
            pool.indirect_dma_start(
                out=pr.agg, out_offset=bass.IndirectOffsetOnAxis(ap=self.scatter_idx[p][:, j:j + 1], axis=0),
                in_=self.out[p][:, j, :], in_offset=None, bounds_check=pr.agg.shape[0] - 1, oob_is_err=False,
            ).then_inc(sig[f"scattered{p}"], 16)

    def start_out(self, pool):
        for p in range(2):
            pool.memset(self.out[p][:, :, :], 0.0).then_inc(self.sig["out_zeroed"], 1)

    def make_sel(self, dve, t, p):
        sig, pr = self.sig, self.pr
        reach(dve, sig[f"dst_loaded{p}"], dma_count(t, p, 16))
        reach(dve, sig["summed"], SUB * t - SUB)
        for j in range(SUB):
            dve.tensor_scalar(self.sel[p][:, j, :], self.drow[p][:, 1 + j * P:1 + (j + 1) * P],
                              pr.dst_f[:, bass.ds(t * SUB + j, 1)], None, ALU.is_equal)
        above = self.drow[p][0:1, 1 + P:2 + STEP:P].unsqueeze(2).to_broadcast([1, SUB, P])
        dve.tensor_tensor(self.cont[p][:, :, :], self.drow[p][0:1, 1:1 + STEP].rearrange("p (j e) -> p j e", j=SUB),
                          above, ALU.is_equal).then_inc(sig["sel_made"], 1)

    def carry(self, pe, t, p, k, handed=None):
        j = SUB - 1 - k
        if k == 0 and handed is not None:
            above = handed
        else:
            above = self.out[p][0:1, j + 1, 0:self.width] if k else self.out[1 - p][0:1, 0, 0:self.width]
            reach(pe, self.sig["out_ready"], SUB * t + k)
        return pe.matmul(self.o_ps[k % 2][:, 0:self.width], self.cont[p][:, j, :], above, start=False, stop=True)

    def take_out(self, act, t, p, k):
        j = SUB - 1 - k
        reach(act, self.sig["summed"], SUB * t + k + 1)
        if k == 0:
            reach(act, self.sig[f"scattered{p}"], dma_count(t - 2, p, 16 * SUB))
        act.activation(self.out[p][:, j, 0:self.width], self.o_ps[k % 2][:, 0:self.width], ACT.Copy).then_inc(
            self.sig["out_ready"], 1)

    def all_scattered(self, pool):
        for p in range(2):
            pool.wait_ge(self.sig[f"scattered{p}"], 16 * SUB * (self.pr.T // 2))


class TensorProduct:

    def __init__(self, pr, ctx, sig, cross, name):
        nc = pr.nc
        self.pr, self.sig, self.cross, self.name = pr, sig, cross, name
        sb = lambda n, shape: ctx.enter_context(nc.sbuf_tensor(f"{pr.name}_{name}_{n}", shape, F32))
        self.msg = [sb(f"msg{p}", [P, SUB, 4, P]) for p in range(2)]
        self.ws = sb("ws", [P, SUB, 2, NS])
        self.vw = sb("vw", [P, SUB, 3, NV])
        self.ve = sb("ve", [P, SUB, 3, NV])
        self.dot = sb("dot", [P, SUB, NV])
        if cross:
            self.c1 = sb("c1", [P, SUB, 3, NV])
            self.c2 = sb("c2", [P, SUB, 3, NV])

    def emit(self, dve, t, p, rows, w, done):
        sig, n, msg = self.sig, self.name, self.msg[p]
        e4 = self.pr.edge4[:, bass.ds(t * (SUB * 6), SUB * 6)].rearrange("p (j k) -> p j k", j=SUB)
        s = rows[:, :, 0:NS]
        v5 = rows[:, :, NS:NS + 5 * NV].rearrange("p j (i c) -> p j i c", i=5)
        e0 = lambda c: e4[:, :, 0:1].to_broadcast([P, SUB, c])
        e_i = lambda a, c: e4[:, :, 1 + a:4 + a].unsqueeze(3).to_broadcast([P, SUB, 3, c])
        e0_3 = e4[:, :, 0:1].unsqueeze(3).to_broadcast([P, SUB, 3, NV])
        vec = msg[:, :, 1:4, :]

        def op(out, a, b, o, name, *after):
            for x in after:
                dve.wait_ge(sig[f"{n}_{x}"], t + 1)
            return dve.tensor_tensor(out, a, b, o).then_inc(sig[done if name == "done" else f"{n}_{name}"], 1)

        if w is not None:
            two_s = s.unsqueeze(2).to_broadcast([P, SUB, 2, NS])
            op(self.ws[:, :, :, :], w[:, :, 0:2 * NS].rearrange("p j (k c) -> p j k c", k=2), two_s, ALU.mult, "ws")
            w3 = w[:, :, 128:160].unsqueeze(2).to_broadcast([P, SUB, 3, NV])
            op(self.vw[:, :, :, :], w3, v5[:, :, 0:3, :], ALU.mult, "vw")
        op(self.ve[:, :, :, :], v5[:, :, 0:3, :], e_i(0, NV), ALU.mult, "ve")
        if self.cross:
            op(self.c1[:, :, :, :], v5[:, :, 1:4, :], e_i(2, NV), ALU.mult, "c1")
            op(self.c2[:, :, :, :], v5[:, :, 2:5, :], e_i(1, NV), ALU.mult, "c2")
        s0, s1 = (self.ws[:, :, 0, :], self.ws[:, :, 1, :]) if w is not None else (s, s)
        first = ("ws",) if w is not None else ()
        if w is None:
            op(msg[:, :, :, 0:NS], s.unsqueeze(2).to_broadcast([P, SUB, 4, NS]),
               e4[:, :, 0:4].unsqueeze(3).to_broadcast([P, SUB, 4, NS]), ALU.mult, "s1")
        else:
            op(msg[:, :, 0, 0:NS], s0, e0(NS), ALU.mult, "s1", *first)
            op(vec[:, :, :, 0:NS], s1.unsqueeze(2).to_broadcast([P, SUB, 3, NS]), e_i(0, NS), ALU.mult, "v1", *first)
        op(self.dot[:, :, :], self.ve[:, :, 0, :], self.ve[:, :, 1, :], ALU.add, "dot1", "ve")
        if self.cross:
            cross = vec[:, :, :, 96:128]
            if w is not None:
                op(self.c1[:, :, :, :], self.c1[:, :, :, :], self.c2[:, :, :, :], ALU.subtract, "cr", "c1", "c2")
            else:
                op(cross, self.c1[:, :, :, :], self.c2[:, :, :, :], ALU.subtract, "cr", "c1", "c2")
        if w is not None:
            op(vec[:, :, :, NS:96], self.vw[:, :, :, :], e0_3, ALU.mult, "v2", "vw")
            op(self.dot[:, :, :], self.dot[:, :, :], self.ve[:, :, 2, :], ALU.add, "dot2", "dot1")
            if self.cross:
                w5 = w[:, :, 192:224].unsqueeze(2).to_broadcast([P, SUB, 3, NV])
                op(cross, w5, self.c1[:, :, :, :], ALU.mult, "v3", "cr")
            last = op(msg[:, :, 0, NS:96], w[:, :, 160:192], self.dot[:, :, :], ALU.mult, "done", "dot2")
        else:
            op(vec[:, :, :, NS:96], v5[:, :, 0:3, :], e0_3, ALU.mult, "v2")
            last = op(msg[:, :, 0, NS:96], self.dot[:, :, :], self.ve[:, :, 2, :], ALU.add, "done", "dot1")
        return last


def edges_conv(pr, name, fc1, fc2, hidden_in, edge_features, cross, s_parts, v_parts, s_cols):
    nc, T, pr.name = pr.nc, pr.T, name
    n_w = fc2.shape[1]
    with ExitStack() as ctx:
        sig = Signals(nc, ctx)
        sb = lambda n, shape, dt=F32: ctx.enter_context(nc.sbuf_tensor(f"{name}_{n}", shape, dt))
        ps = lambda n, shape: ctx.enter_context(nc.psum_tensor(f"{name}_{n}", shape, F32))
        width = s_cols + 3 * NV
        ec = EdgeCommon(pr, ctx, sig, [(pr.table_a, 0)], width, "messages", D + 2 * NV)
        tp = TensorProduct(pr, ctx, sig, cross, "tp")
        feat = [sb(f"feat{p}", [hidden_in, STEP]) for p in range(2)]
        hid = [sb(f"hid{p}", [NS, STEP]) for p in range(2)]
        agg = [sb(f"agg{k}", [P, 4 * P]) for k in range(2)]
        hid_ps, w_ps = ps("hid_ps", [P, STEP]), ps("w_ps", [P, SUB, 256])
        agg_ps = [ps(f"agg_ps{k}", [P, 4 * P]) for k in range(2)]
        c_fc1, c_fc2, c_s, c_v = 0, NS, NS + n_w, NS + n_w + s_cols
        w, w_zero, w_load, w_scale, w_n = weight_tile(pr, ctx, sig, f"{name}_w", c_v + NV, [
            (0, c_fc1, fc1, hidden_in ** -0.5), (0, c_fc2, fc2, NS ** -0.5)]
            + [(r, c_s + c, ap, f) for r, c, ap, f in s_parts] + [(r, c_v, ap, f) for r, ap, f in v_parts])
        block = ctx.enter_context(nc.Block())

        @block.sync
        def _(sp):
            w_load(sp)

            def load(t, p):
                ec.load_dst(sp, t, p)
                reach(sp, sig["hidden"], t - 1)
                sp.dma_start(feat[p][:, :], edge_features[:, bass.ds(t * STEP, STEP)]).then_inc(sig[f"feat_loaded{p}"], 16)

            rolled(sp, T, [(load, 0)])

        @block.gpsimd
        def _(pool):
            w_zero(pool)
            ec.start_out(pool)
            for p in range(2):
                pool.memset(tp.msg[p][:, :, :, :], 0.0).then_inc(sig["msg_zeroed"], 1)
            pool.wait_ge(sig["msg_zeroed"], 2)
            if not cross:
                for p in range(2):
                    pool.memset(tp.msg[p][:, :, 0, 96:97], 1.0).then_inc(sig["msg_zeroed"], 1)
            rolled(pool, T, [(lambda t, p: ec.gather(pool, t, p), 0), (lambda t, p: ec.scatter(pool, t, p), 2)])
            ec.all_scattered(pool)

        @block.tensor
        def _(pe):
            pe.wait_ge(sig["weights_ready"], w_n)
            pe.wait_ge(sig["out_zeroed"], 2)

            def hidden(t, p):
                reach(pe, sig[f"feat_loaded{p}"], dma_count(t, p, 16))
                reach_gate(pe, sig["silu_done"], t, sig["pe_gate"])
                pe.matmul(hid_ps[0:NS, :], w[0:hidden_in, c_fc1:c_fc1 + NS], feat[p][:, :], start=True, stop=True).then_inc(
                    sig["hidden"], 1)

            def weights(t, p):
                reach(pe, sig["silu_done"], t + 1)
                reach(pe, sig["messages"], t)
                for j in range(SUB):
                    mm = pe.matmul(w_ps[:, j, 0:n_w], hid[p][:, j * P:(j + 1) * P], w[0:NS, c_fc2:c_fc2 + n_w],
                                   start=True, stop=True)
                mm.then_inc(sig["weights"], 1)

            def sums(t, p, k):
                j = SUB - 1 - k
                reach(pe, sig["agg_taken"], SUB * t + k - 1)
                for q in range(4):
                    mm = pe.matmul(agg_ps[k % 2][:, q * P:(q + 1) * P], tp.msg[p][:, j, q, :], ec.sel[p][:, j, :],
                                   start=True, stop=True)
                mm.then_inc(sig["agg"], 1)

            def linear(t, p, k):
                reach(pe, sig["agg_taken"], SUB * t + k + 1)
                reach(pe, sig["out_ready"], SUB * t + k - 1)
                out, a = ec.o_ps[k % 2], agg[k % 2]
                pe.matmul(out[:, 0:s_cols], a[:, 0:P], w[:, c_s:c_s + s_cols], start=True, stop=False)
                for i in range(3):
                    pe.matmul(out[:, s_cols + NV * i:s_cols + NV * (i + 1)], a[:, (1 + i) * P:(2 + i) * P],
                              w[:, c_v:c_v + NV], start=False, stop=False)
                ec.carry(pe, t, p, k).then_inc(sig["summed"], 1)

            def back(t, p):
                reach(pe, sig["messages"], t + 1)
                reach(pe, sig["sel_made"], t + 1)
                for k in range(SUB + 1):
                    if k < SUB:
                        sums(t, p, k)
                    if k:
                        linear(t, p, k - 1)

            rolled(pe, T, [(hidden, 0), (weights, 1), (back, 2)])

        @block.scalar
        def _(act):
            def silu(t, p):
                reach(act, sig["hidden"], t + 1)
                reach(act, sig["weights"], t - 1)
                act.activation(hid[p][:, :], hid_ps[0:NS, :], ACT.Silu).then_inc(sig["silu_done"], 1)

            def copies(t, p):
                rows = ec.rows_in[0][p]
                ec.gathered(act, t, p)
                act.activation(rows[:, :, D:D + 2 * NV], rows[:, :, NS:NS + 2 * NV], ACT.Copy).then_inc(sig["rows_doubled"], 1)

            def take(t, p):
                for k in range(SUB + 1):
                    if k < SUB:
                        reach(act, sig["agg"], SUB * t + k + 1)
                        reach(act, sig["summed"], SUB * t + k - 1)
                        act.activation(agg[k % 2][:, :], agg_ps[k % 2][:, :], ACT.Copy).then_inc(sig["agg_taken"], 1)
                    if k:
                        ec.take_out(act, t, p, k - 1)

            act.wait_ge(sig["out_zeroed"], 2)
            rolled(act, T, [(silu, 0), (copies, 1), (take, 2)])

        @block.vector
        def _(dve):
            w_scale(dve)
            dve.wait_ge(sig["msg_zeroed"], 2 if cross else 4)

            def messages(t, p):
                ec.make_sel(dve, t, p)
                ec.gathered(dve, t, p)
                reach(dve, sig["rows_doubled"], t + 1)
                reach(dve, sig["messages"], t)
                reach(dve, sig["weights"], t + 1)
                tp.emit(dve, t, p, ec.rows_in[0][p], w_ps, "messages")

            rolled(dve, T, [(messages, 1)])

    finish_pass(nc, sig)


def edges_layer1(pr):
    nc, T, pr.name = pr.nc, pr.T, "l1"
    with ExitStack() as ctx:
        sig = Signals(nc, ctx)
        sb = lambda n, shape, dt=F32: ctx.enter_context(nc.sbuf_tensor(f"l1_{n}", shape, dt))
        ps = lambda n, shape: ctx.enter_context(nc.psum_tensor(f"l1_{n}", shape, F32))
        ec = EdgeCommon(pr, ctx, sig, [(pr.table_x, 0)], D, "products")
        feat = [sb(f"feat{p}", [17, STEP]) for p in range(2)]
        prod = [sb(f"prod{p}", [P, SUB, 4, 96]) for p in range(2)]
        ve, dot = sb("ve", [P, SUB, 3, NV]), sb("dot", [P, SUB, NV])
        pT = [sb(f"pT{k}", [96, 4 * P]) for k in range(2)]
        rad = [sb(f"rad{p}", [P, SUB, D]) for p in range(2)]
        msg = [sb(f"msg{p}", [P, SUB, D]) for p in range(2)]
        rad_ps, m_ps = ps("rad_ps", [P, SUB, 256]), ps("m_ps", [P, SUB, 256])
        pT_ps = [ps(f"pT_ps{k}", [P, 4 * P]) for k in range(2)]
        r2, r3 = 2.0 ** -0.5, 3.0 ** -0.5
        cs, cv, cr = 0, NS, NS + NV
        w, w_zero, w_load, w_scale, w_n = weight_tile(pr, ctx, sig, "l1_w", cr + D, [
            (0, cs, pr.d["L1_gnn_W_ss"], NS ** -0.5 * r2), (NS, cs, pr.d["L1_gnn_W_vv"], r3 * NV ** -0.5 * r2),
            (0, cv, pr.d["L1_gnn_W_sv"], r3 * NS ** -0.5 * r2), (NS, cv, pr.d["L1_gnn_W_vs"], r3 * NV ** -0.5 * r2),
            (0, cr, pr.d["L1_rad"], 1.0)])
        block = ctx.enter_context(nc.Block())

        @block.sync
        def _(sp):
            w_load(sp)
            sp.wait_ge(sig["ones_set"], 2)

            def load(t, p):
                reach(sp, sig["radial"], t - 1)
                sp.dma_start(feat[p][0:16, :], pr.d["edge_attr_16"][:, bass.ds(t * STEP, STEP)]).then_inc(
                    sig[f"feat_loaded{p}"], 16)

            rolled(sp, T, [(load, 0), (lambda t, p: ec.load_dst(sp, t, p), 1)])

        @block.gpsimd
        def _(pool):
            w_zero(pool)
            ec.start_out(pool)
            for p in range(2):
                pool.memset(feat[p][:, :], 1.0).then_inc(sig["ones_set"], 1)
            rolled(pool, T, [(lambda t, p: ec.gather(pool, t, p), 0), (lambda t, p: ec.scatter(pool, t, p), 2)])
            ec.all_scattered(pool)

        @block.tensor
        def _(pe):
            pe.wait_ge(sig["weights_ready"], w_n)
            pe.wait_ge(sig["out_zeroed"], 2)

            def radial(t, p):
                reach(pe, sig[f"feat_loaded{p}"], dma_count(t, p, 16))
                reach(pe, sig["sigmoid_done"], t)
                for j in range(SUB):
                    mm = pe.matmul(rad_ps[:, j, 0:D], feat[p][:, j * P:(j + 1) * P], w[0:17, cr:cr + D],
                                   start=True, stop=True)
                mm.then_inc(sig["radial"], 1)

            def turn(t, p, k):
                j = SUB - 1 - k
                reach(pe, sig["pT_taken"], SUB * t + k - 1)
                for q in range(4):
                    mm = pe.transpose(pT_ps[k % 2][0:96, q * P:(q + 1) * P], prod[p][:, j, q, :], pr.ident[:, :])
                mm.then_inc(sig["pT"], 1)

            def linear(t, p, k):
                j, a = SUB - 1 - k, pT[k % 2]
                reach(pe, sig["pT_taken"], SUB * t + k + 1)
                pe.matmul(m_ps[:, j, 0:NS], a[:, 0:P], w[0:96, cs:cs + NS], start=True, stop=True)
                for i in range(3):
                    mm = pe.matmul(m_ps[:, j, NS + NV * i:NS + NV * (i + 1)], a[:, (1 + i) * P:(2 + i) * P],
                                   w[0:96, cv:cv + NV], start=True, stop=True)
                mm.then_inc(sig["linear"], 1)

            def sums(t, p, k):
                j = SUB - 1 - k
                reach(pe, sig["out_ready"], SUB * t + k - 1)
                pe.matmul(ec.o_ps[k % 2][:, 0:D], ec.sel[p][:, j, :], msg[p][:, j, :], start=True, stop=False)
                ec.carry(pe, t, p, k).then_inc(sig["summed"], 1)

            def map_products(t, p):
                reach(pe, sig["products"], t + 1)
                reach(pe, sig["scaled"], t)
                for k in range(SUB + 1):
                    if k < SUB:
                        turn(t, p, k)
                    if k:
                        linear(t, p, k - 1)

            def all_sums(t, p):
                reach(pe, sig["scaled"], t + 1)
                reach(pe, sig["sel_made"], t + 1)
                for k in range(SUB):
                    sums(t, p, k)

            rolled(pe, T, [(map_products, 1), (all_sums, 2), (radial, 0)])

        @block.scalar
        def _(act):
            def sigmoid(t, p):
                reach(act, sig["radial"], t + 1)
                reach(act, sig["scaled"], t - 1)
                act.activation(rad[p][:, :, :], rad_ps[:, :, 0:D], ACT.Sigmoid).then_inc(sig["sigmoid_done"], 1)

            def take(t, p):
                for k in range(SUB):
                    reach(act, sig["pT"], SUB * t + k + 1)
                    reach(act, sig["linear"], SUB * t + k - 1)
                    act.activation(pT[k % 2][:, :], pT_ps[k % 2][0:96, :], ACT.Copy).then_inc(sig["pT_taken"], 1)

            def take_out(t, p):
                for k in range(SUB):
                    ec.take_out(act, t, p, k)

            act.wait_ge(sig["out_zeroed"], 2)
            rolled(act, T, [(take, 1), (take_out, 2), (sigmoid, 0)])

        @block.vector
        def _(dve):
            w_scale(dve)

            def products(t, p):
                e4 = pr.edge4[:, bass.ds(t * (SUB * 6), SUB * 6)].rearrange("p (j k) -> p j k", j=SUB)
                rows = ec.rows_in[0][p]
                v = rows[:, :, NS:D].rearrange("p j (i c) -> p j i c", i=3)
                ec.gathered(dve, t, p)
                reach(dve, sig["pT"], SUB * t - SUB)
                reach(dve, sig["products"], t)
                dve.tensor_tensor(ve[:, :, :, :], v, e4[:, :, 1:4].unsqueeze(3).to_broadcast([P, SUB, 3, NV]),
                                  ALU.mult).then_inc(sig["ve"], 1)
                dve.tensor_tensor(prod[p][:, :, :, 0:NS], rows[:, :, 0:NS].unsqueeze(2).to_broadcast([P, SUB, 4, NS]),
                                  e4[:, :, 0:4].unsqueeze(3).to_broadcast([P, SUB, 4, NS]), ALU.mult).then_inc(sig["prod_s"], 1)
                dve.wait_ge(sig["ve"], t + 1)
                dve.tensor_tensor(dot[:, :, :], ve[:, :, 0, :], ve[:, :, 1, :], ALU.add).then_inc(sig["dot"], 1)
                dve.tensor_tensor(prod[p][:, :, 1:4, NS:96], v, e4[:, :, 0:1].unsqueeze(3).to_broadcast([P, SUB, 3, NV]),
                                  ALU.mult).then_inc(sig["prod_v"], 1)
                dve.wait_ge(sig["dot"], t + 1)
                dve.tensor_tensor(prod[p][:, :, 0, NS:96], dot[:, :, :], ve[:, :, 2, :], ALU.add).then_inc(sig["products"], 1)

            def scale(t, p):
                ec.make_sel(dve, t, p)
                reach(dve, sig["sigmoid_done"], t + 1)
                reach(dve, sig["linear"], SUB * t + SUB)
                dve.tensor_tensor(msg[p][:, :, :], m_ps[:, :, 0:D], rad[p][:, :, :], ALU.mult).then_inc(sig["scaled"], 1)

            rolled(dve, T, [(products, 0), (scale, 1)])

    finish_pass(nc, sig)


class Norm:

    def __init__(self, pr, ctx, sig, name, parts):
        nc = pr.nc
        self.sig, self.name, self.parts = sig, name, parts
        sb = lambda n, shape: ctx.enter_context(nc.sbuf_tensor(f"{pr.name}_{name}_{n}", shape, F32))
        n = len(parts)
        self.stats = sb("stats", [P, n, SUB, 6])
        self.mean = [sb(f"mean{p}", [P, n, SUB, 2]) for p in range(2)]
        self.var = [sb(f"var{p}", [P, n, SUB]) for p in range(2)]
        self.rstd = [sb(f"rstd{p}", [P, n, SUB]) for p in range(2)]
        self.half = sb("half", [P, n, SUB])

    def start(self, pool):
        pool.memset(self.half[:, :, :], -0.5).then_inc(self.sig[f"{self.name}_half"], 1)
        pool.wait_ge(self.sig[f"{self.name}_half"], 1)

    def statistics(self, dve, t, p, z, root_mean_square=False):
        sig, n = self.sig, self.name
        for k, (c, width) in enumerate(self.parts):
            for j in range(SUB):
                ins = dve.bn_stats(self.stats[:, k, j, :], z[:, j, c:c + width])
        ins.then_inc(sig[f"{n}_stats"], 1)
        reach_gate(dve, sig[f"{n}_stats"], t + 1, sig["dve_gate"])
        for k in range(len(self.parts)):
            for j in range(SUB):
                ins = dve.bn_aggr(self.mean[p][:, k, j, :], self.stats[:, k, j, :])
        ins.then_inc(sig[f"{n}_mean"], 1)
        dve.wait_ge(sig[f"{n}_mean"], t + 1)
        if root_mean_square:
            m = self.mean[p]
            dve.tensor_tensor(self.var[p][:, 1, :], m[:, 1, :, 0], m[:, 1, :, 0], ALU.mult).then_inc(sig[f"{n}_ms"], 1)
            dve.wait_ge(sig[f"{n}_ms"], 2 * t + 1)
            dve.tensor_tensor(self.var[p][:, 1, :], self.var[p][:, 1, :], m[:, 1, :, 1], ALU.add).then_inc(sig[f"{n}_ms"], 1)
            dve.wait_ge(sig[f"{n}_ms"], 2 * t + 2)
            dve.tensor_scalar(self.var[p][:, 1, :], self.var[p][:, 1, :], 3.0, EPS, ALU.mult, ALU.add)
            dve.tensor_scalar(self.var[p][:, 0, :], m[:, 0, :, 1], EPS, None, ALU.add).then_inc(sig[f"{n}_var"], 1)
        else:
            dve.tensor_scalar(self.var[p][:, :, :], self.mean[p][:, :, :, 1], EPS, None, ALU.add).then_inc(
                sig[f"{n}_var"], 1)

    def power(self, pool, t, p):
        sig, n = self.sig, self.name
        reach_gate(pool, sig[f"{n}_var"], t + 1, sig["pool_gate"])
        reach_gate(pool, sig[f"{n}_applied"], t - 1, sig["pool_gate"])
        pool.tensor_tensor(self.rstd[p][:, :, :], self.var[p][:, :, :], self.half[:, :, :], ALU.pow).then_inc(
            sig[f"{n}_rstd"], 1)

    def apply(self, dve, t, p, out, z, root_mean_square=False):
        sig, n = self.sig, self.name
        reach(dve, sig[f"{n}_rstd"], t + 1)
        for k, (c, width) in enumerate(self.parts):
            for j in range(SUB):
                to, of, r = out[:, j, c:c + width], z[:, j, c:c + width], self.rstd[p][:, k, j:j + 1]
                if root_mean_square and k == 1:
                    ins = dve.tensor_scalar(to, of, r, None, ALU.mult)
                else:
                    ins = dve.tensor_scalar(to, of, self.mean[p][:, k, j, 0:1], r, ALU.subtract, ALU.mult)
        return ins.then_inc(sig[f"{n}_applied"], 1)


class Turn:

    def __init__(self, pr, ctx, sig, name, bank=None):
        nc = pr.nc
        self.pr, self.sig, self.name = pr, sig, name
        self.ps = bank if bank is not None else ctx.enter_context(nc.psum_tensor(f"{pr.name}_{name}_ps", [P, SUB, 2 * P], F32))
        self.s = ctx.enter_context(nc.sbuf_tensor(f"{pr.name}_{name}_s", [NS, SUB, P], F32))
        self.v = ctx.enter_context(nc.sbuf_tensor(f"{pr.name}_{name}_v", [3 * NV, SUB, P], F32))

    def turn(self, pe, t, rows):
        for j in range(SUB):
            pe.transpose(self.ps[0:NS, j, 0:P], rows[:, j, 0:NS], self.pr.ident[:, :])
            mm = pe.transpose(self.ps[0:3 * NV, j, P:2 * P], rows[:, j, NS:D], self.pr.ident[:, :])
        mm.then_inc(self.sig[f"{self.name}_turned"], 1)

    def take(self, act, t, used):
        reach(act, self.sig[f"{self.name}_turned"], t + 1)
        reach(act, self.sig[used], t)
        act.activation(self.s[:, :, :], self.ps[0:NS, :, 0:P], ACT.Copy)
        act.activation(self.v[:, :, :], self.ps[0:3 * NV, :, P:2 * P], ACT.Copy).then_inc(
            self.sig[f"{self.name}_taken"], 1)

    def product(self, pe, t, out, w, maps, done):
        reach(pe, self.sig[f"{self.name}_taken"], t + 1)
        for j in range(SUB):
            for c, ws, wv in maps:
                pe.matmul(out[:, j, c:c + NS], self.s[:, j, :], w[0:NS, ws:ws + NS], start=True, stop=True)
                mm = pe.matmul(out[:, j, c + NS:c + D], self.v[:, j, :], w[0:3 * NV, wv:wv + 3 * NV], start=True, stop=True)
        mm.then_inc(self.sig[done], 1)


def nodes_layer0(pr):
    nc, T, pr.name = pr.nc, pr.T, "n0"
    with ExitStack() as ctx:
        sig = Signals(nc, ctx)
        two = lambda n, shape: [ctx.enter_context(nc.sbuf_tensor(f"n0_{n}{p}", shape, F32)) for p in range(2)]
        xs, xv, x, agg = two("xs", [NS, STEP]), two("xv", [3 * NV, STEP]), two("x", [P, SUB, D]), two("agg", [P, SUB, AGG_W])
        pre, gate, z, x1 = two("pre", [P, SUB, 192]), two("gate", [P, SUB, 96]), two("z", [P, SUB, D]), two("x1", [P, SUB, D])
        acc = [ctx.enter_context(nc.psum_tensor(f"n0_acc{p}", [P, SUB, 256], F32)) for p in range(2)]
        norm = Norm(pr, ctx, sig, "norm", [(0, D)])
        w, w_zero, w_load, w_scale, w_n = weight_tile(pr, ctx, sig, "n0_w", 192, [
            (0, 0, pr.d["L0_gnn_sc_ws"], NS ** -0.5)] + block_diagonal(96, pr.d["L0_gnn_sc_wv"], NV ** -0.5))
        block = ctx.enter_context(nc.Block())

        @block.sync
        def _(sp):
            w_load(sp)

            def load(t, p):
                reach(sp, sig["self_product"], t - 1)
                reach(sp, sig["norm_stats"], t - 1)
                reach(sp, sig["summed_up"], t - 1)
                for to, of in ((xs[p][:, :], pr.d["xT"][0:NS, bass.ds(t * STEP, STEP)]),
                               (xv[p][:, :], pr.d["xT"][NS:D, bass.ds(t * STEP, STEP)]),
                               (x[p][:, :, :].rearrange("p j c -> p (j c)"), pr.rows(pr.d["x"], t)),
                               (agg[p][:, :, :].rearrange("p j c -> p (j c)"), pr.rows(pr.agg, t))):
                    sp.dma_start(to, of).then_inc(sig[f"loaded{p}"], 16)

            rolled(sp, T, [(load, 0)])

        @block.gpsimd
        def _(pool):
            w_zero(pool)
            norm.start(pool)
            rolled(pool, T, [(lambda t, p: norm.power(pool, t, p), 0)])

        @block.tensor
        def _(pe):
            pe.wait_ge(sig["weights_ready"], w_n)

            def product(t, p):
                reach(pe, sig[f"loaded{p}"], dma_count(t, p, 64))
                reach_gate(pe, sig["summed_up"], t - 1, sig["pe_gate"])
                for j in range(SUB):
                    cols = slice(j * P, (j + 1) * P)
                    pe.matmul(acc[p][:, j, 0:96], xs[p][:, cols], w[0:NS, 0:96], start=True, stop=True)
                    mm = pe.matmul(acc[p][:, j, 96:192], xv[p][:, cols], w[0:3 * NV, 96:192], start=True, stop=True)
                mm.then_inc(sig["self_product"], 1)

            rolled(pe, T, [(product, 0)])

        @block.scalar
        def _(act):
            def gates(t, p):
                reach(act, sig["pre"], t + 1)
                reach(act, sig["z"], t - 1)
                act.activation(gate[p][:, :, :], pre[p][:, :, 0:96], ACT.Sigmoid).then_inc(sig["gates"], 1)

            def store(t, p):
                reach(act, sig["norm_applied"], t + 1)
                act.dma_start(pr.rows(pr.table_x, t), x1[p][:, :, :].rearrange("p j c -> p (j c)")).then_inc(
                    sig[f"stored{p}"], 16)

            rolled(act, T, [(gates, 0), (store, 2)])
            for p in range(2):
                act.wait_ge(sig[f"stored{p}"], 16 * (T // 2))

        @block.vector
        def _(dve):
            w_scale(dve)

            def add_up(t, p):
                reach(dve, sig[f"loaded{p}"], dma_count(t, p, 64))
                reach(dve, sig["self_product"], t + 1)
                dve.tensor_tensor(pre[p][:, :, :], acc[p][:, :, 0:192], agg[p][:, :, :], ALU.add).then_inc(sig["summed_up"], 1)
                reach(dve, sig["summed_up"], t + 1)
                dve.tensor_tensor(pre[p][:, :, :], pre[p][:, :, :],
                                  pr.attr[:, bass.ds(t * SUB, SUB)].unsqueeze(2).to_broadcast([P, SUB, 192]),
                                  ALU.mult).then_inc(sig["pre"], 1)

            def gated(t, p):
                reach(dve, sig["norm_applied"], t - 1)
                reach(dve, sig["gates"], t + 1)
                dve.tensor_tensor(pre[p][:, :, 0:NS], pre[p][:, :, 0:NS], gate[p][:, :, 0:NS], ALU.mult).then_inc(sig["gated"], 1)
                vec = pre[p][:, :, 96:192].rearrange("p j (i c) -> p j i c", i=3)
                dve.tensor_tensor(vec, vec, gate[p][:, :, NS:96].unsqueeze(2).to_broadcast([P, SUB, 3, NV]),
                                  ALU.mult).then_inc(sig["gated"], 1)
                reach(dve, sig["gated"], 2 * t + 2)
                dve.tensor_tensor(z[p][:, :, 0:NS], pre[p][:, :, 0:NS], x[p][:, :, 0:NS], ALU.add)
                dve.tensor_tensor(z[p][:, :, NS:D], pre[p][:, :, 96:192], x[p][:, :, NS:D], ALU.add).then_inc(sig["z"], 1)
                reach(dve, sig["z"], t + 1)
                norm.statistics(dve, t, p, z[p])

            def normalise(t, p):
                reach(dve, sig[f"stored{p}"], dma_count(t - 2, p, 16))
                norm.apply(dve, t, p, x1[p], z[p])

            rolled(dve, T, [(normalise, 2), (gated, 1), (add_up, 0)])

    finish_pass(nc, sig)


def nodes_layer1(pr):
    nc, T, pr.name = pr.nc, pr.T, "n1"
    with ExitStack() as ctx:
        sig = Signals(nc, ctx)
        two = lambda n, shape: [ctx.enter_context(nc.sbuf_tensor(f"n1_{n}{p}", shape, F32)) for p in range(2)]
        x, agg, h, z, x2 = (two(n, [P, SUB, D]) for n in ("x", "agg", "h", "z", "x2"))
        fa, fb = two("fa", [P, SUB, D]), two("fb", [P, SUB, D])
        y_ps = ctx.enter_context(nc.psum_tensor("n1_y", [P, SUB, 256], F32))
        f_ps = ctx.enter_context(nc.psum_tensor("n1_f", [P, SUB, 512], F32))
        h_turn = Turn(pr, ctx, sig, "h_turn")
        x_turn = Turn(pr, ctx, sig, "x_turn", h_turn.ps)
        norm = Norm(pr, ctx, sig, "norm", [(0, D)])
        d, ks, kv = pr.d, NS ** -0.5, NV ** -0.5
        w, w_zero, w_load, w_scale, w_n = weight_tile(
            pr, ctx, sig, "n1_w", 3 * D, [(0, 0, d["L1_gnn_L_s"], ks), (0, D, d["L2_gnn_Wl1_0"], ks), (0, 2 * D, d["L2_gnn_Wsc0"], ks)]
            + block_diagonal(NS, d["L1_gnn_L_v"], kv) + block_diagonal(D + NS, d["L2_gnn_Wl1_1"], kv)
            + block_diagonal(2 * D + NS, d["L2_gnn_Wsc1"], kv))
        block = ctx.enter_context(nc.Block())

        @block.sync
        def _(sp):
            w_load(sp)

            def load(t, p):
                reach(sp, sig["z"], t - 1)
                sp.dma_start(x[p][:, :, :].rearrange("p j c -> p (j c)"), pr.rows(pr.table_x, t)).then_inc(sig[f"loaded{p}"], 16)
                sp.dma_start(agg[p][:, :, :], pr.agg.rearrange("(t p j) c -> t p j c", p=P, j=SUB)[bass.ds(t, 1), :, :, 0:D]
                             .rearrange("a p j c -> (a p) j c")).then_inc(sig[f"loaded{p}"], 16)

            rolled(sp, T, [(load, 0)])

        @block.gpsimd
        def _(pool):
            w_zero(pool)
            norm.start(pool)
            rolled(pool, T, [(lambda t, p: norm.power(pool, t, p), 0)])

        @block.tensor
        def _(pe):
            pe.wait_ge(sig["weights_ready"], w_n)

            def turn_h(t, p):
                reach(pe, sig["h"], t + 1)
                reach_gate(pe, sig["x_turn_taken"], t - 1, sig["pe_gate"])
                h_turn.turn(pe, t, h[p])

            def product_y(t, p):
                reach(pe, sig["z"], t)
                h_turn.product(pe, t, y_ps, w, [(0, 0, NS)], "y")

            def turn_x(t, p):
                reach(pe, sig["norm_applied"], t + 1)
                h_steps = t + 2 if not isinstance(t, int) else min(t + 2, T)
                reach_gate(pe, sig["h_turn_taken"], h_steps, sig["pe_gate"])
                x_turn.turn(pe, t, x2[p])

            def product_f(t, p):
                reach(pe, sig["f_read"], t)
                x_turn.product(pe, t, f_ps, w, [(0, D, D + NS), (D, 2 * D, 2 * D + NS)], "f")

            rolled(pe, T, [(turn_h, 0), (product_y, 0), (turn_x, 1), (product_f, 1)])

        @block.scalar
        def _(act):
            def store(t, p):
                reach(act, sig["fb"], t + 1)
                for table, rows in ((pr.table_a, fa[p]), (pr.table_b, fb[p])):
                    act.dma_start(pr.rows(table, t), rows[:, :, :].rearrange("p j c -> p (j c)")).then_inc(sig[f"stored{p}"], 16)

            rolled(act, T, [(lambda t, p: h_turn.take(act, t, "y"), 0), (lambda t, p: x_turn.take(act, t, "f"), 1), (store, 2)])
            for p in range(2):
                act.wait_ge(sig[f"stored{p}"], 32 * (T // 2))

        @block.vector
        def _(dve):
            w_scale(dve)

            def add(t, p):
                reach(dve, sig[f"loaded{p}"], dma_count(t, p, 32))
                reach(dve, sig["h_turn_turned"], t - 1)
                dve.tensor_tensor(h[p][:, :, :], x[p][:, :, :], agg[p][:, :, :], ALU.add).then_inc(sig["h"], 1)

            def residual(t, p):
                reach(dve, sig["norm_applied"], t - 1)
                reach(dve, sig["y"], t + 1)
                dve.tensor_tensor(z[p][:, :, :], y_ps[:, :, 0:D], x[p][:, :, :], ALU.add).then_inc(sig["z"], 1)
                reach(dve, sig["z"], t + 1)
                norm.statistics(dve, t, p, z[p])
                norm.apply(dve, t, p, x2[p], z[p])

            def tables(t, p):
                a = pr.attr[:, bass.ds(t * SUB, SUB)].unsqueeze(2).to_broadcast([P, SUB, D])
                reach(dve, sig["f"], t + 1)
                reach(dve, sig[f"stored{p}"], dma_count(t - 2, p, 32))
                dve.tensor_tensor(fa[p][:, :, :], f_ps[:, :, 0:D], a, ALU.mult).then_inc(sig["fa"], 1)
                dve.tensor_tensor(fb[p][:, :, :], f_ps[:, :, D:2 * D], a, ALU.mult).then_inc(sig["f_read"], 1)
                reach(dve, sig["f_read"], t + 1)
                dve.tensor_tensor(fb[p][:, :, :], fb[p][:, :, :], x2[p][:, :, :], ALU.add).then_inc(sig["fb"], 1)

            rolled(dve, T, [(add, 0), (residual, 0), (tables, 1)])

    finish_pass(nc, sig)


def nodes_layer2(pr):
    nc, T, d, pr.name = pr.nc, pr.T, pr.d, "n2"
    with ExitStack() as ctx:
        sig = Signals(nc, ctx)
        two = lambda n, shape: [ctx.enter_context(nc.sbuf_tensor(f"n2_{n}{p}", shape, F32)) for p in range(2)]
        base, z, x3, hat = (two(n, [P, SUB, D]) for n in ("base", "z", "x3", "hat"))
        agg = two("agg", [P, SUB, AGG_W])
        fa, fb = two("fa", [P, SUB, D]), two("fb", [P, SUB, D])
        share = ctx.enter_context(nc.sbuf_tensor("n2_share", [P, 3, SUB], F32))
        gamma = ctx.enter_context(nc.sbuf_tensor("n2_gamma", [P, D], F32))
        beta = ctx.enter_context(nc.sbuf_tensor("n2_beta", [P, NS], F32))
        f_ps = ctx.enter_context(nc.psum_tensor("n2_f", [P, SUB, 512], F32))
        turn = Turn(pr, ctx, sig, "turn")
        norm = Norm(pr, ctx, sig, "norm", [(0, D)])
        equi = Norm(pr, ctx, sig, "equi", [(0, NS), (NS, 3 * NV)])
        w, w_zero, w_load, w_scale, w_n = weight_tile(
            pr, ctx, sig, "n2_w", 2 * D, [(0, 0, d["L3_gnn_Ws_src"], 1.0), (0, D, d["L3_gnn_Ws_dst"], 1.0)]
            + block_diagonal(NS, d["L3_gnn_Wv_src"], 1.0) + block_diagonal(D + NS, d["L3_gnn_Wv_dst"], 1.0))
        block = ctx.enter_context(nc.Block())

        @block.sync
        def _(sp):
            w_load(sp)
            sp.dma_start(gamma[:, 0:NS], d["L3_gnn_gamma_s"].to_broadcast([P, NS])).then_inc(sig["affine_loaded"], 16)
            sp.dma_start(beta[:, :], d["L3_gnn_beta_s"].to_broadcast([P, NS])).then_inc(sig["affine_loaded"], 16)
            for i in range(3):
                sp.dma_start(gamma[:, NS + NV * i:NS + NV * (i + 1)], d["L3_gnn_gamma_v"].to_broadcast([P, NV])).then_inc(
                    sig["affine_loaded"], 16)

            def load(t, p):
                reach(sp, sig["z"], t - 1)
                sp.dma_start(base[p][:, :, :].rearrange("p j c -> p (j c)"), pr.rows(pr.table_b, t)).then_inc(sig[f"loaded{p}"], 16)
                sp.dma_start(agg[p][:, :, :].rearrange("p j c -> p (j c)"), pr.rows(pr.agg, t)).then_inc(sig[f"loaded{p}"], 16)

            rolled(sp, T, [(load, 0)])

        @block.gpsimd
        def _(pool):
            w_zero(pool)
            norm.start(pool)
            equi.start(pool)
            rolled(pool, T, [(lambda t, p: norm.power(pool, t, p), 0), (lambda t, p: equi.power(pool, t, p), 0)])

        @block.tensor
        def _(pe):
            pe.wait_ge(sig["weights_ready"], w_n)

            def product(t, p):
                reach(pe, sig["hat"], t + 1)
                reach_gate(pe, sig["turn_taken"], t, sig["pe_gate"])
                turn.turn(pe, t, hat[p])
                reach(pe, sig["f_taken"], t)
                turn.product(pe, t, f_ps, w, [(0, 0, NS), (D, D, D + NS)], "f")

            rolled(pe, T, [(product, 1)])

        @block.scalar
        def _(act):
            def take(t, p):
                turn.take(act, t, "f")
                reach(act, sig["f"], t + 1)
                reach(act, sig[f"stored{p}"], dma_count(t - 2, p, 48))
                act.activation(fa[p][:, :, :], f_ps[:, :, 0:D], ACT.Copy)
                act.activation(fb[p][:, :, :], f_ps[:, :, D:2 * D], ACT.Copy).then_inc(sig["f_taken"], 1)

            def store(t, p):
                reach(act, sig["f_taken"], t + 1)
                for table, rows in ((pr.table_a, fa[p]), (pr.table_c, fb[p]), (pr.table_x, x3[p])):
                    act.dma_start(pr.rows(table, t), rows[:, :, :].rearrange("p j c -> p (j c)")).then_inc(sig[f"stored{p}"], 16)

            rolled(act, T, [(take, 1), (store, 1)])
            for p in range(2):
                act.wait_ge(sig[f"stored{p}"], 48 * (T // 2))

        @block.vector
        def _(dve):
            w_scale(dve)
            dve.wait_ge(sig["affine_loaded"], 16 * 5)

            def residual(t, p):
                s = agg[p]
                reach(dve, sig[f"loaded{p}"], dma_count(t, p, 32))
                dve.tensor_scalar(share[:, 0, :], s[:, :, 1], 1.0, None, ALU.max).then_inc(sig["count"], 1)
                reach(dve, sig["count"], t + 1)
                dve.reciprocal(share[:, 1, :], share[:, 0, :]).then_inc(sig["inverse"], 1)
                reach(dve, sig["inverse"], t + 1)
                dve.tensor_tensor(share[:, 0, :], share[:, 1, :], pr.attr[:, bass.ds(t * SUB, SUB)], ALU.mult).then_inc(sig["share"], 1)
                reach(dve, sig["share"], 3 * t + 1)
                dve.tensor_tensor(share[:, 1, :], share[:, 0, :], share[:, 0, :], ALU.mult).then_inc(sig["share"], 1)
                reach(dve, sig["share"], 3 * t + 2)
                dve.tensor_tensor(share[:, 2, :], share[:, 1, :], s[:, :, 0], ALU.mult).then_inc(sig["share"], 1)
                reach(dve, sig["share"], 3 * t + 3)
                for j in range(SUB):
                    ins = dve.scalar_tensor_tensor(out=z[p][:, j, :], in0=s[:, j, 2:2 + D], scalar=share[:, 2, j:j + 1],
                                                   in1=base[p][:, j, :], op0=ALU.mult, op1=ALU.add)
                ins.then_inc(sig["z"], 1)
                reach(dve, sig["z"], t + 1)
                norm.statistics(dve, t, p, z[p])
                reach(dve, sig[f"stored{p}"], dma_count(t - 2, p, 48))
                norm.apply(dve, t, p, x3[p], z[p])
                reach(dve, sig["norm_applied"], t + 1)
                equi.statistics(dve, t, p, x3[p], True)
                reach(dve, sig["turn_turned"], t - 1)
                equi.apply(dve, t, p, hat[p], x3[p], True)
                reach(dve, sig["equi_applied"], t + 1)
                dve.tensor_tensor(hat[p][:, :, :], hat[p][:, :, :], gamma[:, :].unsqueeze(1).to_broadcast([P, SUB, D]),
                                  ALU.mult).then_inc(sig["gamma"], 1)
                reach(dve, sig["gamma"], t + 1)
                dve.tensor_tensor(hat[p][:, :, 0:NS], hat[p][:, :, 0:NS], beta[:, :].unsqueeze(1).to_broadcast([P, SUB, NS]),
                                  ALU.add).then_inc(sig["hat"], 1)

            rolled(dve, T, [(residual, 0)])

    finish_pass(nc, sig)


def nodes_layer3(pr):
    nc, T, d, pr.name = pr.nc, pr.T, pr.d, "n3"
    with ExitStack() as ctx:
        sig = Signals(nc, ctx)
        two = lambda n, shape: [ctx.enter_context(nc.sbuf_tensor(f"n3_{n}{p}", shape, F32)) for p in range(2)]
        x, att, z, o = (two(n, [P, SUB, D]) for n in ("x", "att", "z", "o"))
        agg = two("agg", [P, SUB, AGG_W])
        den = ctx.enter_context(nc.sbuf_tensor("n3_den", [P, 2, SUB, HEADS], F32))
        y_ps = ctx.enter_context(nc.psum_tensor("n3_y", [P, SUB, 256], F32))
        turn = Turn(pr, ctx, sig, "turn")
        norm = Norm(pr, ctx, sig, "norm", [(0, D)])
        w, w_zero, w_load, w_scale, w_n = weight_tile(pr, ctx, sig, "n3_w", D, [(0, 0, d["L3_gnn_Wps"], 1.0)]
                                                      + block_diagonal(NS, d["L3_gnn_Wpv"], 1.0))
        block = ctx.enter_context(nc.Block())

        @block.sync
        def _(sp):
            w_load(sp)

            def load(t, p):
                reach(sp, sig["z"], t - 1)
                sp.dma_start(x[p][:, :, :].rearrange("p j c -> p (j c)"), pr.rows(pr.table_x, t)).then_inc(sig[f"loaded{p}"], 16)
                sp.dma_start(agg[p][:, :, :].rearrange("p j c -> p (j c)"), pr.rows(pr.agg, t)).then_inc(sig[f"loaded{p}"], 16)

            rolled(sp, T, [(load, 0)])

        @block.gpsimd
        def _(pool):
            w_zero(pool)
            norm.start(pool)
            rolled(pool, T, [(lambda t, p: norm.power(pool, t, p), 0)])

        @block.tensor
        def _(pe):
            pe.wait_ge(sig["weights_ready"], w_n)

            def product(t, p):
                reach(pe, sig["attended"], t + 1)
                reach_gate(pe, sig["turn_taken"], t, sig["pe_gate"])
                turn.turn(pe, t, att[p])
                reach(pe, sig["z"], t)
                turn.product(pe, t, y_ps, w, [(0, 0, NS)], "y")

            rolled(pe, T, [(product, 0)])

        @block.scalar
        def _(act):
            def store(t, p):
                reach(act, sig["norm_applied"], t + 1)
                act.dma_start(pr.rows(pr.output, t), o[p][:, :, :].rearrange("p j c -> p (j c)")).then_inc(sig[f"stored{p}"], 16)

            rolled(act, T, [(lambda t, p: turn.take(act, t, "y"), 0), (store, 2)])
            for p in range(2):
                act.wait_ge(sig[f"stored{p}"], 16 * (T // 2))

        @block.vector
        def _(dve):
            w_scale(dve)

            def attend(t, p):
                reach(dve, sig[f"loaded{p}"], dma_count(t, p, 32))
                reach(dve, sig["turn_turned"], t - 1)
                dve.tensor_scalar(den[:, 0, :, :], agg[p][:, :, D:D + HEADS], 1e-16, None, ALU.add).then_inc(sig["den"], 1)
                reach(dve, sig["den"], t + 1)
                dve.reciprocal(den[:, 1, :, :], den[:, 0, :, :]).then_inc(sig["den_inverse"], 1)
                reach(dve, sig["den_inverse"], t + 1)
                share = den[:, 1, :, :].unsqueeze(3)
                for c, per_head in [(0, 16)] + [(NS + NV * i, 8) for i in range(3)]:
                    cols = slice(c, c + HEADS * per_head)
                    ins = dve.tensor_tensor(att[p][:, :, cols].rearrange("p j (h k) -> p j h k", h=HEADS),
                                            agg[p][:, :, cols].rearrange("p j (h k) -> p j h k", h=HEADS),
                                            share.to_broadcast([P, SUB, HEADS, per_head]), ALU.mult)
                ins.then_inc(sig["attended"], 1)

            def residual(t, p):
                reach(dve, sig["norm_applied"], t - 1)
                reach(dve, sig["y"], t + 1)
                dve.scalar_tensor_tensor(out=z[p][:, :, :], in0=x[p][:, :, :], scalar=2.0, in1=y_ps[:, :, 0:D],
                                         op0=ALU.mult, op1=ALU.add).then_inc(sig["z"], 1)
                reach(dve, sig["z"], t + 1)
                norm.statistics(dve, t, p, z[p])

            def normalise(t, p):
                reach(dve, sig[f"stored{p}"], dma_count(t - 2, p, 16))
                norm.apply(dve, t, p, o[p], z[p])

            rolled(dve, T, [(attend, 0), (residual, 1), (normalise, 2)])

    finish_pass(nc, sig)


def tiles_before_first(t):
    if isinstance(t, int):
        return -SUB if t < 0 else SUB * (t + max(t - 2, 0))
    return 2 * SUB * t - 2 * SUB


def tiles_before_second(t, T):
    if isinstance(t, int):
        return -SUB if t < 0 else SUB * (min(t + 3, T) + t)
    return 2 * SUB * t + 3 * SUB


def edges_layer3(pr):
    nc, T, d, pr.name = pr.nc, pr.T, pr.d, "l3"
    r3, r2 = 3.0 ** -0.5, 2.0 ** -0.5
    with ExitStack() as ctx:
        sig = Signals(nc, ctx)
        sb = lambda n, shape, dt=F32: ctx.enter_context(nc.sbuf_tensor(f"l3_{n}", shape, dt))
        ps = lambda n, shape: ctx.enter_context(nc.psum_tensor(f"l3_{n}", shape, F32))
        two = lambda n, shape: [sb(f"{n}{p}", shape) for p in range(2)]
        width = D + HEADS
        ec = EdgeCommon(pr, ctx, sig, [(pr.table_a, 0), (pr.table_c, 2)], width, "rows", banks=1)
        tp1 = TensorProduct(pr, ctx, sig, True, "tp1")
        tp2 = TensorProduct(pr, ctx, sig, True, "tp2")
        feat = two("feat", [16, STEP])
        rows = sb("rows", [P, SUB, D + 2 * NV])
        rows2 = sb("rows2", [P, SUB, D + 2 * NV])
        turned = [sb(f"turned{k}", [P, 4 * P]) for k in range(2)]
        leak, relu, logits = two("leak", [P, SUB, NS]), two("relu", [P, SUB, NS]), two("logits", [P, SUB, HEADS])
        leaky = sb("leaky", [P, SUB, NS])
        values, half_tanh, gates = two("values", [P, SUB, 96]), two("half_tanh", [P, SUB, 96]), sb("gates", [P, SUB, NV])
        mask, running, top = sb("mask", [HEADS, STEP + 1]), sb("running", [HEADS, STEP]), two("top", [HEADS, STEP])
        fall = two("fall", [HEADS, 1])
        below, ex, shrink = sb("below", [P, SUB, HEADS]), two("ex", [P, SUB, HEADS]), two("shrink", [1, HEADS])
        weighted, handed = two("weighted", [P, SUB, width]), two("handed", [1, width])
        dots = sb("dots", [P, NS])
        scale_col = sb("scale_col", [P, 2])
        sval_t = sb("sval_t", [NS, 96])
        wh_ps = ps("wh_ps", [P, SUB, 256])
        a_ps = ps("a_ps", [P, SUB, 256])
        turn_ps = [ps(f"turn_ps{k}", [P, 4 * P]) for k in range(2)]
        small_ps = ps("small_ps", [P, STEP])
        c_rbf, c_a, c_vv, c_hs, c_hv, c_g = 0, 224, 384, 416, 480, 512
        w, w_zero, w_load, w_scale, w_n = weight_tile(pr, ctx, sig, "l3_w", 544, [
            (0, c_rbf, d["L3_gnn_W_rbf"], 1.0),
            (0, c_a, d["L3_gnn_W_alpha"][0:NS, :], 1.0), (NS, c_a, d["L3_gnn_W_alpha"][NS:96, :], r3),
            (0, c_a + 64, d["L3_gnn_Ws_val"][0:NS, :], 1.0), (NS, c_a + 64, d["L3_gnn_Ws_val"][NS:96, :], r3),
            (0, c_vv, d["L3_gnn_Wv_val"][0:96, :], 1.0), (96, c_vv, d["L3_gnn_Wv_val"][96:P, :], r2),
            (0, c_hs, d["L3_gnn_Ws_vlin"][0:NS, :], 1.0), (NS, c_hs, d["L3_gnn_Ws_vlin"][NS:96, :], r3),
            (0, c_hv, d["L3_gnn_Wv_vlin"][0:96, :], 1.0), (96, c_hv, d["L3_gnn_Wv_vlin"][96:P, :], r2),
            (0, c_g, d["L3_gnn_Wg"], 1.0)])
        columns = [(0, 0, "w2_ss"), (NS, 0, "w2_vv0"), (0, 1, "w2_sv"), (NS, 1, "w2_vs"), (96, 1, "w2_vv1")]
        block = ctx.enter_context(nc.Block())

        @block.sync
        def _(sp):
            w_load(sp)
            for r, c, n in columns:
                v = d[f"L3_gnn_{n}"].rearrange("a c -> c a")
                sp.dma_start(scale_col[r:r + v.shape[0], c:c + 1], v).then_inc(sig["constants"], 16)
            sp.dma_start(dots[:, :], d["alpha_dot"].to_broadcast([P, NS])).then_inc(sig["constants"], 16)
            sp.dma_start(sval_t[:, :], d["Ws_val_T"]).then_inc(sig["constants"], 16)

            def load(t, p):
                reach(sp, sig["w"], t - 1)
                sp.dma_start(feat[p][:, :], d["edge_attr_16"][:, bass.ds(t * STEP, STEP)]).then_inc(sig[f"feat_loaded{p}"], 16)

            rolled(sp, T, [(load, 0), (lambda t, p: ec.load_dst(sp, t, p), 3)])

        @block.gpsimd
        def _(pool):
            w_zero(pool)
            ec.start_out(pool)
            for tp in (tp1, tp2):
                for p in range(2):
                    pool.memset(tp.msg[p][:, :, :, :], 0.0).then_inc(sig["msg_zeroed"], 1)
            pool.memset(top[1][:, :], -BIG).then_inc(sig["msg_zeroed"], 1)
            rolled(pool, T, [(lambda t, p: ec.gather(pool, t, p), 0), (lambda t, p: ec.scatter(pool, t, p), 6)])
            ec.all_scattered(pool)

        @block.tensor
        def _(pe):
            pe.wait_ge(sig["weights_ready"], w_n)
            pe.wait_ge(sig["constants"], 16 * 7)
            pe.wait_ge(sig["out_zeroed"], 2)
            pe.matmul(wh_ps[0:96, 0, 0:NV], sval_t[:, :], w[0:NS, c_g:c_g + NV], start=True, stop=True).then_inc(sig["gate_map"], 1)
            pe.wait_ge(sig["maps_made"], 4)

            def weights(t, p):
                reach(pe, sig[f"feat_loaded{p}"], dma_count(t, p, 16))
                reach(pe, sig["messages"], t)
                reach(pe, sig["weighted"], t - 3)
                for j in range(SUB):
                    mm = pe.matmul(wh_ps[:, j, 0:224], feat[p][:, j * P:(j + 1) * P], w[0:16, c_rbf:c_rbf + 224],
                                   start=True, stop=True)
                mm.then_inc(sig["w"], 1)

            def turn(t, k, msg, taken):
                j = SUB - 1 - k
                reach(pe, sig["turn_taken"], taken - 1)
                for q in range(4):
                    mm = pe.transpose(turn_ps[k % 2][:, q * P:(q + 1) * P], msg[:, j, q, :], pr.ident[:, :])
                mm.then_inc(sig["turned"], 1)

            def logits_values(t, p):
                reach(pe, sig["messages"], t + 1)
                reach(pe, sig["values_taken"], t)
                base = tiles_before_first(t)
                for k in range(SUB + 1):
                    if k < SUB:
                        turn(t, k, tp1.msg[p], base + k)
                    if k:
                        j, m = SUB - k, turned[(k - 1) % 2]
                        reach(pe, sig["turn_taken"], base + k)
                        pe.matmul(a_ps[:, j, 0:D], m[:, 0:P], w[:, c_a:c_a + D], start=True, stop=True)
                        for i in range(3):
                            mm = pe.matmul(a_ps[:, j, D + NV * i:D + NV * (i + 1)], m[:, (1 + i) * P:(2 + i) * P],
                                           w[:, c_vv:c_vv + NV], start=True, stop=True)
                        mm.then_inc(sig["mapped"], 1)

            def heads(t, p):
                reach(pe, sig["messages2"], t + 1)
                reach(pe, sig["messages"], t + 4 if not isinstance(t, int) else min(t + 4, T))
                base = tiles_before_second(t, T)
                for k in range(SUB + 1):
                    if k < SUB:
                        turn(t, k, tp2.msg[p], base + k)
                    if k:
                        j, m = SUB - k, turned[(k - 1) % 2]
                        reach(pe, sig["turn_taken"], base + k)
                        pe.matmul(wh_ps[:, j, 0:NS], m[:, 0:P], w[:, c_hs:c_hs + NS], start=True, stop=True)
                        for i in range(3):
                            mm = pe.matmul(wh_ps[:, j, NS + NV * i:NS + NV * (i + 1)], m[:, (1 + i) * P:(2 + i) * P],
                                           w[:, c_hv:c_hv + NV], start=True, stop=True)
                        mm.then_inc(sig["mapped"], 1)

            def turn_logits(t, p):
                reach(pe, sig["logits"], t + 1)
                reach(pe, sig["below"], t)
                reach_gate(pe, sig["shrink"], t, sig["pe_gate"])
                for j in range(SUB):
                    mm = pe.transpose(small_ps[0:HEADS, j * P:(j + 1) * P], logits[p][:, j, :], pr.ident[:, :])
                mm.then_inc(sig["logits_turned"], 1)

            def sums(t, p):
                reach(pe, sig["weighted"], t + 1)
                reach(pe, sig["handed"], t + 1)
                reach(pe, sig["sel_made"], t + 1)
                for k in range(SUB):
                    j = SUB - 1 - k
                    reach(pe, sig["out_ready"], SUB * t + k)
                    pe.matmul(ec.o_ps[k % 2][:, 0:width], ec.sel[p][:, j, :], weighted[p][:, j, :], start=True, stop=False)
                    ec.carry(pe, t, p, k, handed[p][:, :]).then_inc(sig["summed"], 1)

            def turn_top(t, p):
                reach_gate(pe, sig["fall"], t + 1, sig["pe_gate"])
                for j in range(SUB):
                    pe.transpose(small_ps[:, HEADS * j:HEADS * (j + 1)], top[p][:, j * P:(j + 1) * P], pr.ident[0:HEADS, 0:HEADS])
                pe.transpose(small_ps[0:1, 32:36], fall[p][:, :], pr.ident[0:HEADS, 0:HEADS]).then_inc(sig["top_turned"], 1)

            rolled(pe, T, [(logits_values, 2), (turn_top, 4), (heads, 4), (sums, 5), (turn_logits, 3), (weights, 0)])

        @block.scalar
        def _(act):
            def take(t, base):
                for k in range(SUB):
                    reach(act, sig["turned"], base + k + 1)
                    reach(act, sig["mapped"], base + k - 1)
                    act.activation(turned[k % 2][:, :], turn_ps[k % 2][:, :], ACT.Copy).then_inc(sig["turn_taken"], 1)

            def exponentials(t, p):
                reach(act, sig["below"], t + 1)
                reach(act, sig["weighted"], t - 1)
                act.activation(ex[p][:, :, :], below[:, :, :], ACT.Exp).then_inc(sig["ex"], 1)
                reach(act, sig["top_turned"], t + 1)
                reach(act, sig["handed"], t - 1)
                act.activation(shrink[p][:, :], small_ps[0:1, 32:36], ACT.Exp).then_inc(sig["shrink"], 1)

            def gate(t, p):
                reach(act, sig["mapped"], tiles_before_first(t) + SUB)
                reach(act, sig["values"], t - 1)
                act.activation(leak[p][:, :, :], a_ps[:, :, 0:NS], ACT.Copy, scale=0.2)
                act.activation(relu[p][:, :, :], a_ps[:, :, 0:NS], ACT.Relu, scale=0.8).then_inc(sig["relu"], 1)
                act.activation(half_tanh[p][:, :, :], a_ps[:, :, NS:D], ACT.Tanh, scale=0.5)
                act.activation(values[p][:, :, :], a_ps[:, :, D:256], ACT.Copy).then_inc(sig["values_taken"], 1)

            def take_out(t, p):
                for k in range(SUB):
                    ec.take_out(act, t, p, k)

            act.wait_ge(sig["out_zeroed"], 2)
            rolled(act, T, [(lambda t, p: take(t, tiles_before_first(t)), 2), (gate, 2),
                            (lambda t, p: take(t, tiles_before_second(t, T)), 4), (exponentials, 4), (take_out, 5)])

        @block.vector
        def _(dve):
            w_scale(dve)
            dve.wait_ge(sig["constants"], 16 * 7)
            dve.wait_ge(sig["gate_map"], 1)
            dve.wait_ge(sig["weights_ready"], w_n)
            dve.tensor_copy(w[0:NS, c_a + P:c_a + D], wh_ps[0:NS, 0, 0:NV]).then_inc(sig["maps_made"], 1)
            dve.tensor_scalar(w[NS:96, c_a + P:c_a + D], wh_ps[NS:96, 0, 0:NV], r3, None, ALU.mult).then_inc(sig["maps_made"], 1)
            dve.tensor_scalar(w[0:96, c_hs:c_hs + NS], w[0:96, c_hs:c_hs + NS], scale_col[0:96, 0:1], None, ALU.mult).then_inc(
                sig["maps_made"], 1)
            dve.tensor_scalar(w[:, c_hv:c_hv + NV], w[:, c_hv:c_hv + NV], scale_col[:, 1:2], None, ALU.mult).then_inc(
                sig["maps_made"], 1)
            dve.wait_ge(sig["msg_zeroed"], 5)

            def subtract_top(t, p):
                reach(dve, sig["top_turned"], t + 1)
                reach(dve, sig["ex"], t)
                dve.tensor_tensor(below[:, :, :], logits[p][:, :, :],
                                  small_ps[:, 0:SUB * HEADS].rearrange("p (j h) -> p j h", j=SUB),
                                  ALU.subtract).then_inc(sig["below"], 1)

            def first_product(t, p):
                a, b = ec.rows_in[0][p], ec.rows_in[1][p]
                ec.gathered(dve, t, p)
                dve.tensor_tensor(rows[:, :, D:D + 2 * NV], a[:, :, NS:NS + 2 * NV], b[:, :, NS:NS + 2 * NV], ALU.add)
                dve.tensor_tensor(rows[:, :, 0:D], a[:, :, :], b[:, :, :], ALU.add).then_inc(sig["rows"], 1)
                reach(dve, sig["rows"], t + 1)
                reach(dve, sig["w"], t + 1)
                reach(dve, sig["mapped"], tiles_before_first(t - 2) + SUB)
                tp1.emit(dve, t, p, rows, wh_ps, "messages")

            def softmax_values(t, p):
                reach(dve, sig["relu"], t + 1)
                dve.tensor_tensor(leaky[:, :, :], leak[p][:, :, :], relu[p][:, :, :], ALU.add).then_inc(sig["leaky"], 1)
                reach(dve, sig["leaky"], t + 1)
                dve.tensor_tensor(leaky[:, :, :], leaky[:, :, :], dots[:, :].unsqueeze(1).to_broadcast([P, SUB, NS]),
                                  ALU.mult).then_inc(sig["dotted"], 1)
                reach(dve, sig["values_taken"], t + 1)
                dve.tensor_scalar(gates[:, :, :], half_tanh[p][:, :, NS:96], 0.5, 0.5, ALU.mult, ALU.add).then_inc(sig["gates"], 1)
                reach(dve, sig["dotted"], t + 1)
                dve.tensor_reduce(logits[p][:, :, :], leaky[:, :, :].rearrange("p j (h k) -> p j h k", h=HEADS), AXX,
                                  ALU.add).then_inc(sig["logits"], 1)
                dve.tensor_scalar(rows2[:, :, 0:NS], half_tanh[p][:, :, 0:NS], 0.5, 0.5, ALU.mult, ALU.add)
                reach(dve, sig["gates"], t + 1)
                v5 = rows2[:, :, NS:D + 2 * NV].rearrange("p j (i c) -> p j i c", i=5)
                vals = values[p][:, :, :].rearrange("p j (i c) -> p j i c", i=3)
                g = gates[:, :, :].unsqueeze(2)
                dve.tensor_tensor(v5[:, :, 3:5, :], vals[:, :, 0:2, :], g.to_broadcast([P, SUB, 2, NV]), ALU.mult)
                dve.tensor_tensor(v5[:, :, 0:3, :], vals, g.to_broadcast([P, SUB, 3, NV]), ALU.mult).then_inc(sig["values"], 1)
                reach(dve, sig["values"], t + 1)
                reach(dve, sig["mapped"], tiles_before_second(t - 2, T) + SUB)
                tp2.emit(dve, t, p, rows2, None, "messages2")

            def maxima(t, p):
                reach(dve, sig[f"dst_loaded{p}"], dma_count(t, p, 16))
                dr = ec.drow[p]
                dve.tensor_tensor(mask[:, :], dr[0:HEADS, 0:STEP + 1], dr[0:HEADS, 1:STEP + 2], ALU.is_equal).then_inc(sig["mask"], 1)
                reach(dve, sig["mask"], 2 * t + 1)
                dve.tensor_scalar(mask[:, :], mask[:, :], 0.5, BIG, ALU.subtract, ALU.mult).then_inc(sig["mask"], 1)
                reach(dve, sig["logits_turned"], t + 1)
                reach(dve, sig["mask"], 2 * t + 2)
                reach(dve, sig["top"], t)
                dve.tensor_tensor_scan(out=running[:, ::-1], data0=mask[:, STEP:0:-1], data1=small_ps[0:HEADS, ::-1],
                                       initial=top[1 - p][:, 0:1], op0=ALU.min, op1=ALU.max).then_inc(sig["running"], 1)
                reach(dve, sig["running"], t + 1)
                reach(dve, sig["top_turned"], t - 1)
                dve.tensor_tensor_scan(out=top[p][:, :], data0=mask[:, 0:STEP], data1=running[:, :], initial=-BIG,
                                       op0=ALU.min, op1=ALU.max).then_inc(sig["top"], 1)
                reach(dve, sig["top"], t + 1)
                dve.tensor_scalar(fall[p][:, :], top[1 - p][:, 0:1], top[p][:, STEP - 1:STEP], 0.0, ALU.subtract,
                                  ALU.min).then_inc(sig["fall"], 1)

            def weigh(t, p):
                ec.make_sel(dve, t, p)
                reach(dve, sig["ex"], t + 1)
                reach(dve, sig["mapped"], tiles_before_second(t, T) + SUB)
                e = ex[p][:, :, :].unsqueeze(3)
                for c, per_head in [(0, 16)] + [(NS + NV * i, 8) for i in range(3)]:
                    cols = slice(c, c + HEADS * per_head)
                    dve.tensor_tensor(weighted[p][:, :, cols].rearrange("p j (h k) -> p j h k", h=HEADS),
                                      wh_ps[:, :, cols].rearrange("p j (h k) -> p j h k", h=HEADS),
                                      e.to_broadcast([P, SUB, HEADS, per_head]), ALU.mult)
                dve.tensor_copy(weighted[p][:, :, D:width], ex[p][:, :, :]).then_inc(sig["weighted"], 1)

            def hand_down(t, p):
                reach(dve, sig["shrink"], t + 1)
                reach(dve, sig["out_ready"], SUB * t)
                above = ec.out[1 - p][0:1, 0, :]
                f = shrink[p][:, :].unsqueeze(2)
                for c, per_head in [(0, 16)] + [(NS + NV * i, 8) for i in range(3)] + [(D, 1)]:
                    cols = slice(c, c + HEADS * per_head)
                    ins = dve.tensor_tensor(handed[p][:, cols].rearrange("p (h k) -> p h k", h=HEADS),
                                            above[:, cols].rearrange("p (h k) -> p h k", h=HEADS),
                                            f.to_broadcast([1, HEADS, per_head]), ALU.mult)
                ins.then_inc(sig["handed"], 1)

            rolled(dve, T, [(hand_down, 5), (first_product, 1), (maxima, 4), (softmax_values, 3), (subtract_top, 4), (weigh, 4)])

    finish_pass(nc, sig)


def build(nc, d, out, T):
    with ExitStack() as ctx:
        pr = Program(nc, d, T, out, ctx)
        n = T * STEP
        pr.table_a = nc.dram_tensor("table_a", (n, D), F32, kind="Internal").ap()
        pr.table_b = nc.dram_tensor("table_b", (n, D), F32, kind="Internal").ap()
        pr.table_c = nc.dram_tensor("table_c", (n, D), F32, kind="Internal").ap()
        pr.table_x = nc.dram_tensor("table_x", (n, D), F32, kind="Internal").ap()
        pr.agg = nc.dram_tensor("agg", (n, AGG_W), F32, kind="Internal").ap()
        pr.rows = lambda table, t: table.rearrange("(t p j) c -> t p (j c)", p=P, j=SUB)[bass.ds(t, 1)].rearrange("a p c -> (a p) c")
        pr.ident = ctx.enter_context(nc.sbuf_tensor("ident", [P, P], F32))
        pr.index = ctx.enter_context(nc.sbuf_tensor("index", [P, T * 3 * SUB], I32))
        pr.dst_f = ctx.enter_context(nc.sbuf_tensor("dst_f", [P, T * SUB], F32))
        pr.edge4 = ctx.enter_context(nc.sbuf_tensor("edge4", [P, T * SUB * 6], F32))
        pr.attr = ctx.enter_context(nc.sbuf_tensor("attr", [P, T * SUB], F32))
        prepare(pr)
        r3, r2 = 3.0 ** -0.5, 2.0 ** -0.5
        k_s, k_v = 0.25 * 96 ** -0.5, 0.25 * 128 ** -0.5
        l2s, l2v = d["L0_gnn_lin2_ws"], d["L0_gnn_lin2_wv"]
        edges_conv(pr, "l0", d["L0_gnn_fc_w1"], d["L0_gnn_fc_w2"], NS, d["edge_attr_64"], True,
                   [(0, 0, l2s[0:NS, :], k_s), (NS, 0, l2s[NS:96, :], k_s * r3)],
                   [(0, l2v[0:NS, :], k_v), (NS, l2v[NS:96, :], k_v), (96, l2v[96:128, :], k_v * r2)], 96)
        nodes_layer0(pr)
        edges_layer1(pr)
        nodes_layer1(pr)
        k_m = 96 ** -0.5
        wa, ws, wv = d["L2_gnn_Wa"], d["L2_gnn_Wl2_s"], d["L2_gnn_Wl2_v"]
        edges_conv(pr, "l2", d["L2_gnn_Wfc1"], d["L2_gnn_Wfc2"], 16, d["edge_attr_16"], False,
                   [(0, 0, wa[0:NS, :], k_m), (NS, 0, wa[NS:96, :], k_m * r3), (96, 1, d["one"], 1.0),
                    (0, 2, ws[0:NS, :], k_m), (NS, 2, ws[NS:96, :], k_m * r3)],
                   [(0, wv, k_m)], NS + 2)
        nodes_layer2(pr)
        edges_layer3(pr)
        nodes_layer3(pr)


WEIGHTS = """
L0_gnn_lin1_ws L0_gnn_lin1_wv L0_gnn_fc_w1 L0_gnn_fc_w2 L0_gnn_sc_ws L0_gnn_sc_wv L0_gnn_lin2_ws
L0_gnn_lin2_wv L1_gnn_W_ss L1_gnn_W_sv L1_gnn_W_vs L1_gnn_W_vv L1_gnn_L_s L1_gnn_L_v L2_gnn_Wfc1 L2_gnn_Wfc2
L2_gnn_Wsc0 L2_gnn_Wsc1 L2_gnn_Wl1_0 L2_gnn_Wl1_1 L2_gnn_Wl2_s L2_gnn_Wl2_v L2_gnn_Wa L3_gnn_gamma_s
L3_gnn_beta_s L3_gnn_gamma_v L3_gnn_Ws_src L3_gnn_Wv_src L3_gnn_Ws_dst L3_gnn_Wv_dst L3_gnn_W_rbf
L3_gnn_W_alpha L3_gnn_alpha_dot L3_gnn_Ws_val L3_gnn_Wv_val L3_gnn_Wg L3_gnn_w2_ss L3_gnn_w2_sv L3_gnn_w2_vs
L3_gnn_w2_vv0 L3_gnn_w2_vv1 L3_gnn_Ws_vlin L3_gnn_Wv_vlin L3_gnn_Wps L3_gnn_Wpv
""".split()


def kernel(**inputs):
    import concourse.bacc as bacc
    from concourse.bass_utils import run_bass_kernel_spmd

    a = {k: np.asarray(v) for k, v in inputs.items()}
    n, e = a["x"].shape[0], a["src"].shape[0]
    steps = -(-max(n, e) // STEP)
    steps += steps % 2
    size = steps * STEP

    def padded(v, fill=0):
        return np.concatenate([v, np.full((size - v.shape[0],) + v.shape[1:], fill, v.dtype)])

    def by_component(v):
        vec = v[..., NS:].reshape(v.shape[:-1] + (NV, 3))
        return np.concatenate([v[..., :NS], np.swapaxes(vec, -1, -2).reshape(v.shape[:-1] + (3 * NV,))], -1)

    def steps_down(v):
        v = v.reshape((steps, SUB, P) + v.shape[1:])[::-1]
        return np.moveaxis(v, 2, 0)

    def columns_down(v):
        c = v.shape[1]
        return np.ascontiguousarray(v.reshape(steps, STEP, c)[::-1].reshape(size, c).T)

    src, dst = padded(a["src"]), padded(a["dst"], n)
    before = np.concatenate([np.full(1, -1, dst.dtype), dst[:-1]])
    index = np.stack([steps_down(src), steps_down(before), steps_down(dst)], 2)
    around = np.concatenate([np.full(1, -1, dst.dtype), dst, np.full(1, -2, dst.dtype)])
    e4 = steps_down(padded(a["edge_attr_4"]))
    x = padded(by_component(a["x"]))
    d = {
        "x": x,
        "xT": np.ascontiguousarray(x.reshape(steps, P, SUB, D).transpose(3, 0, 2, 1).reshape(D, size)),
        "node_attr": np.ascontiguousarray(padded(a["node_vec1"]).reshape(steps, P, SUB).transpose(1, 0, 2).reshape(P, -1)),
        "edge_index": np.ascontiguousarray(index.reshape(P, -1)),
        "dst_rows": np.ascontiguousarray(np.stack([around[t * STEP:(t + 1) * STEP + 2] for t in range(steps)])[::-1]),
        "edge_attr_4": np.ascontiguousarray(np.concatenate([e4, e4[..., 1:3]], -1).reshape(P, -1)),
        "edge_attr_16": columns_down(padded(a["edge_attr_16"])),
        "edge_attr_64": columns_down(padded(a["edge_attr_64"])),
        "identity": np.eye(P, dtype=np.float32),
        "one": np.ones((1, 1), np.float32),
        "alpha_dot": a["L3_gnn_alpha_dot"].reshape(1, NS),
        "Ws_val_T": np.ascontiguousarray(a["L3_gnn_Ws_val"].T),
        "L1_rad": np.concatenate([by_component(a["L1_gnn_W_rad"].T), by_component(a["L1_gnn_b_rad"][None])]),
    }
    for k in WEIGHTS:
        d[k] = a[k].reshape(-1, a[k].shape[-1])
    nc = bacc.Bacc("TRN2", target_bir_lowering=False, num_devices=1)
    aps = {k: nc.dram_tensor(f"in_{k}", v.shape, mybir.dt.from_np(v.dtype), kind="ExternalInput").ap() for k, v in d.items()}
    out = nc.dram_tensor("out", (size, D), F32, kind="ExternalOutput").ap()
    build(nc, aps, out, steps)
    got = run_bass_kernel_spmd(nc, [{f"in_{k}": v for k, v in d.items()}], core_ids=[0]).results[0]["out"][:n]
    vec = got[:, NS:].reshape(n, 3, NV)
    return np.concatenate([got[:, :NS], np.swapaxes(vec, 1, 2).reshape(n, 3 * NV)], 1)
```

```python
from contextlib import ExitStack

import numpy as np

import concourse.bass as bass
from concourse import mybir

F32 = mybir.dt.float32
I32 = mybir.dt.int32
ALU = mybir.AluOpType
ACT = mybir.ActivationFunctionType
AXX = mybir.AxisListType.X

P = 128
SUB = 4
STEP = P * SUB
NS, NV = 64, 32
D = NS + 3 * NV
SCR = 1 << 20
AGG_W = 192
EPS = 1e-5
HEADS = 4
BIG = 3.0e38


class Signals(dict):

    def __init__(self, nc, ctx):
        self.nc, self.ctx, self.kept = nc, ctx, []

    def __missing__(self, name):
        self[name] = self.ctx.enter_context(self.nc.semaphore(name))
        return self[name]


def reach(eng, sem, count):
    if isinstance(count, int) and count <= 0:
        return
    eng.wait_ge(sem, count)


def reach_gate(eng, sem, count, gate):
    if isinstance(count, int) and count <= 0:
        return
    eng.wait_ge(sem, count)
    eng.sem_inc(gate, 1)


def dma_count(t, p, each):
    if isinstance(t, int):
        return each * (t // 2 + 1) if t >= 0 else 0
    return (t - p) * (each // 2) + each


def rolled(eng, steps, stages):
    deep = max(sum(stage[1:]) for stage in stages)
    head = (deep + 3) // 2 * 2

    def one(s, k):
        for f, lag, *also in stages:
            t = s + k - lag
            if isinstance(t, int) and not 0 <= t < steps + sum(also):
                continue
            f(t, (k - lag) % 2)

    for s in range(head):
        one(0, s)
    with eng.Fori(head, steps - 1, 2) as i:
        one(i, 0)
        one(i, 1)
    for s in range(deep):
        one(steps, s)


def present(t, steps):
    return not isinstance(t, int) or 0 <= t < steps


class Program:

    def __init__(self, nc, d, steps, output, lasting):
        self.nc, self.d, self.T, self.output, self.lasting = nc, d, steps, output, lasting


def finish_pass(nc, sig):
    nc.all_engine_barrier()
    for name, sem in sig.items():
        if name not in sig.kept:
            nc.gpsimd.sem_clear(sem)
    nc.all_engine_barrier()


def weight_tile(pr, ctx, sig, name, cols, parts):
    tile = ctx.enter_context(pr.nc.sbuf_tensor(name, [P, cols], F32))

    def zero(pool):
        pool.memset(tile[:, :], 0.0).then_inc(sig["weights_zeroed"], 1)

    def load(sp):
        sp.wait_ge(sig["weights_zeroed"], 1)
        for r, c, ap, _ in parts:
            sp.dma_start(tile[r:r + ap.shape[0], c:c + ap.shape[1]], ap).then_inc(sig["weights_loaded"], 16)

    def scale(dve):
        dve.wait_ge(sig["weights_loaded"], 16 * len(parts))
        for r, c, ap, factor in parts:
            part = tile[r:r + ap.shape[0], c:c + ap.shape[1]]
            dve.tensor_scalar(part, part, float(factor), None, ALU.mult).then_inc(sig["weights_ready"], 1)

    return tile, zero, load, scale, len(parts)


def block_diagonal(c, ap, factor):
    n = ap.shape[1]
    return [(NV * i, c + n * i, ap, factor) for i in range(3)]


def prepare(pr):
    nc, T, pr.name = pr.nc, pr.T, "p"
    with ExitStack() as ctx:
        sig = Signals(nc, ctx)
        sb = lambda name, shape, dt=F32: ctx.enter_context(nc.sbuf_tensor(name, shape, dt))
        zeros = sb("zeros", [P, T * SUB * AGG_W // 12])
        same = sb("same_as_previous", [P, T, SUB])
        xs = [sb(f"p_xs{p}", [NS, STEP]) for p in range(2)]
        xv = [sb(f"p_xv{p}", [3 * NV, STEP]) for p in range(2)]
        hs = [sb(f"p_h{p}", [P, SUB, D]) for p in range(2)]
        acc = [ctx.enter_context(nc.psum_tensor(f"p_acc{p}", [P, SUB, 256], F32)) for p in range(2)]
        w, w_zero, w_load, w_scale, w_n = weight_tile(pr, ctx, sig, "p_w", D, [
            (0, 0, pr.d["L0_gnn_lin1_ws"], NS ** -0.5)] + block_diagonal(NS, pr.d["L0_gnn_lin1_wv"], NV ** -0.5))
        block = ctx.enter_context(nc.Block())
        agg_flat = pr.agg.rearrange("(p r) c -> p (r c)", p=P)
        piece = T * SUB * AGG_W // 12

        @block.gpsimd
        def _(pool):
            w_zero(pool)
            pool.memset(zeros[:, :], 0.0).then_inc(sig["zeros_made"], 1)

        @block.sync
        def _(sp):
            w_load(sp)
            sp.dma_start(pr.ident[:, :], pr.d["identity"]).then_inc(sig["resident"], 16)
            sp.dma_start(pr.index[:, :], pr.d["edge_index"]).then_inc(sig["resident"], 16)
            sp.dma_start(pr.edge4[:, :], pr.d["edge_attr_4"]).then_inc(sig["resident"], 16)
            sp.dma_start(pr.attr[:, :], pr.d["node_attr"]).then_inc(sig["resident"], 16)
            sp.wait_ge(sig["zeros_made"], 1)
            for k in range(12):
                sp.dma_start(agg_flat[:, k * piece:(k + 1) * piece], zeros[:, :]).then_inc(sig["agg_zeroed"], 16)

            def load(t, p):
                reach(sp, sig["h_product"], t - 1)
                sp.dma_start(xs[p][:, :], pr.d["xT"][0:NS, bass.ds(t * STEP, STEP)]).then_inc(sig[f"x_loaded{p}"], 16)
                sp.dma_start(xv[p][:, :], pr.d["xT"][NS:D, bass.ds(t * STEP, STEP)]).then_inc(sig[f"x_loaded{p}"], 16)

            rolled(sp, T, [(load, 0)])
            sp.wait_ge(sig["agg_zeroed"], 12 * 16)
            sp.wait_ge(sig["resident"], 4 * 16)

        @block.tensor
        def _(pe):
            pe.wait_ge(sig["weights_ready"], w_n)

            def product(t, p):
                reach(pe, sig[f"x_loaded{p}"], dma_count(t, p, 32))
                reach_gate(pe, sig["h_out"], t - 1, sig["pe_gate"])
                for j in range(SUB):
                    cols = slice(j * P, (j + 1) * P)
                    pe.matmul(acc[p][:, j, 0:NS], xs[p][:, cols], w[0:NS, 0:NS], start=True, stop=True)
                    mm = pe.matmul(acc[p][:, j, NS:D], xv[p][:, cols], w[0:3 * NV, NS:D], start=True, stop=True)
                mm.then_inc(sig["h_product"], 1)

            rolled(pe, T, [(product, 0)])

        @block.vector
        def _(dve):
            w_scale(dve)
            dve.wait_ge(sig["resident"], 4 * 16)
            index = pr.index[:, :].rearrange("p (t k j) -> p t k j", k=3, j=SUB)
            dve.tensor_tensor(same[:, :, :], index[:, :, 1, :], index[:, :, 2, :], ALU.is_equal).then_inc(sig["same"], 1)
            dve.wait_ge(sig["same"], 1)
            dve.scalar_tensor_tensor(out=index[:, :, 1, :], in0=same[:, :, :], scalar=float(SCR), in1=index[:, :, 2, :],
                                     op0=ALU.mult, op1=ALU.add).then_inc(sig["same"], 1)
            dve.tensor_copy(pr.dst_f[:, :].rearrange("p (t j) -> p t j", j=SUB), index[:, :, 2, :]).then_inc(sig["same"], 1)
            dve.wait_ge(sig["same"], 3)

            def out(t, p):
                reach(dve, sig["h_product"], t + 1)
                reach(dve, sig[f"h_stored{p}"], dma_count(t - 2, p, 16))
                dve.tensor_tensor(hs[p][:, :, :], acc[p][:, :, 0:D],
                                  pr.attr[:, bass.ds(t * SUB, SUB)].unsqueeze(2).to_broadcast([P, SUB, D]),
                                  ALU.mult).then_inc(sig["h_out"], 1)

            rolled(dve, T, [(out, 0)])

        @block.scalar
        def _(act):
            def store(t, p):
                reach(act, sig["h_out"], t + 1)
                act.dma_start(pr.rows(pr.table_a, t), hs[p][:, :, :].rearrange("p j c -> p (j c)")).then_inc(
                    sig[f"h_stored{p}"], 16)

            rolled(act, T, [(store, 0)])
            for p in range(2):
                act.wait_ge(sig[f"h_stored{p}"], 16 * (T // 2))

    finish_pass(nc, sig)


class EdgeCommon:

    def __init__(self, pr, ctx, sig, tables, width, rows_read, row_width=D, banks=2):
        nc = pr.nc
        self.pr, self.sig, self.tables, self.width, self.rows_read = pr, sig, tables, width, rows_read
        for n in ("gathered0", "gathered1", "scattered0", "scattered1"):
            sig[n] = pr.lasting.enter_context(nc.semaphore(f"{pr.name}_{n}"))
            sig.kept.append(n)
        sb = lambda name, shape, dt=F32: ctx.enter_context(nc.sbuf_tensor(f"{pr.name}_{name}", shape, dt))
        self.gather_idx = [sb(f"e_gidx{p}", [P, 3 * SUB], I32) for p in range(2)]
        self.scatter_idx = [sb(f"e_sidx{p}", [P, SUB], I32) for p in range(2)]
        self.rows_in = [[sb(f"e_g{k}_{p}", [P, SUB, row_width]) for p in range(2)] for k in range(len(tables))]
        self.drow = [sb(f"e_drow{p}", [P, STEP + 2], I32) for p in range(2)]
        self.sel = [sb(f"e_sel{p}", [P, SUB, P]) for p in range(2)]
        self.cont = [sb(f"e_cont{p}", [1, SUB, P]) for p in range(2)]
        self.out = [sb(f"e_out{p}", [P, SUB, AGG_W]) for p in range(2)]
        self.o_ps = [ctx.enter_context(nc.psum_tensor(f"{pr.name}_e_sums{k}", [P, 512], F32)) for k in range(banks)] * (2 // banks)

    def load_dst(self, sp, t, p):
        sig = self.sig
        reach(sp, sig["sel_made"], t - 1)
        row = self.pr.d["dst_rows"][bass.ds(t, 1), :]
        sp.dma_start(self.drow[p][:, :], row.to_broadcast([P, STEP + 2])).then_inc(sig[f"dst_loaded{p}"], 16)

    def gather(self, pool, t, p):
        sig, pr = self.sig, self.pr
        reach_gate(pool, sig[self.rows_read], t - 1, sig["pool_gate"])
        pool.tensor_copy(self.gather_idx[p][:, :], pr.index[:, bass.ds(t * (3 * SUB), 3 * SUB)]).then_inc(
            sig["index_copied"], 1)
        reach_gate(pool, sig["index_copied"], t + 1, sig["pool_gate"])
        for j in reversed(range(SUB)):
            for k, (table, slot) in enumerate(self.tables):
                pool.indirect_dma_start(
                    out=self.rows_in[k][p][:, j, 0:D], out_offset=None, in_=table,
                    in_offset=bass.IndirectOffsetOnAxis(ap=self.gather_idx[p][:, slot * SUB + j:slot * SUB + j + 1], axis=0),
                ).then_inc(sig[f"gathered{p}"], 16)

    def gathered(self, eng, t, p):
        reach(eng, self.sig[f"gathered{p}"], dma_count(t, p, 16 * SUB * len(self.tables)))

    def scatter(self, pool, t, p):
        sig, pr = self.sig, self.pr
        reach_gate(pool, sig[f"scattered{p}"], dma_count(t - 2, p, 16 * SUB), sig["pool_gate"])
        pool.tensor_copy(self.scatter_idx[p][:, :], pr.index[:, bass.ds(t * (3 * SUB) + SUB, SUB)]).then_inc(
            sig["scatter_index_copied"], 1)
        reach_gate(pool, sig["scatter_index_copied"], t + 1, sig["pool_gate"])
        reach_gate(pool, sig["out_ready"], SUB * t + SUB, sig["pool_gate"])
        for j in range(SUB):
            pool.indirect_dma_start(
                out=pr.agg, out_offset=bass.IndirectOffsetOnAxis(ap=self.scatter_idx[p][:, j:j + 1], axis=0),
                in_=self.out[p][:, j, :], in_offset=None, bounds_check=pr.agg.shape[0] - 1, oob_is_err=False,
            ).then_inc(sig[f"scattered{p}"], 16)

    def start_out(self, pool):
        for p in range(2):
            pool.memset(self.out[p][:, :, :], 0.0).then_inc(self.sig["out_zeroed"], 1)

    def make_sel(self, dve, t, p):
        sig, pr = self.sig, self.pr
        reach(dve, sig[f"dst_loaded{p}"], dma_count(t, p, 16))
        reach(dve, sig["summed"], SUB * t - SUB)
        for j in range(SUB):
            dve.tensor_scalar(self.sel[p][:, j, :], self.drow[p][:, 1 + j * P:1 + (j + 1) * P],
                              pr.dst_f[:, bass.ds(t * SUB + j, 1)], None, ALU.is_equal)
        above = self.drow[p][0:1, 1 + P:2 + STEP:P].unsqueeze(2).to_broadcast([1, SUB, P])
        dve.tensor_tensor(self.cont[p][:, :, :], self.drow[p][0:1, 1:1 + STEP].rearrange("p (j e) -> p j e", j=SUB),
                          above, ALU.is_equal).then_inc(sig["sel_made"], 1)

    def carry(self, pe, t, p, k, handed=None):
        j = SUB - 1 - k
        if k == 0 and handed is not None:
            above = handed
        else:
            above = self.out[p][0:1, j + 1, 0:self.width] if k else self.out[1 - p][0:1, 0, 0:self.width]
            reach(pe, self.sig["out_ready"], SUB * t + k)
        return pe.matmul(self.o_ps[k % 2][:, 0:self.width], self.cont[p][:, j, :], above, start=False, stop=True)

    def take_out(self, act, t, p, k):
        j = SUB - 1 - k
        reach(act, self.sig["summed"], SUB * t + k + 1)
        if k == 0:
            reach(act, self.sig[f"scattered{p}"], dma_count(t - 2, p, 16 * SUB))
        act.activation(self.out[p][:, j, 0:self.width], self.o_ps[k % 2][:, 0:self.width], ACT.Copy).then_inc(
            self.sig["out_ready"], 1)

    def all_scattered(self, pool):
        for p in range(2):
            pool.wait_ge(self.sig[f"scattered{p}"], 16 * SUB * (self.pr.T // 2))


class TensorProduct:

    def __init__(self, pr, ctx, sig, cross, name, split=False):
        nc = pr.nc
        self.pr, self.sig, self.cross, self.name, self.split = pr, sig, cross, name, split
        sb = lambda n, shape: ctx.enter_context(nc.sbuf_tensor(f"{pr.name}_{name}_{n}", shape, F32))
        self.msg = [sb(f"msg{p}", [P, SUB, 3 if split else 4, P]) for p in range(2)]
        self.ws = sb("ws", [P, SUB, 2, NS])
        self.vw = sb("vw", [P, SUB, 3, NV])
        self.ve = sb("ve", [P, SUB, 3, NV])
        self.dot = sb("dot", [P, SUB, NV])
        if cross:
            self.c1 = sb("c1", [P, SUB, 3, NV])
            self.c2 = sb("c2", [P, SUB, 3, NV])

    def groups(self, p):
        return self.msg[p][:, :, 1:3, :].rearrange("p j q c -> p j (q c)").rearrange("p j (g c) -> p j g c", g=4)

    def emit(self, dve, t, p, rows, w, done):
        sig, n, msg = self.sig, self.name, self.msg[p]
        e4 = self.pr.edge4[:, bass.ds(t * (SUB * 6), SUB * 6)].rearrange("p (j k) -> p j k", j=SUB)
        s = self.groups(p)[:, :, 3, :] if self.split and w is None else rows[:, :, 0:NS]
        v5 = rows[:, :, NS:NS + 5 * NV].rearrange("p j (i c) -> p j i c", i=5)
        e0 = lambda c: e4[:, :, 0:1].to_broadcast([P, SUB, c])
        e_i = lambda a, c: e4[:, :, 1 + a:4 + a].unsqueeze(3).to_broadcast([P, SUB, 3, c])
        e0_3 = e4[:, :, 0:1].unsqueeze(3).to_broadcast([P, SUB, 3, NV])
        if self.split:
            scaled, cross = self.groups(p)[:, :, 0:3, 0:NV], self.groups(p)[:, :, 0:3, NV:2 * NV]
        else:
            vec = msg[:, :, 1:4, :]
            scaled, cross = vec[:, :, :, NS:96], vec[:, :, :, 96:P]

        def op(out, a, b, o, name, *after):
            for x in after:
                dve.wait_ge(sig[f"{n}_{x}"], t + 1)
            return dve.tensor_tensor(out, a, b, o).then_inc(sig[done if name == "done" else f"{n}_{name}"], 1)

        if w is not None:
            two_s = s.unsqueeze(2).to_broadcast([P, SUB, 2, NS])
            if self.split:
                op(self.ws[:, :, 0, :], w[:, :, 0:NS], s, ALU.mult, "ws")
                op(self.groups(p)[:, :, 3, :], w[:, :, NS:2 * NS], s, ALU.mult, "v1")
            else:
                op(self.ws[:, :, :, :], w[:, :, 0:2 * NS].rearrange("p j (k c) -> p j k c", k=2), two_s, ALU.mult, "ws")
            w3 = w[:, :, 128:160].unsqueeze(2).to_broadcast([P, SUB, 3, NV])
            op(self.vw[:, :, :, :], w3, v5[:, :, 0:3, :], ALU.mult, "vw")
        op(self.ve[:, :, :, :], v5[:, :, 0:3, :], e_i(0, NV), ALU.mult, "ve")
        if self.cross:
            op(self.c1[:, :, :, :], v5[:, :, 1:4, :], e_i(2, NV), ALU.mult, "c1")
            op(self.c2[:, :, :, :], v5[:, :, 2:5, :], e_i(1, NV), ALU.mult, "c2")
        s0, s1 = (self.ws[:, :, 0, :], self.ws[:, :, 1, :]) if w is not None else (s, s)
        first = ("ws",) if w is not None else ()
        op(msg[:, :, 0, 0:NS], s0, e0(NS), ALU.mult, "s1", *first)
        if not self.split:
            op(vec[:, :, :, 0:NS], s1.unsqueeze(2).to_broadcast([P, SUB, 3, NS]), e_i(0, NS), ALU.mult, "v1", *first)
        op(self.dot[:, :, :], self.ve[:, :, 0, :], self.ve[:, :, 1, :], ALU.add, "dot1", "ve")
        if self.cross:
            if w is not None:
                op(self.c1[:, :, :, :], self.c1[:, :, :, :], self.c2[:, :, :, :], ALU.subtract, "cr", "c1", "c2")
            else:
                op(cross, self.c1[:, :, :, :], self.c2[:, :, :, :], ALU.subtract, "cr", "c1", "c2")
        if w is not None:
            op(scaled, self.vw[:, :, :, :], e0_3, ALU.mult, "v2", "vw")
            op(self.dot[:, :, :], self.dot[:, :, :], self.ve[:, :, 2, :], ALU.add, "dot2", "dot1")
            if self.cross:
                w5 = w[:, :, 192:224].unsqueeze(2).to_broadcast([P, SUB, 3, NV])
                op(cross, w5, self.c1[:, :, :, :], ALU.mult, "v3", "cr")
            last = op(msg[:, :, 0, NS:96], w[:, :, 160:192], self.dot[:, :, :], ALU.mult, "done", "dot2")
        else:
            op(scaled, v5[:, :, 0:3, :], e0_3, ALU.mult, "v2")
            last = op(msg[:, :, 0, NS:96], self.dot[:, :, :], self.ve[:, :, 2, :], ALU.add, "done", "dot1")
        return last


def edges_conv(pr, name, fc1, fc2, hidden_in, edge_features, cross, s_parts, v_parts, s_cols):
    nc, T, pr.name = pr.nc, pr.T, name
    n_w = fc2.shape[1]
    with ExitStack() as ctx:
        sig = Signals(nc, ctx)
        sb = lambda n, shape, dt=F32: ctx.enter_context(nc.sbuf_tensor(f"{name}_{n}", shape, dt))
        ps = lambda n, shape: ctx.enter_context(nc.psum_tensor(f"{name}_{n}", shape, F32))
        width = s_cols + 3 * NV
        ec = EdgeCommon(pr, ctx, sig, [(pr.table_a, 0)], width, "messages", D + 2 * NV)
        tp = TensorProduct(pr, ctx, sig, cross, "tp")
        feat = [sb(f"feat{p}", [hidden_in, STEP]) for p in range(2)]
        hid = [sb(f"hid{p}", [NS, STEP]) for p in range(2)]
        agg = [sb(f"agg{k}", [P, 4 * P]) for k in range(2)]
        hid_ps, w_ps = ps("hid_ps", [P, STEP]), ps("w_ps", [P, SUB, 256])
        agg_ps = [ps(f"agg_ps{k}", [P, 4 * P]) for k in range(2)]
        c_fc1, c_fc2, c_s, c_v = 0, NS, NS + n_w, NS + n_w + s_cols
        w, w_zero, w_load, w_scale, w_n = weight_tile(pr, ctx, sig, f"{name}_w", c_v + NV, [
            (0, c_fc1, fc1, hidden_in ** -0.5), (0, c_fc2, fc2, NS ** -0.5)]
            + [(r, c_s + c, ap, f) for r, c, ap, f in s_parts] + [(r, c_v, ap, f) for r, ap, f in v_parts])
        block = ctx.enter_context(nc.Block())

        @block.sync
        def _(sp):
            w_load(sp)

            def load(t, p):
                ec.load_dst(sp, t, p)
                reach(sp, sig["hidden"], t - 1)
                sp.dma_start(feat[p][:, :], edge_features[:, bass.ds(t * STEP, STEP)]).then_inc(sig[f"feat_loaded{p}"], 16)

            rolled(sp, T, [(load, 0)])

        @block.gpsimd
        def _(pool):
            w_zero(pool)
            ec.start_out(pool)
            for p in range(2):
                pool.memset(tp.msg[p][:, :, :, :], 0.0).then_inc(sig["msg_zeroed"], 1)
            pool.wait_ge(sig["msg_zeroed"], 2)
            if not cross:
                for p in range(2):
                    pool.memset(tp.msg[p][:, :, 0, 96:97], 1.0).then_inc(sig["msg_zeroed"], 1)
            rolled(pool, T, [(lambda t, p: ec.gather(pool, t, p), 0), (lambda t, p: ec.scatter(pool, t, p), 2)])
            ec.all_scattered(pool)

        @block.tensor
        def _(pe):
            pe.wait_ge(sig["weights_ready"], w_n)
            pe.wait_ge(sig["out_zeroed"], 2)

            def hidden(t, p):
                reach(pe, sig[f"feat_loaded{p}"], dma_count(t, p, 16))
                reach_gate(pe, sig["silu_done"], t, sig["pe_gate"])
                pe.matmul(hid_ps[0:NS, :], w[0:hidden_in, c_fc1:c_fc1 + NS], feat[p][:, :], start=True, stop=True).then_inc(
                    sig["hidden"], 1)

            def weights(t, p):
                reach(pe, sig["silu_done"], t + 1)
                reach(pe, sig["messages"], t)
                for j in range(SUB):
                    mm = pe.matmul(w_ps[:, j, 0:n_w], hid[p][:, j * P:(j + 1) * P], w[0:NS, c_fc2:c_fc2 + n_w],
                                   start=True, stop=True)
                mm.then_inc(sig["weights"], 1)

            def sums(t, p, k):
                j = SUB - 1 - k
                reach(pe, sig["agg_taken"], SUB * t + k - 1)
                for q in range(4):
                    mm = pe.matmul(agg_ps[k % 2][:, q * P:(q + 1) * P], tp.msg[p][:, j, q, :], ec.sel[p][:, j, :],
                                   start=True, stop=True)
                mm.then_inc(sig["agg"], 1)

            def linear(t, p, k):
                reach(pe, sig["agg_taken"], SUB * t + k + 1)
                reach(pe, sig["out_ready"], SUB * t + k - 1)
                out, a = ec.o_ps[k % 2], agg[k % 2]
                pe.matmul(out[:, 0:s_cols], a[:, 0:P], w[:, c_s:c_s + s_cols], start=True, stop=False)
                for i in range(3):
                    pe.matmul(out[:, s_cols + NV * i:s_cols + NV * (i + 1)], a[:, (1 + i) * P:(2 + i) * P],
                              w[:, c_v:c_v + NV], start=False, stop=False)
                ec.carry(pe, t, p, k).then_inc(sig["summed"], 1)

            def back(t, p):
                reach(pe, sig["messages"], t + 1)
                reach(pe, sig["sel_made"], t + 1)
                for k in range(SUB + 1):
                    if k < SUB:
                        sums(t, p, k)
                    if k:
                        linear(t, p, k - 1)

            rolled(pe, T, [(hidden, 0), (weights, 1), (back, 2)])

        @block.scalar
        def _(act):
            def silu(t, p):
                reach(act, sig["hidden"], t + 1)
                reach(act, sig["weights"], t - 1)
                act.activation(hid[p][:, :], hid_ps[0:NS, :], ACT.Silu).then_inc(sig["silu_done"], 1)

            def copies(t, p):
                rows = ec.rows_in[0][p]
                ec.gathered(act, t, p)
                act.activation(rows[:, :, D:D + 2 * NV], rows[:, :, NS:NS + 2 * NV], ACT.Copy).then_inc(sig["rows_doubled"], 1)

            def take(t, p):
                for k in range(SUB + 1):
                    if k < SUB:
                        reach(act, sig["agg"], SUB * t + k + 1)
                        reach(act, sig["summed"], SUB * t + k - 1)
                        act.activation(agg[k % 2][:, :], agg_ps[k % 2][:, :], ACT.Copy).then_inc(sig["agg_taken"], 1)
                    if k:
                        ec.take_out(act, t, p, k - 1)

            act.wait_ge(sig["out_zeroed"], 2)
            rolled(act, T, [(silu, 0), (copies, 1), (take, 2)])

        @block.vector
        def _(dve):
            w_scale(dve)
            dve.wait_ge(sig["msg_zeroed"], 2 if cross else 4)

            def messages(t, p):
                ec.make_sel(dve, t, p)
                ec.gathered(dve, t, p)
                reach(dve, sig["rows_doubled"], t + 1)
                reach(dve, sig["messages"], t)
                reach(dve, sig["weights"], t + 1)
                tp.emit(dve, t, p, ec.rows_in[0][p], w_ps, "messages")

            rolled(dve, T, [(messages, 1)])

    finish_pass(nc, sig)


def edges_layer1(pr):
    nc, T, pr.name = pr.nc, pr.T, "l1"
    with ExitStack() as ctx:
        sig = Signals(nc, ctx)
        sb = lambda n, shape, dt=F32: ctx.enter_context(nc.sbuf_tensor(f"l1_{n}", shape, dt))
        ps = lambda n, shape: ctx.enter_context(nc.psum_tensor(f"l1_{n}", shape, F32))
        ec = EdgeCommon(pr, ctx, sig, [(pr.table_x, 0)], D, "products")
        feat = [sb(f"feat{p}", [17, STEP]) for p in range(2)]
        prod = [sb(f"prod{p}", [P, SUB, 4, 96]) for p in range(2)]
        ve, dot = sb("ve", [P, SUB, 3, NV]), sb("dot", [P, SUB, NV])
        pT = [sb(f"pT{k}", [96, 4 * P]) for k in range(2)]
        rad = [sb(f"rad{p}", [P, SUB, D]) for p in range(2)]
        msg = [sb(f"msg{p}", [P, SUB, D]) for p in range(2)]
        rad_ps, m_ps = ps("rad_ps", [P, SUB, 256]), ps("m_ps", [P, SUB, 256])
        pT_ps = [ps(f"pT_ps{k}", [P, 4 * P]) for k in range(2)]
        r2, r3 = 2.0 ** -0.5, 3.0 ** -0.5
        cs, cv, cr = 0, NS, NS + NV
        w, w_zero, w_load, w_scale, w_n = weight_tile(pr, ctx, sig, "l1_w", cr + D, [
            (0, cs, pr.d["L1_gnn_W_ss"], NS ** -0.5 * r2), (NS, cs, pr.d["L1_gnn_W_vv"], r3 * NV ** -0.5 * r2),
            (0, cv, pr.d["L1_gnn_W_sv"], r3 * NS ** -0.5 * r2), (NS, cv, pr.d["L1_gnn_W_vs"], r3 * NV ** -0.5 * r2),
            (0, cr, pr.d["L1_rad"], 1.0)])
        block = ctx.enter_context(nc.Block())

        @block.sync
        def _(sp):
            w_load(sp)
            sp.wait_ge(sig["ones_set"], 2)

            def load(t, p):
                reach(sp, sig["radial"], t - 1)
                sp.dma_start(feat[p][0:16, :], pr.d["edge_attr_16"][:, bass.ds(t * STEP, STEP)]).then_inc(
                    sig[f"feat_loaded{p}"], 16)

            rolled(sp, T, [(load, 0), (lambda t, p: ec.load_dst(sp, t, p), 1)])

        @block.gpsimd
        def _(pool):
            w_zero(pool)
            ec.start_out(pool)
            for p in range(2):
                pool.memset(feat[p][:, :], 1.0).then_inc(sig["ones_set"], 1)
            rolled(pool, T, [(lambda t, p: ec.gather(pool, t, p), 0), (lambda t, p: ec.scatter(pool, t, p), 2)])
            ec.all_scattered(pool)

        @block.tensor
        def _(pe):
            pe.wait_ge(sig["weights_ready"], w_n)
            pe.wait_ge(sig["out_zeroed"], 2)

            def radial(t, p):
                reach(pe, sig[f"feat_loaded{p}"], dma_count(t, p, 16))
                reach(pe, sig["sigmoid_done"], t)
                for j in range(SUB):
                    mm = pe.matmul(rad_ps[:, j, 0:D], feat[p][:, j * P:(j + 1) * P], w[0:17, cr:cr + D],
                                   start=True, stop=True)
                mm.then_inc(sig["radial"], 1)

            def turn(t, p, k):
                j = SUB - 1 - k
                reach(pe, sig["pT_taken"], SUB * t + k - 1)
                for q in range(4):
                    mm = pe.transpose(pT_ps[k % 2][0:96, q * P:(q + 1) * P], prod[p][:, j, q, :], pr.ident[:, :])
                mm.then_inc(sig["pT"], 1)

            def linear(t, p, k):
                j, a = SUB - 1 - k, pT[k % 2]
                reach(pe, sig["pT_taken"], SUB * t + k + 1)
                pe.matmul(m_ps[:, j, 0:NS], a[:, 0:P], w[0:96, cs:cs + NS], start=True, stop=True)
                for i in range(3):
                    mm = pe.matmul(m_ps[:, j, NS + NV * i:NS + NV * (i + 1)], a[:, (1 + i) * P:(2 + i) * P],
                                   w[0:96, cv:cv + NV], start=True, stop=True)
                mm.then_inc(sig["linear"], 1)

            def sums(t, p, k):
                j = SUB - 1 - k
                reach(pe, sig["out_ready"], SUB * t + k - 1)
                pe.matmul(ec.o_ps[k % 2][:, 0:D], ec.sel[p][:, j, :], msg[p][:, j, :], start=True, stop=False)
                ec.carry(pe, t, p, k).then_inc(sig["summed"], 1)

            def map_and_sum(t, p):
                maps, summing = present(t, T), present(t - 1, T)
                if maps:
                    reach(pe, sig["products"], t + 1)
                    turn(t, p, 0)
                reach(pe, sig["scaled"], t)
                reach(pe, sig["sel_made"], t)
                for k in range(SUB):
                    if maps and k + 1 < SUB:
                        turn(t, p, k + 1)
                    if summing:
                        sums(t - 1, 1 - p, k)
                    if maps:
                        linear(t, p, k)

            rolled(pe, T, [(map_and_sum, 1, 1), (radial, 0)])

        @block.scalar
        def _(act):
            def sigmoid(t, p):
                reach(act, sig["radial"], t + 1)
                reach(act, sig["scaled"], t - 1)
                act.activation(rad[p][:, :, :], rad_ps[:, :, 0:D], ACT.Sigmoid).then_inc(sig["sigmoid_done"], 1)

            def take(t, p, k):
                reach(act, sig["pT"], SUB * t + k + 1)
                reach(act, sig["linear"], SUB * t + k - 1)
                act.activation(pT[k % 2][:, :], pT_ps[k % 2][0:96, :], ACT.Copy).then_inc(sig["pT_taken"], 1)

            def take_both(t, p):
                for k in range(-1, SUB):
                    if present(t, T) and k + 1 < SUB:
                        take(t, p, k + 1)
                    if present(t - 1, T) and k >= 0:
                        ec.take_out(act, t - 1, 1 - p, k)

            act.wait_ge(sig["out_zeroed"], 2)
            rolled(act, T, [(take_both, 1, 1), (sigmoid, 0)])

        @block.vector
        def _(dve):
            w_scale(dve)

            def products(t, p):
                e4 = pr.edge4[:, bass.ds(t * (SUB * 6), SUB * 6)].rearrange("p (j k) -> p j k", j=SUB)
                rows = ec.rows_in[0][p]
                v = rows[:, :, NS:D].rearrange("p j (i c) -> p j i c", i=3)
                ec.gathered(dve, t, p)
                reach(dve, sig["pT"], SUB * t - SUB)
                reach(dve, sig["products"], t)
                dve.tensor_tensor(ve[:, :, :, :], v, e4[:, :, 1:4].unsqueeze(3).to_broadcast([P, SUB, 3, NV]),
                                  ALU.mult).then_inc(sig["ve"], 1)
                dve.tensor_tensor(prod[p][:, :, :, 0:NS], rows[:, :, 0:NS].unsqueeze(2).to_broadcast([P, SUB, 4, NS]),
                                  e4[:, :, 0:4].unsqueeze(3).to_broadcast([P, SUB, 4, NS]), ALU.mult).then_inc(sig["prod_s"], 1)
                dve.wait_ge(sig["ve"], t + 1)
                dve.tensor_tensor(dot[:, :, :], ve[:, :, 0, :], ve[:, :, 1, :], ALU.add).then_inc(sig["dot"], 1)
                dve.tensor_tensor(prod[p][:, :, 1:4, NS:96], v, e4[:, :, 0:1].unsqueeze(3).to_broadcast([P, SUB, 3, NV]),
                                  ALU.mult).then_inc(sig["prod_v"], 1)
                dve.wait_ge(sig["dot"], t + 1)
                dve.tensor_tensor(prod[p][:, :, 0, NS:96], dot[:, :, :], ve[:, :, 2, :], ALU.add).then_inc(sig["products"], 1)

            def scale(t, p):
                ec.make_sel(dve, t, p)
                reach(dve, sig["sigmoid_done"], t + 1)
                reach(dve, sig["linear"], SUB * t + SUB)
                dve.tensor_tensor(msg[p][:, :, :], m_ps[:, :, 0:D], rad[p][:, :, :], ALU.mult).then_inc(sig["scaled"], 1)

            rolled(dve, T, [(products, 0), (scale, 1)])

    finish_pass(nc, sig)


class Norm:

    def __init__(self, pr, ctx, sig, name, parts):
        nc = pr.nc
        self.sig, self.name, self.parts = sig, name, parts
        sb = lambda n, shape: ctx.enter_context(nc.sbuf_tensor(f"{pr.name}_{name}_{n}", shape, F32))
        n = len(parts)
        self.stats = sb("stats", [P, n, SUB, 6])
        self.mean = [sb(f"mean{p}", [P, n, SUB, 2]) for p in range(2)]
        self.var = [sb(f"var{p}", [P, n, SUB]) for p in range(2)]
        self.rstd = [sb(f"rstd{p}", [P, n, SUB]) for p in range(2)]
        self.half = sb("half", [P, n, SUB])

    def start(self, pool):
        pool.memset(self.half[:, :, :], -0.5).then_inc(self.sig[f"{self.name}_half"], 1)
        pool.wait_ge(self.sig[f"{self.name}_half"], 1)

    def statistics(self, dve, t, p, z, root_mean_square=False):
        sig, n = self.sig, self.name
        for k, (c, width) in enumerate(self.parts):
            for j in range(SUB):
                ins = dve.bn_stats(self.stats[:, k, j, :], z[:, j, c:c + width])
        ins.then_inc(sig[f"{n}_stats"], 1)
        reach_gate(dve, sig[f"{n}_stats"], t + 1, sig["dve_gate"])
        for k in range(len(self.parts)):
            for j in range(SUB):
                ins = dve.bn_aggr(self.mean[p][:, k, j, :], self.stats[:, k, j, :])
        ins.then_inc(sig[f"{n}_mean"], 1)
        dve.wait_ge(sig[f"{n}_mean"], t + 1)
        if root_mean_square:
            m = self.mean[p]
            dve.tensor_tensor(self.var[p][:, 1, :], m[:, 1, :, 0], m[:, 1, :, 0], ALU.mult).then_inc(sig[f"{n}_ms"], 1)
            dve.wait_ge(sig[f"{n}_ms"], 2 * t + 1)
            dve.tensor_tensor(self.var[p][:, 1, :], self.var[p][:, 1, :], m[:, 1, :, 1], ALU.add).then_inc(sig[f"{n}_ms"], 1)
            dve.wait_ge(sig[f"{n}_ms"], 2 * t + 2)
            dve.tensor_scalar(self.var[p][:, 1, :], self.var[p][:, 1, :], 3.0, EPS, ALU.mult, ALU.add)
            dve.tensor_scalar(self.var[p][:, 0, :], m[:, 0, :, 1], EPS, None, ALU.add).then_inc(sig[f"{n}_var"], 1)
        else:
            dve.tensor_scalar(self.var[p][:, :, :], self.mean[p][:, :, :, 1], EPS, None, ALU.add).then_inc(
                sig[f"{n}_var"], 1)

    def power(self, pool, t, p):
        sig, n = self.sig, self.name
        reach_gate(pool, sig[f"{n}_var"], t + 1, sig["pool_gate"])
        reach_gate(pool, sig[f"{n}_applied"], t - 1, sig["pool_gate"])
        pool.tensor_tensor(self.rstd[p][:, :, :], self.var[p][:, :, :], self.half[:, :, :], ALU.pow).then_inc(
            sig[f"{n}_rstd"], 1)

    def apply(self, dve, t, p, out, z, root_mean_square=False):
        sig, n = self.sig, self.name
        reach(dve, sig[f"{n}_rstd"], t + 1)
        for k, (c, width) in enumerate(self.parts):
            for j in range(SUB):
                to, of, r = out[:, j, c:c + width], z[:, j, c:c + width], self.rstd[p][:, k, j:j + 1]
                if root_mean_square and k == 1:
                    ins = dve.tensor_scalar(to, of, r, None, ALU.mult)
                else:
                    ins = dve.tensor_scalar(to, of, self.mean[p][:, k, j, 0:1], r, ALU.subtract, ALU.mult)
        return ins.then_inc(sig[f"{n}_applied"], 1)


class Turn:

    def __init__(self, pr, ctx, sig, name, bank=None):
        nc = pr.nc
        self.pr, self.sig, self.name = pr, sig, name
        self.ps = bank if bank is not None else ctx.enter_context(nc.psum_tensor(f"{pr.name}_{name}_ps", [P, SUB, 2 * P], F32))
        self.s = ctx.enter_context(nc.sbuf_tensor(f"{pr.name}_{name}_s", [NS, SUB, P], F32))
        self.v = ctx.enter_context(nc.sbuf_tensor(f"{pr.name}_{name}_v", [3 * NV, SUB, P], F32))

    def turn(self, pe, t, rows):
        for j in range(SUB):
            pe.transpose(self.ps[0:NS, j, 0:P], rows[:, j, 0:NS], self.pr.ident[:, :])
            mm = pe.transpose(self.ps[0:3 * NV, j, P:2 * P], rows[:, j, NS:D], self.pr.ident[:, :])
        mm.then_inc(self.sig[f"{self.name}_turned"], 1)

    def take(self, act, t, used):
        reach(act, self.sig[f"{self.name}_turned"], t + 1)
        reach(act, self.sig[used], t)
        act.activation(self.s[:, :, :], self.ps[0:NS, :, 0:P], ACT.Copy)
        act.activation(self.v[:, :, :], self.ps[0:3 * NV, :, P:2 * P], ACT.Copy).then_inc(
            self.sig[f"{self.name}_taken"], 1)

    def product(self, pe, t, out, w, col, maps, done, tiles=range(SUB)):
        reach(pe, self.sig[f"{self.name}_taken"], t + 1)
        weights = w[:, col:col + maps * D].rearrange("p (k c) -> p k c", k=maps)
        for j in tiles:
            rows = out[:, j - tiles[0], 0:maps * D].rearrange("p (k c) -> p k c", k=maps)
            pe.matmul(rows[:, :, 0:NS], self.s[:, j, :], weights[0:NS, :, 0:NS], start=True, stop=True)
            mm = pe.matmul(rows[:, :, NS:D], self.v[:, j, :], weights[0:3 * NV, :, NS:D], start=True, stop=True)
        mm.then_inc(self.sig[done], 1)


def nodes_layer0(pr):
    nc, T, pr.name = pr.nc, pr.T, "n0"
    with ExitStack() as ctx:
        sig = Signals(nc, ctx)
        two = lambda n, shape: [ctx.enter_context(nc.sbuf_tensor(f"n0_{n}{p}", shape, F32)) for p in range(2)]
        xs, xv, x, agg = two("xs", [NS, STEP]), two("xv", [3 * NV, STEP]), two("x", [P, SUB, D]), two("agg", [P, SUB, AGG_W])
        pre, gate, z, x1 = two("pre", [P, SUB, 192]), two("gate", [P, SUB, 96]), two("z", [P, SUB, D]), two("x1", [P, SUB, D])
        acc = [ctx.enter_context(nc.psum_tensor(f"n0_acc{p}", [P, SUB, 256], F32)) for p in range(2)]
        norm = Norm(pr, ctx, sig, "norm", [(0, D)])
        w, w_zero, w_load, w_scale, w_n = weight_tile(pr, ctx, sig, "n0_w", 192, [
            (0, 0, pr.d["L0_gnn_sc_ws"], NS ** -0.5)] + block_diagonal(96, pr.d["L0_gnn_sc_wv"], NV ** -0.5))
        block = ctx.enter_context(nc.Block())

        @block.sync
        def _(sp):
            w_load(sp)

            def load(t, p):
                reach(sp, sig["self_product"], t - 1)
                reach(sp, sig["norm_stats"], t - 1)
                reach(sp, sig["summed_up"], t - 1)
                for to, of in ((xs[p][:, :], pr.d["xT"][0:NS, bass.ds(t * STEP, STEP)]),
                               (xv[p][:, :], pr.d["xT"][NS:D, bass.ds(t * STEP, STEP)]),
                               (x[p][:, :, :].rearrange("p j c -> p (j c)"), pr.rows(pr.d["x"], t)),
                               (agg[p][:, :, :].rearrange("p j c -> p (j c)"), pr.rows(pr.agg, t))):
                    sp.dma_start(to, of).then_inc(sig[f"loaded{p}"], 16)

            rolled(sp, T, [(load, 0)])

        @block.gpsimd
        def _(pool):
            w_zero(pool)
            norm.start(pool)
            rolled(pool, T, [(lambda t, p: norm.power(pool, t, p), 0)])

        @block.tensor
        def _(pe):
            pe.wait_ge(sig["weights_ready"], w_n)

            def product(t, p):
                reach(pe, sig[f"loaded{p}"], dma_count(t, p, 64))
                reach_gate(pe, sig["summed_up"], t - 1, sig["pe_gate"])
                for j in range(SUB):
                    cols = slice(j * P, (j + 1) * P)
                    pe.matmul(acc[p][:, j, 0:96], xs[p][:, cols], w[0:NS, 0:96], start=True, stop=True)
                    mm = pe.matmul(acc[p][:, j, 96:192], xv[p][:, cols], w[0:3 * NV, 96:192], start=True, stop=True)
                mm.then_inc(sig["self_product"], 1)

            rolled(pe, T, [(product, 0)])

        @block.scalar
        def _(act):
            def gates(t, p):
                reach(act, sig["pre"], t + 1)
                reach(act, sig["z"], t - 1)
                act.activation(gate[p][:, :, :], pre[p][:, :, 0:96], ACT.Sigmoid).then_inc(sig["gates"], 1)

            def store(t, p):
                reach(act, sig["norm_applied"], t + 1)
                act.dma_start(pr.rows(pr.table_x, t), x1[p][:, :, :].rearrange("p j c -> p (j c)")).then_inc(
                    sig[f"stored{p}"], 16)

            rolled(act, T, [(gates, 0), (store, 2)])
            for p in range(2):
                act.wait_ge(sig[f"stored{p}"], 16 * (T // 2))

        @block.vector
        def _(dve):
            w_scale(dve)

            def add_up(t, p):
                reach(dve, sig[f"loaded{p}"], dma_count(t, p, 64))
                reach(dve, sig["self_product"], t + 1)
                dve.tensor_tensor(pre[p][:, :, :], acc[p][:, :, 0:192], agg[p][:, :, :], ALU.add).then_inc(sig["summed_up"], 1)
                reach(dve, sig["summed_up"], t + 1)
                dve.tensor_tensor(pre[p][:, :, :], pre[p][:, :, :],
                                  pr.attr[:, bass.ds(t * SUB, SUB)].unsqueeze(2).to_broadcast([P, SUB, 192]),
                                  ALU.mult).then_inc(sig["pre"], 1)

            def gated(t, p):
                reach(dve, sig["norm_applied"], t - 1)
                reach(dve, sig["gates"], t + 1)
                dve.tensor_tensor(pre[p][:, :, 0:NS], pre[p][:, :, 0:NS], gate[p][:, :, 0:NS], ALU.mult).then_inc(sig["gated"], 1)
                vec = pre[p][:, :, 96:192].rearrange("p j (i c) -> p j i c", i=3)
                dve.tensor_tensor(vec, vec, gate[p][:, :, NS:96].unsqueeze(2).to_broadcast([P, SUB, 3, NV]),
                                  ALU.mult).then_inc(sig["gated"], 1)
                reach(dve, sig["gated"], 2 * t + 2)
                dve.tensor_tensor(z[p][:, :, 0:NS], pre[p][:, :, 0:NS], x[p][:, :, 0:NS], ALU.add)
                dve.tensor_tensor(z[p][:, :, NS:D], pre[p][:, :, 96:192], x[p][:, :, NS:D], ALU.add).then_inc(sig["z"], 1)
                reach(dve, sig["z"], t + 1)
                norm.statistics(dve, t, p, z[p])

            def normalise(t, p):
                reach(dve, sig[f"stored{p}"], dma_count(t - 2, p, 16))
                norm.apply(dve, t, p, x1[p], z[p])

            rolled(dve, T, [(normalise, 2), (gated, 1), (add_up, 0)])

    finish_pass(nc, sig)


def nodes_layer1(pr):
    nc, T, pr.name = pr.nc, pr.T, "n1"
    with ExitStack() as ctx:
        sig = Signals(nc, ctx)
        two = lambda n, shape: [ctx.enter_context(nc.sbuf_tensor(f"n1_{n}{p}", shape, F32)) for p in range(2)]
        x, agg, h, z, x2 = (two(n, [P, SUB, D]) for n in ("x", "agg", "h", "z", "x2"))
        f = two("f", [P, SUB, 2 * D])
        y_ps = ctx.enter_context(nc.psum_tensor("n1_y", [P, SUB, 256], F32))
        f_ps = ctx.enter_context(nc.psum_tensor("n1_f", [P, 2, 512], F32))
        h_turn = Turn(pr, ctx, sig, "h_turn")
        x_turn = Turn(pr, ctx, sig, "x_turn")
        norm = Norm(pr, ctx, sig, "norm", [(0, D)])
        d, ks, kv = pr.d, NS ** -0.5, NV ** -0.5
        w, w_zero, w_load, w_scale, w_n = weight_tile(
            pr, ctx, sig, "n1_w", 3 * D, [(0, 0, d["L1_gnn_L_s"], ks), (0, D, d["L2_gnn_Wl1_0"], ks), (0, 2 * D, d["L2_gnn_Wsc0"], ks)]
            + block_diagonal(NS, d["L1_gnn_L_v"], kv) + block_diagonal(D + NS, d["L2_gnn_Wl1_1"], kv)
            + block_diagonal(2 * D + NS, d["L2_gnn_Wsc1"], kv))
        block = ctx.enter_context(nc.Block())

        @block.sync
        def _(sp):
            w_load(sp)

            def load(t, p):
                reach(sp, sig["z"], t - 1)
                sp.dma_start(x[p][:, :, :].rearrange("p j c -> p (j c)"), pr.rows(pr.table_x, t)).then_inc(sig[f"loaded{p}"], 16)
                sp.dma_start(agg[p][:, :, :], pr.agg.rearrange("(t p j) c -> t p j c", p=P, j=SUB)[bass.ds(t, 1), :, :, 0:D]
                             .rearrange("a p j c -> (a p) j c")).then_inc(sig[f"loaded{p}"], 16)

            rolled(sp, T, [(load, 0)])

        @block.gpsimd
        def _(pool):
            w_zero(pool)
            norm.start(pool)
            rolled(pool, T, [(lambda t, p: norm.power(pool, t, p), 0)])

        @block.tensor
        def _(pe):
            pe.wait_ge(sig["weights_ready"], w_n)

            def turn_h(t, p):
                reach(pe, sig["h"], t + 1)
                reach_gate(pe, sig["h_turn_taken"], t, sig["pe_gate"])
                h_turn.turn(pe, t, h[p])

            def product_y(t, p):
                reach(pe, sig["z"], t)
                h_turn.product(pe, t, y_ps, w, 0, 1, "y")

            def turn_x(t, p):
                reach(pe, sig["norm_applied"], t + 1)
                reach_gate(pe, sig["x_turn_taken"], t, sig["pe_gate"])
                x_turn.turn(pe, t, x2[p])

            def product_f0(t, p):
                reach(pe, sig["f1_read"], t)
                x_turn.product(pe, t, f_ps, w, D, 2, "f0_product", range(2))

            def product_f1(t, p):
                reach(pe, sig["f0_read"], t + 1)
                x_turn.product(pe, t, f_ps, w, D, 2, "f1_product", range(2, SUB))

            rolled(pe, T, [(turn_h, 1), (product_f1, 3), (product_y, 1), (turn_x, 2), (product_f0, 2)])

        @block.scalar
        def _(act):
            def store(t, p):
                reach(act, sig["tables"], t + 1)
                for k, table in enumerate((pr.table_a, pr.table_b)):
                    act.dma_start(pr.rows(table, t).rearrange("p (j c) -> p j c", j=SUB), f[p][:, :, k * D:(k + 1) * D]).then_inc(
                        sig[f"stored{p}"], 16)

            rolled(act, T, [(lambda t, p: h_turn.take(act, t, "y"), 1), (store, 4),
                            (lambda t, p: x_turn.take(act, t, "f1_product"), 2)])
            for p in range(2):
                act.wait_ge(sig[f"stored{p}"], 32 * (T // 2))

        @block.vector
        def _(dve):
            w_scale(dve)

            def add(t, p):
                reach(dve, sig[f"loaded{p}"], dma_count(t, p, 32))
                reach(dve, sig["h_turn_turned"], t - 1)
                dve.tensor_tensor(h[p][:, :, :], x[p][:, :, :], agg[p][:, :, :], ALU.add).then_inc(sig["h"], 1)

            def residual(t, p):
                reach(dve, sig["norm_applied"], t - 1)
                reach(dve, sig["y"], t + 1)
                dve.tensor_tensor(z[p][:, :, :], y_ps[:, :, 0:D], x[p][:, :, :], ALU.add).then_inc(sig["z"], 1)
                reach(dve, sig["z"], t + 1)
                norm.statistics(dve, t, p, z[p])

            def normalise(t, p):
                reach(dve, sig["x_turn_turned"], t - 1)
                norm.apply(dve, t, p, x2[p], z[p])

            def take_half(t, p, half):
                reach(dve, sig[f"f{half}_product"], t + 1)
                js = slice(2 * half, 2 * half + 2)
                dve.tensor_tensor(f[p][:, js, :], f_ps[:, :, 0:2 * D],
                                  pr.attr[:, bass.ds(t * SUB + 2 * half, 2)].unsqueeze(2).to_broadcast([P, 2, 2 * D]),
                                  ALU.mult).then_inc(sig[f"f{half}_read"], 1)

            def take_f0(t, p):
                reach(dve, sig[f"stored{p}"], dma_count(t - 2, p, 32))
                take_half(t, p, 0)

            def take_f1(t, p):
                take_half(t, p, 1)
                reach(dve, sig["f1_read"], t + 1)
                dve.tensor_tensor(f[p][:, :, D:2 * D], f[p][:, :, D:2 * D], x2[p][:, :, :], ALU.add).then_inc(sig["tables"], 1)

            rolled(dve, T, [(normalise, 2), (take_f0, 3), (add, 0), (take_f1, 3), (residual, 1)])

    finish_pass(nc, sig)


def nodes_layer2(pr):
    nc, T, d, pr.name = pr.nc, pr.T, pr.d, "n2"
    with ExitStack() as ctx:
        sig = Signals(nc, ctx)
        two = lambda n, shape: [ctx.enter_context(nc.sbuf_tensor(f"n2_{n}{p}", shape, F32)) for p in range(2)]
        base, z, x3, hat = (two(n, [P, SUB, D]) for n in ("base", "z", "x3", "hat"))
        agg = two("agg", [P, SUB, AGG_W])
        fa, fb = two("fa", [P, SUB, D]), two("fb", [P, SUB, D])
        share = ctx.enter_context(nc.sbuf_tensor("n2_share", [P, 3, SUB], F32))
        gamma = ctx.enter_context(nc.sbuf_tensor("n2_gamma", [P, D], F32))
        beta = ctx.enter_context(nc.sbuf_tensor("n2_beta", [P, NS], F32))
        f_ps = ctx.enter_context(nc.psum_tensor("n2_f", [P, SUB, 512], F32))
        turn = Turn(pr, ctx, sig, "turn")
        norm = Norm(pr, ctx, sig, "norm", [(0, D)])
        equi = Norm(pr, ctx, sig, "equi", [(0, NS), (NS, 3 * NV)])
        w, w_zero, w_load, w_scale, w_n = weight_tile(
            pr, ctx, sig, "n2_w", 2 * D, [(0, 0, d["L3_gnn_Ws_src"], 1.0), (0, D, d["L3_gnn_Ws_dst"], 1.0)]
            + block_diagonal(NS, d["L3_gnn_Wv_src"], 1.0) + block_diagonal(D + NS, d["L3_gnn_Wv_dst"], 1.0))
        block = ctx.enter_context(nc.Block())

        @block.sync
        def _(sp):
            w_load(sp)
            sp.dma_start(gamma[:, 0:NS], d["L3_gnn_gamma_s"].to_broadcast([P, NS])).then_inc(sig["affine_loaded"], 16)
            sp.dma_start(beta[:, :], d["L3_gnn_beta_s"].to_broadcast([P, NS])).then_inc(sig["affine_loaded"], 16)
            for i in range(3):
                sp.dma_start(gamma[:, NS + NV * i:NS + NV * (i + 1)], d["L3_gnn_gamma_v"].to_broadcast([P, NV])).then_inc(
                    sig["affine_loaded"], 16)

            def load(t, p):
                reach(sp, sig["z"], t - 1)
                sp.dma_start(base[p][:, :, :].rearrange("p j c -> p (j c)"), pr.rows(pr.table_b, t)).then_inc(sig[f"loaded{p}"], 16)
                sp.dma_start(agg[p][:, :, :].rearrange("p j c -> p (j c)"), pr.rows(pr.agg, t)).then_inc(sig[f"loaded{p}"], 16)

            rolled(sp, T, [(load, 0)])

        @block.gpsimd
        def _(pool):
            w_zero(pool)
            norm.start(pool)
            equi.start(pool)
            rolled(pool, T, [(lambda t, p: equi.power(pool, t, p), 1), (lambda t, p: norm.power(pool, t, p), 0)])

        @block.tensor
        def _(pe):
            pe.wait_ge(sig["weights_ready"], w_n)

            def product(t, p):
                reach(pe, sig["hat"], t + 1)
                reach_gate(pe, sig["turn_taken"], t, sig["pe_gate"])
                turn.turn(pe, t, hat[p])
                reach(pe, sig["f_taken"], t)
                turn.product(pe, t, f_ps, w, 0, 2, "f")

            rolled(pe, T, [(product, 2)])

        @block.scalar
        def _(act):
            def take(t, p):
                turn.take(act, t, "f")
                reach(act, sig["f"], t + 1)
                reach(act, sig[f"stored{p}"], dma_count(t - 2, p, 32))
                act.activation(fa[p][:, :, :], f_ps[:, :, 0:D], ACT.Copy)
                act.activation(fb[p][:, :, :], f_ps[:, :, D:2 * D], ACT.Copy).then_inc(sig["f_taken"], 1)

            def store(t, p):
                reach(act, sig["f_taken"], t + 1)
                for table, rows in ((pr.table_a, fa[p]), (pr.table_c, fb[p])):
                    act.dma_start(pr.rows(table, t), rows[:, :, :].rearrange("p j c -> p (j c)")).then_inc(sig[f"stored{p}"], 16)

            def store_x3(t, p):
                reach(act, sig["norm_applied"], t + 1)
                act.dma_start(pr.rows(pr.table_x, t), x3[p][:, :, :].rearrange("p j c -> p (j c)")).then_inc(
                    sig[f"x3_stored{p}"], 16)

            rolled(act, T, [(take, 2), (store_x3, 1), (store, 2)])
            for p in range(2):
                act.wait_ge(sig[f"stored{p}"], 32 * (T // 2))
                act.wait_ge(sig[f"x3_stored{p}"], 16 * (T // 2))

        @block.vector
        def _(dve):
            w_scale(dve)
            dve.wait_ge(sig["affine_loaded"], 16 * 5)

            def residual(t, p):
                s = agg[p]
                reach(dve, sig[f"loaded{p}"], dma_count(t, p, 32))
                dve.tensor_scalar(share[:, 0, :], s[:, :, 1], 1.0, None, ALU.max).then_inc(sig["count"], 1)
                reach(dve, sig["count"], t + 1)
                dve.reciprocal(share[:, 1, :], share[:, 0, :]).then_inc(sig["inverse"], 1)
                reach(dve, sig["inverse"], t + 1)
                dve.tensor_tensor(share[:, 0, :], share[:, 1, :], pr.attr[:, bass.ds(t * SUB, SUB)], ALU.mult).then_inc(sig["share"], 1)
                reach(dve, sig["share"], 3 * t + 1)
                dve.tensor_tensor(share[:, 1, :], share[:, 0, :], share[:, 0, :], ALU.mult).then_inc(sig["share"], 1)
                reach(dve, sig["share"], 3 * t + 2)
                dve.tensor_tensor(share[:, 2, :], share[:, 1, :], s[:, :, 0], ALU.mult).then_inc(sig["share"], 1)
                reach(dve, sig["share"], 3 * t + 3)
                for j in range(SUB):
                    ins = dve.scalar_tensor_tensor(out=z[p][:, j, :], in0=s[:, j, 2:2 + D], scalar=share[:, 2, j:j + 1],
                                                   in1=base[p][:, j, :], op0=ALU.mult, op1=ALU.add)
                ins.then_inc(sig["z"], 1)
                reach(dve, sig["z"], t + 1)
                norm.statistics(dve, t, p, z[p])

            def normalise(t, p):
                reach(dve, sig[f"x3_stored{p}"], dma_count(t - 2, p, 16))
                norm.apply(dve, t, p, x3[p], z[p])
                reach(dve, sig["norm_applied"], t + 1)
                equi.statistics(dve, t, p, x3[p], True)

            def second_norm(t, p):
                reach(dve, sig["turn_turned"], t - 1)
                equi.apply(dve, t, p, hat[p], x3[p], True)
                reach(dve, sig["equi_applied"], t + 1)
                dve.tensor_tensor(hat[p][:, :, :], hat[p][:, :, :], gamma[:, :].unsqueeze(1).to_broadcast([P, SUB, D]),
                                  ALU.mult).then_inc(sig["gamma"], 1)
                reach(dve, sig["gamma"], t + 1)
                dve.tensor_tensor(hat[p][:, :, 0:NS], hat[p][:, :, 0:NS], beta[:, :].unsqueeze(1).to_broadcast([P, SUB, NS]),
                                  ALU.add).then_inc(sig["hat"], 1)

            rolled(dve, T, [(second_norm, 2), (normalise, 1), (residual, 0)])

    finish_pass(nc, sig)


def nodes_layer3(pr):
    nc, T, d, pr.name = pr.nc, pr.T, pr.d, "n3"
    with ExitStack() as ctx:
        sig = Signals(nc, ctx)
        two = lambda n, shape: [ctx.enter_context(nc.sbuf_tensor(f"n3_{n}{p}", shape, F32)) for p in range(2)]
        x, att, z, o = (two(n, [P, SUB, D]) for n in ("x", "att", "z", "o"))
        agg = two("agg", [P, SUB, AGG_W])
        den = ctx.enter_context(nc.sbuf_tensor("n3_den", [P, 2, SUB, HEADS], F32))
        y_ps = ctx.enter_context(nc.psum_tensor("n3_y", [P, SUB, 256], F32))
        turn = Turn(pr, ctx, sig, "turn")
        norm = Norm(pr, ctx, sig, "norm", [(0, D)])
        w, w_zero, w_load, w_scale, w_n = weight_tile(pr, ctx, sig, "n3_w", D, [(0, 0, d["L3_gnn_Wps"], 1.0)]
                                                      + block_diagonal(NS, d["L3_gnn_Wpv"], 1.0))
        block = ctx.enter_context(nc.Block())

        @block.sync
        def _(sp):
            w_load(sp)

            def load(t, p):
                reach(sp, sig["z"], t - 1)
                sp.dma_start(x[p][:, :, :].rearrange("p j c -> p (j c)"), pr.rows(pr.table_x, t)).then_inc(sig[f"loaded{p}"], 16)
                sp.dma_start(agg[p][:, :, :].rearrange("p j c -> p (j c)"), pr.rows(pr.agg, t)).then_inc(sig[f"loaded{p}"], 16)

            rolled(sp, T, [(load, 0)])

        @block.gpsimd
        def _(pool):
            w_zero(pool)
            norm.start(pool)
            rolled(pool, T, [(lambda t, p: norm.power(pool, t, p), 0)])

        @block.tensor
        def _(pe):
            pe.wait_ge(sig["weights_ready"], w_n)

            def product(t, p):
                reach(pe, sig["attended"], t + 1)
                reach_gate(pe, sig["turn_taken"], t, sig["pe_gate"])
                turn.turn(pe, t, att[p])
                reach(pe, sig["z"], t)
                turn.product(pe, t, y_ps, w, 0, 1, "y")

            rolled(pe, T, [(product, 0)])

        @block.scalar
        def _(act):
            def store(t, p):
                reach(act, sig["norm_applied"], t + 1)
                act.dma_start(pr.rows(pr.output, t), o[p][:, :, :].rearrange("p j c -> p (j c)")).then_inc(sig[f"stored{p}"], 16)

            rolled(act, T, [(lambda t, p: turn.take(act, t, "y"), 0), (store, 2)])
            for p in range(2):
                act.wait_ge(sig[f"stored{p}"], 16 * (T // 2))

        @block.vector
        def _(dve):
            w_scale(dve)

            def attend(t, p):
                reach(dve, sig[f"loaded{p}"], dma_count(t, p, 32))
                reach(dve, sig["turn_turned"], t - 1)
                dve.tensor_scalar(den[:, 0, :, :], agg[p][:, :, D:D + HEADS], 1e-16, None, ALU.add).then_inc(sig["den"], 1)
                reach(dve, sig["den"], t + 1)
                dve.reciprocal(den[:, 1, :, :], den[:, 0, :, :]).then_inc(sig["den_inverse"], 1)
                reach(dve, sig["den_inverse"], t + 1)
                share = den[:, 1, :, :].unsqueeze(3)
                for c, per_head in [(0, 16)] + [(NS + NV * i, 8) for i in range(3)]:
                    cols = slice(c, c + HEADS * per_head)
                    ins = dve.tensor_tensor(att[p][:, :, cols].rearrange("p j (h k) -> p j h k", h=HEADS),
                                            agg[p][:, :, cols].rearrange("p j (h k) -> p j h k", h=HEADS),
                                            share.to_broadcast([P, SUB, HEADS, per_head]), ALU.mult)
                ins.then_inc(sig["attended"], 1)

            def residual(t, p):
                reach(dve, sig["norm_applied"], t - 1)
                reach(dve, sig["y"], t + 1)
                dve.scalar_tensor_tensor(out=z[p][:, :, :], in0=x[p][:, :, :], scalar=2.0, in1=y_ps[:, :, 0:D],
                                         op0=ALU.mult, op1=ALU.add).then_inc(sig["z"], 1)
                reach(dve, sig["z"], t + 1)
                norm.statistics(dve, t, p, z[p])

            def normalise(t, p):
                reach(dve, sig[f"stored{p}"], dma_count(t - 2, p, 16))
                norm.apply(dve, t, p, o[p], z[p])

            rolled(dve, T, [(attend, 0), (residual, 1), (normalise, 2)])

    finish_pass(nc, sig)


def tiles_before_first(t):
    if isinstance(t, int):
        return -SUB if t < 0 else SUB * (t + max(t - 1, 0))
    return 2 * SUB * t - SUB


def tiles_before_second(t, T):
    if isinstance(t, int):
        return -SUB if t < 0 else SUB * (min(t + 2, T) + t)
    return 2 * SUB * t + 2 * SUB


def edges_layer3(pr):
    nc, T, d, pr.name = pr.nc, pr.T, pr.d, "l3"
    r3, r2 = 3.0 ** -0.5, 2.0 ** -0.5
    with ExitStack() as ctx:
        sig = Signals(nc, ctx)
        sb = lambda n, shape, dt=F32: ctx.enter_context(nc.sbuf_tensor(f"l3_{n}", shape, dt))
        ps = lambda n, shape: ctx.enter_context(nc.psum_tensor(f"l3_{n}", shape, F32))
        two = lambda n, shape: [sb(f"{n}{p}", shape) for p in range(2)]
        width = D + HEADS
        ec = EdgeCommon(pr, ctx, sig, [(pr.table_a, 0), (pr.table_c, 2)], width, "rows", banks=1)
        tp1 = TensorProduct(pr, ctx, sig, True, "tp1", split=True)
        tp2 = TensorProduct(pr, ctx, sig, True, "tp2", split=True)
        feat = two("feat", [16, STEP])
        rows = sb("rows", [P, SUB, D + 2 * NV])
        rows2 = sb("rows2", [P, SUB, D + 2 * NV])
        turned = [sb(f"turned{k}", [P, 3 * P]) for k in range(2)]
        leak, relu, logits = two("leak", [P, SUB, NS]), two("relu", [P, SUB, NS]), two("logits", [P, SUB, HEADS])
        leaky = sb("leaky", [P, SUB, NS])
        values, half_tanh, gates = two("values", [P, SUB, P]), two("half_tanh", [P, SUB, 96]), sb("gates", [P, SUB, NV])
        mask, running, top = sb("mask", [HEADS, STEP + 1]), sb("running", [HEADS, STEP]), two("top", [HEADS, STEP])
        fall = two("fall", [HEADS, 1])
        below, ex, shrink = sb("below", [P, SUB, HEADS]), two("ex", [P, SUB, HEADS]), two("shrink", [1, HEADS])
        weighted, handed = two("weighted", [P, SUB, width]), two("handed", [1, width])
        e_s, e_h = sb("e_s", [P, SUB, 3, NV]), sb("e_h", [P, SUB, 3, NV])
        dots = sb("dots", [P, NS])
        scale_col = sb("scale_col", [P, 3])
        sval_t = sb("sval_t", [NS, 96])
        wh_ps = ps("wh_ps", [P, SUB, 256])
        a_ps = ps("a_ps", [P, SUB, 256])
        turn_ps = [ps(f"turn_ps{k}", [P, 4 * P]) for k in range(2)]
        tail_ps = ec.o_ps[0][:, 192:192 + SUB * 2 * NV].rearrange("p (j c) -> p j c", j=SUB)
        small_ps = ps("small_ps", [P, STEP])
        c_rbf, c_a, c_v, c_hs, c_hv, c_g = 0, 224, 384, 512, 576, 704

        def grouped(c, m):
            parts = [(r, c + (r // NS) * NV, m[NS:96, :], 1.0) for r in (0, NS)] + [(0, c + NS, m[NS:96, :], 1.0)]
            parts += [(r + NV, c + (r // NS) * NV, m[96:P, :], r2) for r in (0, NS)] + [(NV, c + NS, m[96:P, :], r2)]
            return parts + [(NS, c + NS + NV, m[0:NS, :], 1.0)]

        w, w_zero, w_load, w_scale, w_n = weight_tile(pr, ctx, sig, "l3_w", 736, [
            (0, c_rbf, d["L3_gnn_W_rbf"], 1.0),
            (0, c_a, d["L3_gnn_W_alpha"][0:NS, :], 1.0), (NS, c_a, d["L3_gnn_W_alpha"][NS:96, :], r3),
            (0, c_a + 64, d["L3_gnn_Ws_val"][0:NS, :], 1.0), (NS, c_a + 64, d["L3_gnn_Ws_val"][NS:96, :], r3),
            (0, c_hs, d["L3_gnn_Ws_vlin"][0:NS, :], 1.0), (NS, c_hs, d["L3_gnn_Ws_vlin"][NS:96, :], r3),
            (0, c_g, d["L3_gnn_Wg"], 1.0)] + grouped(c_v, d["L3_gnn_Wv_val"]) + grouped(c_hv, d["L3_gnn_Wv_vlin"]))
        columns = [(0, 0, "w2_ss"), (NS, 0, "w2_vv0")] + [
            (r, c, n) for c in (1, 2) for r, n in ((0, "w2_vs"), (NV, "w2_vv1"))] + [
            (NS, 1, "w2_vs"), (NS + NV, 1, "w2_vv1"), (NS, 2, "w2_sv")]
        block = ctx.enter_context(nc.Block())

        @block.sync
        def _(sp):
            w_load(sp)
            for r, c, n in columns:
                v = d[f"L3_gnn_{n}"].rearrange("a c -> c a")
                sp.dma_start(scale_col[r:r + v.shape[0], c:c + 1], v).then_inc(sig["constants"], 16)
            sp.dma_start(dots[:, :], d["alpha_dot"].to_broadcast([P, NS])).then_inc(sig["constants"], 16)
            sp.dma_start(sval_t[:, :], d["Ws_val_T"]).then_inc(sig["constants"], 16)

            def load(t, p):
                reach(sp, sig["w"], t - 1)
                sp.dma_start(feat[p][:, :], d["edge_attr_16"][:, bass.ds(t * STEP, STEP)]).then_inc(sig[f"feat_loaded{p}"], 16)

            rolled(sp, T, [(load, 0), (lambda t, p: ec.load_dst(sp, t, p), 2)])

        @block.gpsimd
        def _(pool):
            w_zero(pool)
            ec.start_out(pool)
            for tp in (tp1, tp2):
                for p in range(2):
                    pool.memset(tp.msg[p][:, :, :, :], 0.0).then_inc(sig["msg_zeroed"], 1)
            pool.memset(top[1][:, :], -BIG).then_inc(sig["msg_zeroed"], 1)
            rolled(pool, T, [(lambda t, p: ec.gather(pool, t, p), 0), (lambda t, p: ec.scatter(pool, t, p), 6)])
            ec.all_scattered(pool)

        @block.tensor
        def _(pe):
            pe.wait_ge(sig["weights_ready"], w_n)
            pe.wait_ge(sig["constants"], 16 * (len(columns) + 2))
            pe.wait_ge(sig["out_zeroed"], 2)
            pe.matmul(wh_ps[0:96, 0, 0:NV], sval_t[:, :], w[0:NS, c_g:c_g + NV], start=True, stop=True).then_inc(sig["gate_map"], 1)
            pe.wait_ge(sig["maps_made"], 5)

            def weights(t, p):
                reach(pe, sig[f"feat_loaded{p}"], dma_count(t, p, 16))
                reach(pe, sig["messages"], t)
                reach(pe, sig["weighted"], t - 2)
                for j in range(SUB):
                    mm = pe.matmul(wh_ps[:, j, 0:224], feat[p][:, j * P:(j + 1) * P], w[0:16, c_rbf:c_rbf + 224],
                                   start=True, stop=True)
                mm.then_inc(sig["w"], 1)

            def turn(t, k, msg, taken):
                j = SUB - 1 - k
                reach(pe, sig["turn_taken"], taken - 1)
                for q in range(3):
                    mm = pe.transpose(turn_ps[k % 2][:, q * P:(q + 1) * P], msg[:, j, q, :], pr.ident[:, :])
                mm.then_inc(sig["turned"], 1)

            def logits_values(t, p):
                reach(pe, sig["messages"], t + 1)
                reach(pe, sig["values_taken"], t)
                reach(pe, sig["out_ready"], SUB * (t - 2))
                base = tiles_before_first(t)
                for k in range(SUB + 1):
                    if k < SUB:
                        turn(t, k, tp1.msg[p], base + k)
                    if k:
                        j, m = SUB - k, turned[(k - 1) % 2]
                        reach(pe, sig["turn_taken"], base + k)
                        pe.matmul(a_ps[:, j, 0:D], m[:, 0:P], w[:, c_a:c_a + D], start=True, stop=True)
                        pe.matmul(a_ps[:, j, D:D + NS], m[:, P:2 * P], w[:, c_v:c_v + NS], start=True, stop=True)
                        mm = pe.matmul(tail_ps[:, j, :], m[:, 2 * P:3 * P], w[:, c_v + NS:c_v + P], start=True, stop=True)
                        mm.then_inc(sig["mapped"], 1)

            def head_tile(t, k, base):
                j, m = SUB - 1 - k, turned[k % 2]
                reach(pe, sig["turn_taken"], base + k + 1)
                pe.matmul(wh_ps[:, j, 0:NS], m[:, 0:P], w[:, c_hs:c_hs + NS], start=True, stop=True)
                for q in range(2):
                    mm = pe.matmul(wh_ps[:, j, NS * (1 + q):NS * (2 + q)], m[:, (1 + q) * P:(2 + q) * P],
                                   w[:, c_hv + NS * q:c_hv + NS * (1 + q)], start=True, stop=True)
                mm.then_inc(sig["mapped"], 1)

            def sums(t, p, k):
                j = SUB - 1 - k
                reach(pe, sig["out_ready"], SUB * t + k)
                pe.matmul(ec.o_ps[k % 2][:, 0:width], ec.sel[p][:, j, :], weighted[p][:, j, :], start=True, stop=False)
                ec.carry(pe, t, p, k, handed[p][:, :]).then_inc(sig["summed"], 1)

            def heads_and_sums(t, p):
                heads, summing, base = present(t, T), present(t - 1, T), tiles_before_second(t, T)
                if heads:
                    reach(pe, sig["messages2"], t + 1)
                    reach(pe, sig["messages"], t + 3 if not isinstance(t, int) else min(t + 3, T))
                    turn(t, 0, tp2.msg[p], base)
                if summing:
                    reach(pe, sig["values_taken"], t + 2 if not isinstance(t, int) else min(t + 2, T))
                    reach(pe, sig["weighted"], t)
                    reach(pe, sig["handed"], t)
                    reach(pe, sig["sel_made"], t)
                for k in range(SUB):
                    if heads and k + 1 < SUB:
                        turn(t, k + 1, tp2.msg[p], base + k + 1)
                    if summing:
                        sums(t - 1, 1 - p, k)
                    if heads:
                        head_tile(t, k, base)

            def turn_logits(t, p):
                reach(pe, sig["logits"], t + 1)
                reach(pe, sig["below"], t)
                reach_gate(pe, sig["shrink"], t, sig["pe_gate"])
                for j in range(SUB):
                    mm = pe.transpose(small_ps[0:HEADS, j * P:(j + 1) * P], logits[p][:, j, :], pr.ident[:, :])
                mm.then_inc(sig["logits_turned"], 1)

            def turn_top(t, p):
                reach_gate(pe, sig["fall"], t + 1, sig["pe_gate"])
                for j in range(SUB):
                    pe.transpose(small_ps[:, HEADS * j:HEADS * (j + 1)], top[p][:, j * P:(j + 1) * P], pr.ident[0:HEADS, 0:HEADS])
                pe.transpose(small_ps[0:1, 32:36], fall[p][:, :], pr.ident[0:HEADS, 0:HEADS]).then_inc(sig["top_turned"], 1)

            rolled(pe, T, [(turn_top, 4), (heads_and_sums, 4, 1), (turn_logits, 3), (weights, 1), (logits_values, 2)])

        @block.scalar
        def _(act):
            def take(k, base):
                reach(act, sig["turned"], base + k + 1)
                reach(act, sig["mapped"], base + k - 1)
                act.activation(turned[k % 2][:, :], turn_ps[k % 2][:, 0:3 * P], ACT.Copy).then_inc(sig["turn_taken"], 1)

            def take_first(t, p):
                for k in range(SUB):
                    take(k, tiles_before_first(t))

            def take_second(t, p):
                for k in range(-1, SUB):
                    if present(t, T) and k + 1 < SUB:
                        take(k + 1, tiles_before_second(t, T))
                    if present(t - 1, T) and k >= 0:
                        ec.take_out(act, t - 1, 1 - p, k)

            def exponentials(t, p):
                reach(act, sig["below"], t + 1)
                reach(act, sig["weighted"], t - 1)
                act.activation(ex[p][:, :, :], below[:, :, :], ACT.Exp).then_inc(sig["ex"], 1)
                reach(act, sig["top_turned"], t + 1)
                reach(act, sig["handed"], t - 1)
                act.activation(shrink[p][:, :], small_ps[0:1, 32:36], ACT.Exp).then_inc(sig["shrink"], 1)

            def gate(t, p):
                reach(act, sig["mapped"], tiles_before_first(t) + SUB)
                reach(act, sig["values"], t - 1)
                act.activation(leak[p][:, :, :], a_ps[:, :, 0:NS], ACT.Copy, scale=0.2)
                act.activation(relu[p][:, :, :], a_ps[:, :, 0:NS], ACT.Relu, scale=0.8).then_inc(sig["relu"], 1)
                act.activation(half_tanh[p][:, :, :], a_ps[:, :, NS:D], ACT.Tanh, scale=0.5)
                act.activation(values[p][:, :, 0:NS], a_ps[:, :, D:D + NS], ACT.Copy)
                act.activation(values[p][:, :, NS:P], tail_ps[:, :, :], ACT.Copy).then_inc(sig["values_taken"], 1)

            act.wait_ge(sig["out_zeroed"], 2)
            rolled(act, T, [(exponentials, 4), (take_second, 4, 1), (take_first, 2), (gate, 2)])

        @block.vector
        def _(dve):
            w_scale(dve)
            dve.wait_ge(sig["constants"], 16 * (len(columns) + 2))
            dve.wait_ge(sig["gate_map"], 1)
            dve.wait_ge(sig["weights_ready"], w_n)
            dve.tensor_copy(w[0:NS, c_a + P:c_a + D], wh_ps[0:NS, 0, 0:NV]).then_inc(sig["maps_made"], 1)
            dve.tensor_scalar(w[NS:96, c_a + P:c_a + D], wh_ps[NS:96, 0, 0:NV], r3, None, ALU.mult).then_inc(sig["maps_made"], 1)
            dve.tensor_scalar(w[0:96, c_hs:c_hs + NS], w[0:96, c_hs:c_hs + NS], scale_col[0:96, 0:1], None, ALU.mult).then_inc(
                sig["maps_made"], 1)
            for q in range(2):
                half = w[:, c_hv + NS * q:c_hv + NS * (1 + q)]
                dve.tensor_scalar(half, half, scale_col[:, 1 + q:2 + q], None, ALU.mult).then_inc(sig["maps_made"], 1)
            dve.wait_ge(sig["msg_zeroed"], 5)

            def e_i(t):
                e4 = pr.edge4[:, bass.ds(t * (SUB * 6), SUB * 6)].rearrange("p (j k) -> p j k", j=SUB)
                return e4[:, :, 1:4].unsqueeze(3).to_broadcast([P, SUB, 3, NV])

            def subtract_top(t, p):
                reach(dve, sig["top_turned"], t + 1)
                reach(dve, sig["ex"], t)
                dve.tensor_tensor(below[:, :, :], logits[p][:, :, :],
                                  small_ps[:, 0:SUB * HEADS].rearrange("p (j h) -> p j h", j=SUB),
                                  ALU.subtract).then_inc(sig["below"], 1)

            def first_product(t, p):
                a, b = ec.rows_in[0][p], ec.rows_in[1][p]
                ec.gathered(dve, t, p)
                dve.tensor_tensor(rows[:, :, D:D + 2 * NV], a[:, :, NS:NS + 2 * NV], b[:, :, NS:NS + 2 * NV], ALU.add)
                dve.tensor_tensor(rows[:, :, 0:D], a[:, :, :], b[:, :, :], ALU.add).then_inc(sig["rows"], 1)
                reach(dve, sig["rows"], t + 1)
                reach(dve, sig["w"], t + 1)
                reach(dve, sig["mapped"], tiles_before_first(t - 2) + SUB)
                tp1.emit(dve, t, p, rows, wh_ps, "messages")

            def softmax_values(t, p):
                reach(dve, sig["relu"], t + 1)
                dve.tensor_tensor(leaky[:, :, :], leak[p][:, :, :], relu[p][:, :, :], ALU.add).then_inc(sig["leaky"], 1)
                reach(dve, sig["leaky"], t + 1)
                dve.tensor_tensor(leaky[:, :, :], leaky[:, :, :], dots[:, :].unsqueeze(1).to_broadcast([P, SUB, NS]),
                                  ALU.mult).then_inc(sig["dotted"], 1)
                reach(dve, sig["values_taken"], t + 1)
                dve.tensor_scalar(gates[:, :, :], half_tanh[p][:, :, NS:96], 0.5, 0.5, ALU.mult, ALU.add).then_inc(sig["gates"], 1)
                dve.tensor_tensor(e_s[:, :, :, :], values[p][:, :, 96:P].unsqueeze(2).to_broadcast([P, SUB, 3, NV]), e_i(t),
                                  ALU.mult).then_inc(sig["e_s"], 1)
                reach(dve, sig["dotted"], t + 1)
                dve.tensor_reduce(logits[p][:, :, :], leaky[:, :, :].rearrange("p j (h k) -> p j h k", h=HEADS), AXX,
                                  ALU.add).then_inc(sig["logits"], 1)
                reach(dve, sig["e_s"], 2 * t + 1)
                dve.tensor_tensor(e_s[:, :, :, :], values[p][:, :, 0:96].rearrange("p j (i c) -> p j i c", i=3), e_s[:, :, :, :],
                                  ALU.add).then_inc(sig["e_s"], 1)
                reach(dve, sig["mapped"], tiles_before_second(t - 2, T) + SUB)
                dve.tensor_scalar(tp2.groups(p)[:, :, 3, :], half_tanh[p][:, :, 0:NS], 0.5, 0.5, ALU.mult, ALU.add)
                reach(dve, sig["gates"], t + 1)
                reach(dve, sig["e_s"], 2 * t + 2)
                v5 = rows2[:, :, NS:D + 2 * NV].rearrange("p j (i c) -> p j i c", i=5)
                g = gates[:, :, :].unsqueeze(2)
                dve.tensor_tensor(v5[:, :, 3:5, :], e_s[:, :, 0:2, :], g.to_broadcast([P, SUB, 2, NV]), ALU.mult)
                dve.tensor_tensor(v5[:, :, 0:3, :], e_s[:, :, :, :], g.to_broadcast([P, SUB, 3, NV]), ALU.mult).then_inc(
                    sig["values"], 1)
                reach(dve, sig["values"], t + 1)
                tp2.emit(dve, t, p, rows2, None, "messages2")

            def maxima(t, p):
                reach(dve, sig[f"dst_loaded{p}"], dma_count(t, p, 16))
                dr = ec.drow[p]
                dve.tensor_tensor(mask[:, :], dr[0:HEADS, 0:STEP + 1], dr[0:HEADS, 1:STEP + 2], ALU.is_equal).then_inc(sig["mask"], 1)
                reach(dve, sig["mask"], 2 * t + 1)
                dve.tensor_scalar(mask[:, :], mask[:, :], 0.5, BIG, ALU.subtract, ALU.mult).then_inc(sig["mask"], 1)
                reach(dve, sig["logits_turned"], t + 1)
                reach(dve, sig["mask"], 2 * t + 2)
                reach(dve, sig["top"], t)
                dve.tensor_tensor_scan(out=running[:, ::-1], data0=mask[:, STEP:0:-1], data1=small_ps[0:HEADS, ::-1],
                                       initial=top[1 - p][:, 0:1], op0=ALU.min, op1=ALU.max).then_inc(sig["running"], 1)
                reach(dve, sig["running"], t + 1)
                reach(dve, sig["top_turned"], t - 1)
                dve.tensor_tensor_scan(out=top[p][:, :], data0=mask[:, 0:STEP], data1=running[:, :], initial=-BIG,
                                       op0=ALU.min, op1=ALU.max).then_inc(sig["top"], 1)
                reach(dve, sig["top"], t + 1)
                dve.tensor_scalar(fall[p][:, :], top[1 - p][:, 0:1], top[p][:, STEP - 1:STEP], 0.0, ALU.subtract,
                                  ALU.min).then_inc(sig["fall"], 1)

            def weigh(t, p):
                reach(dve, sig["ex"], t + 1)
                reach(dve, sig["mapped"], tiles_before_second(t, T) + SUB)
                by_head = lambda x: x.rearrange("p j (h k) -> p j h k", h=HEADS)
                e = ex[p][:, :, :].unsqueeze(3)
                dve.tensor_tensor(e_h[:, :, :, :], wh_ps[:, :, D:192].unsqueeze(2).to_broadcast([P, SUB, 3, NV]), e_i(t),
                                  ALU.mult).then_inc(sig["e_h"], 1)
                dve.tensor_tensor(by_head(weighted[p][:, :, 0:NS]), by_head(wh_ps[:, :, 0:NS]),
                                  e.to_broadcast([P, SUB, HEADS, 16]), ALU.mult)
                reach(dve, sig["e_h"], 2 * t + 1)
                dve.tensor_tensor(e_h[:, :, :, :], wh_ps[:, :, NS:D].rearrange("p j (i c) -> p j i c", i=3), e_h[:, :, :, :],
                                  ALU.add).then_inc(sig["e_h"], 1)
                reach(dve, sig["e_h"], 2 * t + 2)
                for i in range(3):
                    dve.tensor_tensor(by_head(weighted[p][:, :, NS + NV * i:NS + NV * (i + 1)]), by_head(e_h[:, :, i, :]),
                                      e.to_broadcast([P, SUB, HEADS, 8]), ALU.mult)
                dve.tensor_copy(weighted[p][:, :, D:width], ex[p][:, :, :]).then_inc(sig["weighted"], 1)

            def hand_down(t, p):
                reach(dve, sig["shrink"], t + 1)
                reach(dve, sig["out_ready"], SUB * t)
                above = ec.out[1 - p][0:1, 0, :]
                f = shrink[p][:, :].unsqueeze(2)
                for c, per_head in [(0, 16)] + [(NS + NV * i, 8) for i in range(3)] + [(D, 1)]:
                    cols = slice(c, c + HEADS * per_head)
                    ins = dve.tensor_tensor(handed[p][:, cols].rearrange("p (h k) -> p h k", h=HEADS),
                                            above[:, cols].rearrange("p (h k) -> p h k", h=HEADS),
                                            f.to_broadcast([1, HEADS, per_head]), ALU.mult)
                ins.then_inc(sig["handed"], 1)

            rolled(dve, T, [(lambda t, p: ec.make_sel(dve, t, p), 4), (subtract_top, 4), (softmax_values, 3),
                            (weigh, 4), (maxima, 3), (hand_down, 4), (first_product, 1)])

    finish_pass(nc, sig)


def build(nc, d, out, T):
    with ExitStack() as ctx:
        pr = Program(nc, d, T, out, ctx)
        n = T * STEP
        pr.table_a = nc.dram_tensor("table_a", (n, D), F32, kind="Internal").ap()
        pr.table_b = nc.dram_tensor("table_b", (n, D), F32, kind="Internal").ap()
        pr.table_c = nc.dram_tensor("table_c", (n, D), F32, kind="Internal").ap()
        pr.table_x = nc.dram_tensor("table_x", (n, D), F32, kind="Internal").ap()
        pr.agg = nc.dram_tensor("agg", (n, AGG_W), F32, kind="Internal").ap()
        pr.rows = lambda table, t: table.rearrange("(t p j) c -> t p (j c)", p=P, j=SUB)[bass.ds(t, 1)].rearrange("a p c -> (a p) c")
        pr.ident = ctx.enter_context(nc.sbuf_tensor("ident", [P, P], F32))
        pr.index = ctx.enter_context(nc.sbuf_tensor("index", [P, T * 3 * SUB], I32))
        pr.dst_f = ctx.enter_context(nc.sbuf_tensor("dst_f", [P, T * SUB], F32))
        pr.edge4 = ctx.enter_context(nc.sbuf_tensor("edge4", [P, T * SUB * 6], F32))
        pr.attr = ctx.enter_context(nc.sbuf_tensor("attr", [P, T * SUB], F32))
        prepare(pr)
        r3, r2 = 3.0 ** -0.5, 2.0 ** -0.5
        k_s, k_v = 0.25 * 96 ** -0.5, 0.25 * 128 ** -0.5
        l2s, l2v = d["L0_gnn_lin2_ws"], d["L0_gnn_lin2_wv"]
        edges_conv(pr, "l0", d["L0_gnn_fc_w1"], d["L0_gnn_fc_w2"], NS, d["edge_attr_64"], True,
                   [(0, 0, l2s[0:NS, :], k_s), (NS, 0, l2s[NS:96, :], k_s * r3)],
                   [(0, l2v[0:NS, :], k_v), (NS, l2v[NS:96, :], k_v), (96, l2v[96:128, :], k_v * r2)], 96)
        nodes_layer0(pr)
        edges_layer1(pr)
        nodes_layer1(pr)
        k_m = 96 ** -0.5
        wa, ws, wv = d["L2_gnn_Wa"], d["L2_gnn_Wl2_s"], d["L2_gnn_Wl2_v"]
        edges_conv(pr, "l2", d["L2_gnn_Wfc1"], d["L2_gnn_Wfc2"], 16, d["edge_attr_16"], False,
                   [(0, 0, wa[0:NS, :], k_m), (NS, 0, wa[NS:96, :], k_m * r3), (96, 1, d["one"], 1.0),
                    (0, 2, ws[0:NS, :], k_m), (NS, 2, ws[NS:96, :], k_m * r3)],
                   [(0, wv, k_m)], NS + 2)
        nodes_layer2(pr)
        edges_layer3(pr)
        nodes_layer3(pr)


WEIGHTS = """
L0_gnn_lin1_ws L0_gnn_lin1_wv L0_gnn_fc_w1 L0_gnn_fc_w2 L0_gnn_sc_ws L0_gnn_sc_wv L0_gnn_lin2_ws
L0_gnn_lin2_wv L1_gnn_W_ss L1_gnn_W_sv L1_gnn_W_vs L1_gnn_W_vv L1_gnn_L_s L1_gnn_L_v L2_gnn_Wfc1 L2_gnn_Wfc2
L2_gnn_Wsc0 L2_gnn_Wsc1 L2_gnn_Wl1_0 L2_gnn_Wl1_1 L2_gnn_Wl2_s L2_gnn_Wl2_v L2_gnn_Wa L3_gnn_gamma_s
L3_gnn_beta_s L3_gnn_gamma_v L3_gnn_Ws_src L3_gnn_Wv_src L3_gnn_Ws_dst L3_gnn_Wv_dst L3_gnn_W_rbf
L3_gnn_W_alpha L3_gnn_alpha_dot L3_gnn_Ws_val L3_gnn_Wv_val L3_gnn_Wg L3_gnn_w2_ss L3_gnn_w2_sv L3_gnn_w2_vs
L3_gnn_w2_vv0 L3_gnn_w2_vv1 L3_gnn_Ws_vlin L3_gnn_Wv_vlin L3_gnn_Wps L3_gnn_Wpv
""".split()


def kernel(**inputs):
    import concourse.bacc as bacc
    from concourse.bass_utils import run_bass_kernel_spmd

    a = {k: np.asarray(v) for k, v in inputs.items()}
    n, e = a["x"].shape[0], a["src"].shape[0]
    steps = -(-max(n, e) // STEP)
    steps += steps % 2
    size = steps * STEP

    def padded(v, fill=0):
        return np.concatenate([v, np.full((size - v.shape[0],) + v.shape[1:], fill, v.dtype)])

    def by_component(v):
        vec = v[..., NS:].reshape(v.shape[:-1] + (NV, 3))
        return np.concatenate([v[..., :NS], np.swapaxes(vec, -1, -2).reshape(v.shape[:-1] + (3 * NV,))], -1)

    def steps_down(v):
        v = v.reshape((steps, SUB, P) + v.shape[1:])[::-1]
        return np.moveaxis(v, 2, 0)

    def columns_down(v):
        c = v.shape[1]
        return np.ascontiguousarray(v.reshape(steps, STEP, c)[::-1].reshape(size, c).T)

    src, dst = padded(a["src"]), padded(a["dst"], n)
    before = np.concatenate([np.full(1, -1, dst.dtype), dst[:-1]])
    index = np.stack([steps_down(src), steps_down(before), steps_down(dst)], 2)
    around = np.concatenate([np.full(1, -1, dst.dtype), dst, np.full(1, -2, dst.dtype)])
    e4 = steps_down(padded(a["edge_attr_4"]))
    x = padded(by_component(a["x"]))
    d = {
        "x": x,
        "xT": np.ascontiguousarray(x.reshape(steps, P, SUB, D).transpose(3, 0, 2, 1).reshape(D, size)),
        "node_attr": np.ascontiguousarray(padded(a["node_vec1"]).reshape(steps, P, SUB).transpose(1, 0, 2).reshape(P, -1)),
        "edge_index": np.ascontiguousarray(index.reshape(P, -1)),
        "dst_rows": np.ascontiguousarray(np.stack([around[t * STEP:(t + 1) * STEP + 2] for t in range(steps)])[::-1]),
        "edge_attr_4": np.ascontiguousarray(np.concatenate([e4, e4[..., 1:3]], -1).reshape(P, -1)),
        "edge_attr_16": columns_down(padded(a["edge_attr_16"])),
        "edge_attr_64": columns_down(padded(a["edge_attr_64"])),
        "identity": np.eye(P, dtype=np.float32),
        "one": np.ones((1, 1), np.float32),
        "alpha_dot": a["L3_gnn_alpha_dot"].reshape(1, NS),
        "Ws_val_T": np.ascontiguousarray(a["L3_gnn_Ws_val"].T),
        "L1_rad": np.concatenate([by_component(a["L1_gnn_W_rad"].T), by_component(a["L1_gnn_b_rad"][None])]),
    }
    for k in WEIGHTS:
        d[k] = a[k].reshape(-1, a[k].shape[-1])
    nc = bacc.Bacc("TRN2", target_bir_lowering=False, num_devices=1)
    aps = {k: nc.dram_tensor(f"in_{k}", v.shape, mybir.dt.from_np(v.dtype), kind="ExternalInput").ap() for k, v in d.items()}
    out = nc.dram_tensor("out", (size, D), F32, kind="ExternalOutput").ap()
    build(nc, aps, out, steps)
    got = run_bass_kernel_spmd(nc, [{f"in_{k}": v for k, v in d.items()}], core_ids=[0]).results[0]["out"][:n]
    vec = got[:, NS:].reshape(n, 3, NV)
    return np.concatenate([got[:, :NS], np.swapaxes(vec, 1, 2).reshape(n, 3 * NV)], 1)
```

```python
from contextlib import ExitStack

import numpy as np

import concourse.bass as bass
from concourse import mybir

F32 = mybir.dt.float32
I32 = mybir.dt.int32
ALU = mybir.AluOpType
ACT = mybir.ActivationFunctionType
AXX = mybir.AxisListType.X

P = 128
SUB = 4
STEP = P * SUB
NS, NV = 64, 32
D = NS + 3 * NV
SCR = 1 << 20
AGG_W = 192
EPS = 1e-5
HEADS = 4
BIG = 3.0e38


class Signals(dict):

    def __init__(self, nc, ctx):
        self.nc, self.ctx, self.kept = nc, ctx, []

    def __missing__(self, name):
        self[name] = self.ctx.enter_context(self.nc.semaphore(name))
        return self[name]


def reach(eng, sem, count):
    if isinstance(count, int) and count <= 0:
        return
    eng.wait_ge(sem, count)


def reach_gate(eng, sem, count, gate):
    if isinstance(count, int) and count <= 0:
        return
    eng.wait_ge(sem, count)
    eng.sem_inc(gate, 1)


def dma_count(t, p, each):
    if isinstance(t, int):
        return each * (t // 2 + 1) if t >= 0 else 0
    return (t - p) * (each // 2) + each


def rolled(eng, steps, stages):
    deep = max(sum(stage[1:]) for stage in stages)
    head = (deep + 3) // 2 * 2

    def one(s, k):
        for f, lag, *also in stages:
            t = s + k - lag
            if isinstance(t, int) and not 0 <= t < steps + sum(also):
                continue
            f(t, (k - lag) % 2)

    for s in range(head):
        one(0, s)
    with eng.Fori(head, steps - 1, 2) as i:
        one(i, 0)
        one(i, 1)
    for s in range(deep):
        one(steps, s)


def present(t, steps):
    return not isinstance(t, int) or 0 <= t < steps


class Program:

    def __init__(self, nc, d, steps, output, lasting):
        self.nc, self.d, self.T, self.output, self.lasting = nc, d, steps, output, lasting


def finish_pass(nc, sig):
    nc.all_engine_barrier()
    for name, sem in sig.items():
        if name not in sig.kept:
            nc.gpsimd.sem_clear(sem)
    nc.all_engine_barrier()


def weight_tile(pr, ctx, sig, name, cols, parts):
    tile = ctx.enter_context(pr.nc.sbuf_tensor(name, [P, cols], F32))

    def zero(pool):
        pool.memset(tile[:, :], 0.0).then_inc(sig["weights_zeroed"], 1)

    def load(sp):
        sp.wait_ge(sig["weights_zeroed"], 1)
        for r, c, ap, _ in parts:
            sp.dma_start(tile[r:r + ap.shape[0], c:c + ap.shape[1]], ap).then_inc(sig["weights_loaded"], 16)

    def scale(dve):
        dve.wait_ge(sig["weights_loaded"], 16 * len(parts))
        for r, c, ap, factor in parts:
            part = tile[r:r + ap.shape[0], c:c + ap.shape[1]]
            dve.tensor_scalar(part, part, float(factor), None, ALU.mult).then_inc(sig["weights_ready"], 1)

    return tile, zero, load, scale, len(parts)


def block_diagonal(c, ap, factor):
    n = ap.shape[1]
    return [(NV * i, c + n * i, ap, factor) for i in range(3)]


def prepare(pr):
    nc, T, pr.name = pr.nc, pr.T, "p"
    with ExitStack() as ctx:
        sig = Signals(nc, ctx)
        sb = lambda name, shape, dt=F32: ctx.enter_context(nc.sbuf_tensor(name, shape, dt))
        zeros = sb("zeros", [P, T * SUB * AGG_W // 12])
        same = sb("same_as_previous", [P, T, SUB])
        dst = sb("dst_of_steps", [T, STEP + 2], I32)
        cont, mask = sb("cont_of_steps", [T, SUB, P]), sb("mask_of_steps", [T, STEP + 1])
        xs = [sb(f"p_xs{p}", [NS, STEP]) for p in range(2)]
        xv = [sb(f"p_xv{p}", [3 * NV, STEP]) for p in range(2)]
        hs = [sb(f"p_h{p}", [P, SUB, D]) for p in range(2)]
        acc = [ctx.enter_context(nc.psum_tensor(f"p_acc{p}", [P, SUB, 256], F32)) for p in range(2)]
        w, w_zero, w_load, w_scale, w_n = weight_tile(pr, ctx, sig, "p_w", D, [
            (0, 0, pr.d["L0_gnn_lin1_ws"], NS ** -0.5)] + block_diagonal(NS, pr.d["L0_gnn_lin1_wv"], NV ** -0.5))
        block = ctx.enter_context(nc.Block())
        agg_flat = pr.agg.rearrange("(p r) c -> p (r c)", p=P)
        piece = T * SUB * AGG_W // 12

        @block.gpsimd
        def _(pool):
            w_zero(pool)
            pool.memset(zeros[:, :], 0.0).then_inc(sig["zeros_made"], 1)

        @block.sync
        def _(sp):
            w_load(sp)
            sp.dma_start(pr.ident[:, :], pr.d["identity"]).then_inc(sig["resident"], 16)
            sp.dma_start(pr.index[:, :], pr.d["edge_index"]).then_inc(sig["resident"], 16)
            sp.dma_start(pr.edge4[:, :], pr.d["edge_attr_4"]).then_inc(sig["resident"], 16)
            sp.dma_start(pr.attr[:, :], pr.d["node_attr"]).then_inc(sig["resident"], 16)
            sp.dma_start(dst[:, :], pr.d["dst_rows"]).then_inc(sig["dst_loaded"], 16)
            sp.wait_ge(sig["cont_made"], 1)
            sp.dma_start(pr.cont_rows, cont[:, :, :].rearrange("t j e -> t (j e)")).then_inc(sig["rows_stored"], 16)
            sp.wait_ge(sig["mask"], 2)
            sp.dma_start(pr.mask_rows, mask[:, :]).then_inc(sig["rows_stored"], 16)
            sp.wait_ge(sig["zeros_made"], 1)
            for k in range(12):
                sp.dma_start(agg_flat[:, k * piece:(k + 1) * piece], zeros[:, :]).then_inc(sig["agg_zeroed"], 16)

            def load(t, p):
                reach(sp, sig["h_product"], t - 1)
                sp.dma_start(xs[p][:, :], pr.d["xT"][0:NS, bass.ds(t * STEP, STEP)]).then_inc(sig[f"x_loaded{p}"], 16)
                sp.dma_start(xv[p][:, :], pr.d["xT"][NS:D, bass.ds(t * STEP, STEP)]).then_inc(sig[f"x_loaded{p}"], 16)

            rolled(sp, T, [(load, 0)])
            sp.wait_ge(sig["agg_zeroed"], 12 * 16)
            sp.wait_ge(sig["resident"], 4 * 16)
            sp.wait_ge(sig["rows_stored"], 2 * 16)

        @block.tensor
        def _(pe):
            pe.wait_ge(sig["weights_ready"], w_n)

            def product(t, p):
                reach(pe, sig[f"x_loaded{p}"], dma_count(t, p, 32))
                reach_gate(pe, sig["h_out"], t - 1, sig["pe_gate"])
                for j in range(SUB):
                    cols = slice(j * P, (j + 1) * P)
                    pe.matmul(acc[p][:, j, 0:NS], xs[p][:, cols], w[0:NS, 0:NS], start=True, stop=True)
                    mm = pe.matmul(acc[p][:, j, NS:D], xv[p][:, cols], w[0:3 * NV, NS:D], start=True, stop=True)
                mm.then_inc(sig["h_product"], 1)

            rolled(pe, T, [(product, 0)])

        @block.vector
        def _(dve):
            w_scale(dve)
            dve.wait_ge(sig["dst_loaded"], 16)
            above = dst[:, 1 + P:2 + STEP:P].unsqueeze(2).to_broadcast([T, SUB, P])
            dve.tensor_tensor(cont[:, :, :], dst[:, 1:1 + STEP].rearrange("t (j e) -> t j e", j=SUB), above,
                              ALU.is_equal).then_inc(sig["cont_made"], 1)
            dve.tensor_tensor(mask[:, :], dst[:, 0:STEP + 1], dst[:, 1:STEP + 2], ALU.is_equal).then_inc(sig["mask"], 1)
            dve.wait_ge(sig["mask"], 1)
            dve.tensor_scalar(mask[:, :], mask[:, :], 0.5, BIG, ALU.subtract, ALU.mult).then_inc(sig["mask"], 1)
            dve.wait_ge(sig["resident"], 4 * 16)
            index = pr.index[:, :].rearrange("p (t k j) -> p t k j", k=3, j=SUB)
            dve.tensor_tensor(same[:, :, :], index[:, :, 1, :], index[:, :, 2, :], ALU.is_equal).then_inc(sig["same"], 1)
            dve.wait_ge(sig["same"], 1)
            dve.scalar_tensor_tensor(out=index[:, :, 1, :], in0=same[:, :, :], scalar=float(SCR), in1=index[:, :, 2, :],
                                     op0=ALU.mult, op1=ALU.add).then_inc(sig["same"], 1)
            dve.tensor_copy(pr.dst_f[:, :].rearrange("p (t j) -> p t j", j=SUB), index[:, :, 2, :]).then_inc(sig["same"], 1)
            dve.wait_ge(sig["same"], 3)

            def out(t, p):
                reach(dve, sig["h_product"], t + 1)
                reach(dve, sig[f"h_stored{p}"], dma_count(t - 2, p, 16))
                dve.tensor_tensor(hs[p][:, :, :], acc[p][:, :, 0:D],
                                  pr.attr[:, bass.ds(t * SUB, SUB)].unsqueeze(2).to_broadcast([P, SUB, D]),
                                  ALU.mult).then_inc(sig["h_out"], 1)

            rolled(dve, T, [(out, 0)])

        @block.scalar
        def _(act):
            def store(t, p):
                reach(act, sig["h_out"], t + 1)
                act.dma_start(pr.rows(pr.table_a, t), hs[p][:, :, :].rearrange("p j c -> p (j c)")).then_inc(
                    sig[f"h_stored{p}"], 16)

            rolled(act, T, [(store, 0)])
            for p in range(2):
                act.wait_ge(sig[f"h_stored{p}"], 16 * (T // 2))

    finish_pass(nc, sig)


class EdgeCommon:

    def __init__(self, pr, ctx, sig, tables, width, rows_read, row_width=D, banks=2):
        nc = pr.nc
        self.pr, self.sig, self.tables, self.width, self.rows_read = pr, sig, tables, width, rows_read
        for n in ("gathered0", "gathered1", "scattered0", "scattered1"):
            sig[n] = pr.lasting.enter_context(nc.semaphore(f"{pr.name}_{n}"))
            sig.kept.append(n)
        sb = lambda name, shape, dt=F32: ctx.enter_context(nc.sbuf_tensor(f"{pr.name}_{name}", shape, dt))
        self.gather_idx = [sb(f"e_gidx{p}", [P, 3 * SUB], I32) for p in range(2)]
        self.scatter_idx = [sb(f"e_sidx{p}", [P, SUB], I32) for p in range(2)]
        self.rows_in = [[sb(f"e_g{k}_{p}", [P, SUB, row_width]) for p in range(2)] for k in range(len(tables))]
        self.drow = [sb(f"e_drow{p}", [P, STEP + 2], I32) for p in range(2)]
        self.sel = [sb(f"e_sel{p}", [P, SUB, P]) for p in range(2)]
        self.cont = [sb(f"e_cont{p}", [1, STEP]) for p in range(2)]
        self.out = [sb(f"e_out{p}", [P, SUB, AGG_W]) for p in range(2)]
        self.o_ps = [ctx.enter_context(nc.psum_tensor(f"{pr.name}_e_sums{k}", [P, 512], F32)) for k in range(banks)] * (2 // banks)

    def load_dst(self, sp, t, p):
        sig = self.sig
        reach(sp, sig["sel_made"], t - 1)
        reach(sp, sig["summed"], SUB * t - SUB)
        sp.dma_start(self.cont[p][:, :], self.pr.cont_rows[bass.ds(t, 1), :]).then_inc(sig[f"dst_loaded{p}"], 16)
        row = self.pr.d["dst_rows"][bass.ds(t, 1), :]
        sp.dma_start(self.drow[p][:, :], row.to_broadcast([P, STEP + 2])).then_inc(sig[f"dst_loaded{p}"], 16)

    def gather(self, pool, t, p):
        sig, pr = self.sig, self.pr
        reach_gate(pool, sig[self.rows_read], t - 1, sig["pool_gate"])
        pool.tensor_copy(self.gather_idx[p][:, :], pr.index[:, bass.ds(t * (3 * SUB), 3 * SUB)]).then_inc(
            sig["index_copied"], 1)
        reach_gate(pool, sig["index_copied"], t + 1, sig["pool_gate"])
        for j in reversed(range(SUB)):
            for k, (table, slot) in enumerate(self.tables):
                pool.indirect_dma_start(
                    out=self.rows_in[k][p][:, j, 0:D], out_offset=None, in_=table,
                    in_offset=bass.IndirectOffsetOnAxis(ap=self.gather_idx[p][:, slot * SUB + j:slot * SUB + j + 1], axis=0),
                ).then_inc(sig[f"gathered{p}"], 16)

    def gathered(self, eng, t, p):
        reach(eng, self.sig[f"gathered{p}"], dma_count(t, p, 16 * SUB * len(self.tables)))

    def scatter(self, pool, t, p):
        sig, pr = self.sig, self.pr
        reach_gate(pool, sig[f"scattered{p}"], dma_count(t - 2, p, 16 * SUB), sig["pool_gate"])
        pool.tensor_copy(self.scatter_idx[p][:, :], pr.index[:, bass.ds(t * (3 * SUB) + SUB, SUB)]).then_inc(
            sig["scatter_index_copied"], 1)
        reach_gate(pool, sig["scatter_index_copied"], t + 1, sig["pool_gate"])
        reach_gate(pool, sig["out_ready"], SUB * t + SUB, sig["pool_gate"])
        for j in range(SUB):
            pool.indirect_dma_start(
                out=pr.agg, out_offset=bass.IndirectOffsetOnAxis(ap=self.scatter_idx[p][:, j:j + 1], axis=0),
                in_=self.out[p][:, j, :], in_offset=None, bounds_check=pr.agg.shape[0] - 1, oob_is_err=False,
            ).then_inc(sig[f"scattered{p}"], 16)

    def start_out(self, pool):
        for p in range(2):
            pool.memset(self.out[p][:, :, :], 0.0).then_inc(self.sig["out_zeroed"], 1)

    def make_sel(self, dve, t, p):
        sig, pr = self.sig, self.pr
        reach(dve, sig[f"dst_loaded{p}"], dma_count(t, p, 32))
        reach(dve, sig["summed"], SUB * t - SUB)
        for j in range(SUB):
            ins = dve.tensor_scalar(self.sel[p][:, j, :], self.drow[p][:, 1 + j * P:1 + (j + 1) * P],
                                    pr.dst_f[:, bass.ds(t * SUB + j, 1)], None, ALU.is_equal)
        ins.then_inc(sig["sel_made"], 1)

    def carry(self, pe, t, p, k, handed=None):
        j = SUB - 1 - k
        if k == 0 and handed is not None:
            above = handed
        else:
            above = self.out[p][0:1, j + 1, 0:self.width] if k else self.out[1 - p][0:1, 0, 0:self.width]
            reach(pe, self.sig["out_ready"], SUB * t + k)
        return pe.matmul(self.o_ps[k % 2][:, 0:self.width], self.cont[p][:, j * P:(j + 1) * P], above, start=False, stop=True)

    def take_out(self, act, t, p, k):
        j = SUB - 1 - k
        reach(act, self.sig["summed"], SUB * t + k + 1)
        if k == 0:
            reach(act, self.sig[f"scattered{p}"], dma_count(t - 2, p, 16 * SUB))
        act.activation(self.out[p][:, j, 0:self.width], self.o_ps[k % 2][:, 0:self.width], ACT.Copy).then_inc(
            self.sig["out_ready"], 1)

    def all_scattered(self, pool):
        for p in range(2):
            pool.wait_ge(self.sig[f"scattered{p}"], 16 * SUB * (self.pr.T // 2))


class TensorProduct:

    def __init__(self, pr, ctx, sig, cross, name):
        nc = pr.nc
        self.pr, self.sig, self.cross, self.name, self.blocks = pr, sig, cross, name, 3 if cross else 2
        sb = lambda n, shape: ctx.enter_context(nc.sbuf_tensor(f"{pr.name}_{name}_{n}", shape, F32))
        self.msg = [sb(f"msg{p}", [P, SUB, self.blocks * P]) for p in range(2)]
        self.ws = sb("ws", [P, SUB, NS])
        self.we = sb("we", [P, SUB, NV])
        self.ve = sb("ve", [P, SUB, 3, NV])
        self.dot = sb("dot", [P, SUB, NV])
        if cross:
            self.c1 = sb("c1", [P, SUB, 3, NV])
            self.c2 = sb("c2", [P, SUB, 3, NV])

    def scalars(self, p):
        return self.msg[p][:, :, self.blocks * P - NS:self.blocks * P]

    def emit(self, dve, t, p, rows, w, done):
        sig, n, msg = self.sig, self.name, self.msg[p]
        e4 = self.pr.edge4[:, bass.ds(t * (SUB * 6), SUB * 6)].rearrange("p (j k) -> p j k", j=SUB)
        e_i = lambda a: e4[:, :, 1 + a:4 + a].unsqueeze(3).to_broadcast([P, SUB, 3, NV])
        s = self.scalars(p) if w is None else rows[:, :, 0:NS]
        if self.cross:
            v5 = rows[:, :, NS:NS + 5 * NV].rearrange("p j (i c) -> p j i c", i=5)
            groups = msg[:, :, P:3 * P].rearrange("p j (g c) -> p j g c", g=4)
            scaled, cross = groups[:, :, 0:3, 0:NV], groups[:, :, 0:3, NV:2 * NV]
        else:
            v5 = rows[:, :, NS:D].rearrange("p j (i c) -> p j i c", i=3)
            scaled = msg[:, :, 96:192].rearrange("p j (i c) -> p j i c", i=3)
        v = v5[:, :, 0:3, :]

        def op(out, a, b, o, name, *after):
            for x in after:
                dve.wait_ge(sig[f"{n}_{x}"], t + 1)
            return dve.tensor_tensor(out, a, b, o).then_inc(sig[done if name == "done" else f"{n}_{name}"], 1)

        if w is not None:
            op(self.ws[:, :, :], w[:, :, 0:NS], s, ALU.mult, "ws")
            op(self.scalars(p), w[:, :, NS:2 * NS], s, ALU.mult, "s2")
            op(self.we[:, :, :], w[:, :, 128:160], e4[:, :, 0:1].to_broadcast([P, SUB, NV]), ALU.mult, "we")
        op(self.ve[:, :, :, :], v, e_i(0), ALU.mult, "ve")
        if self.cross:
            op(self.c1[:, :, :, :], v5[:, :, 1:4, :], e_i(2), ALU.mult, "c1")
            op(self.c2[:, :, :, :], v5[:, :, 2:5, :], e_i(1), ALU.mult, "c2")
        e0 = e4[:, :, 0:1].to_broadcast([P, SUB, NS])
        if w is not None:
            op(msg[:, :, 0:NS], self.ws[:, :, :], e0, ALU.mult, "s1", "ws")
        else:
            op(msg[:, :, 0:NS], s, e0, ALU.mult, "s1")
        op(self.dot[:, :, :], self.ve[:, :, 0, :], self.ve[:, :, 1, :], ALU.add, "dot1", "ve")
        if w is None:
            op(cross, self.c1[:, :, :, :], self.c2[:, :, :, :], ALU.subtract, "cr", "c1", "c2")
            op(scaled, v, e4[:, :, 0:1].unsqueeze(3).to_broadcast([P, SUB, 3, NV]), ALU.mult, "v2")
            return op(msg[:, :, NS:96], self.dot[:, :, :], self.ve[:, :, 2, :], ALU.add, "done", "dot1")
        if self.cross:
            op(self.c1[:, :, :, :], self.c1[:, :, :, :], self.c2[:, :, :, :], ALU.subtract, "cr", "c1", "c2")
        op(scaled, self.we[:, :, :].unsqueeze(2).to_broadcast([P, SUB, 3, NV]), v, ALU.mult, "v2", "we")
        op(self.dot[:, :, :], self.dot[:, :, :], self.ve[:, :, 2, :], ALU.add, "dot2", "dot1")
        if self.cross:
            op(cross, w[:, :, 192:224].unsqueeze(2).to_broadcast([P, SUB, 3, NV]), self.c1[:, :, :, :], ALU.mult, "v3", "cr")
        return op(msg[:, :, NS:96], w[:, :, 160:192], self.dot[:, :, :], ALU.mult, "done", "dot2")


def grouped(c, m, scalar_factor, vector_factor, cross_factor):
    v, x = m[NS:96, :], m[96:P, :]
    return [(0, c, v, vector_factor), (NV, c, x, cross_factor), (NS, c + NV, v, vector_factor), (96, c + NV, x, cross_factor),
            (0, c + NS, v, vector_factor), (NV, c + NS, x, cross_factor), (NS, c + 96, m[0:NS, :], scalar_factor)]


def edges_conv(pr, name, fc1, fc2, hidden_in, edge_features, cross, s_parts, v_map, v_factors, n_s, s_columns, v_col):
    nc, T, pr.name = pr.nc, pr.T, name
    n_w = fc2.shape[1]
    with ExitStack() as ctx:
        sig = Signals(nc, ctx)
        sb = lambda n, shape, dt=F32: ctx.enter_context(nc.sbuf_tensor(f"{name}_{n}", shape, dt))
        ps = lambda n, shape: ctx.enter_context(nc.psum_tensor(f"{name}_{n}", shape, F32))
        width = v_col + 3 * NV
        ec = EdgeCommon(pr, ctx, sig, [(pr.table_a, 0)], width, "messages", D + 2 * NV, banks=1)
        tp = TensorProduct(pr, ctx, sig, cross, "tp")
        feat = [sb(f"feat{p}", [hidden_in, STEP]) for p in range(2)]
        hid = [sb(f"hid{p}", [NS, STEP]) for p in range(2)]
        turned = [sb(f"turned{k}", [P, tp.blocks * P]) for k in range(2)]
        e_s = sb("e_s", [P, SUB, 3, NV])
        mapped = [sb(f"mapped{p}", [P, SUB, width]) for p in range(2)]
        hid_ps, w_ps, m_ps = ps("hid_ps", [P, STEP]), ps("w_ps", [P, SUB, 256]), ps("m_ps", [P, SUB, 256])
        turn_ps = [ps(f"turn_ps{k}", [P, 4 * P]) for k in range(2)]
        c_fc1, c_fc2, c_m = 0, NS, NS + n_w
        x_col, e_col = n_s, n_s + 96
        f_s, f_v, f_x = v_factors
        if cross:
            v_parts = grouped(c_m + x_col, v_map, f_s, f_v, f_x)
            cuts = (0, n_s, n_s + NS, n_s + P)
        else:
            v = v_map[NS:96, :]
            v_parts = [(96, c_m + x_col, v, f_v), (0, c_m + x_col + NV, v, f_v), (NV, c_m + x_col + 2 * NV, v, f_v),
                       (NS, c_m + e_col, v_map[0:NS, :], f_s)]
            cuts = (0, n_s + NV, n_s + P)
        w, w_zero, w_load, w_scale, w_n = weight_tile(pr, ctx, sig, f"{name}_w", c_m + n_s + P, [
            (0, c_fc1, fc1, hidden_in ** -0.5), (0, c_fc2, fc2, NS ** -0.5)]
            + [(r, c_m + c, ap, f) for r, c, ap, f in s_parts] + v_parts)
        block = ctx.enter_context(nc.Block())

        @block.sync
        def _(sp):
            w_load(sp)

            def load(t, p):
                reach(sp, sig["hidden"], t - 1)
                sp.dma_start(feat[p][:, :], edge_features[:, bass.ds(t * STEP, STEP)]).then_inc(sig[f"feat_loaded{p}"], 16)

            rolled(sp, T, [(load, 0)])

        @block.gpsimd
        def _(pool):
            w_zero(pool)
            ec.start_out(pool)
            for p in range(2):
                pool.memset(tp.msg[p][:, :, :], 0.0).then_inc(sig["constants_set"], 1)
                pool.memset(mapped[p][:, :, :], 1.0).then_inc(sig["constants_set"], 1)
            rolled(pool, T, [(lambda t, p: ec.gather(pool, t, p), 0), (lambda t, p: ec.scatter(pool, t, p), 3)])
            ec.all_scattered(pool)

        @block.tensor
        def _(pe):
            pe.wait_ge(sig["weights_ready"], w_n)
            pe.wait_ge(sig["out_zeroed"], 2)

            def hidden(t, p):
                reach(pe, sig[f"feat_loaded{p}"], dma_count(t, p, 16))
                reach_gate(pe, sig["silu_done"], t, sig["pe_gate"])
                pe.matmul(hid_ps[0:NS, :], w[0:hidden_in, c_fc1:c_fc1 + NS], feat[p][:, :], start=True, stop=True).then_inc(
                    sig["hidden"], 1)

            def weights(t, p):
                reach(pe, sig["silu_done"], t + 1)
                reach(pe, sig["messages"], t)
                for j in range(SUB):
                    mm = pe.matmul(w_ps[:, j, 0:n_w], hid[p][:, j * P:(j + 1) * P], w[0:NS, c_fc2:c_fc2 + n_w],
                                   start=True, stop=True)
                mm.then_inc(sig["weights"], 1)

            def turn(t, p, k):
                j = SUB - 1 - k
                reach(pe, sig["turn_taken"], SUB * t + k - 1)
                for q in range(tp.blocks):
                    mm = pe.transpose(turn_ps[k % 2][:, q * P:(q + 1) * P], tp.msg[p][:, j, q * P:(q + 1) * P], pr.ident[:, :])
                mm.then_inc(sig["turned"], 1)

            def linear(t, p, k):
                j = SUB - 1 - k
                reach(pe, sig["turn_taken"], SUB * t + k + 1)
                for q in range(tp.blocks):
                    mm = pe.matmul(m_ps[:, j, cuts[q]:cuts[q + 1]], turned[k % 2][:, q * P:(q + 1) * P],
                                   w[:, c_m + cuts[q]:c_m + cuts[q + 1]], start=True, stop=True)
                mm.then_inc(sig["linear"], 1)

            def sums(t, p, k):
                j = SUB - 1 - k
                reach(pe, sig["out_ready"], SUB * t + k)
                pe.matmul(ec.o_ps[k % 2][:, 0:width], ec.sel[p][:, j, :], mapped[p][:, j, :], start=True, stop=False)
                ec.carry(pe, t, p, k).then_inc(sig["summed"], 1)

            def map_and_sum(t, p):
                maps, summing = present(t, T), present(t - 1, T)
                if maps:
                    reach(pe, sig["messages"], t + 1)
                    turn(t, p, 0)
                reach(pe, sig["combined"], t)
                reach(pe, sig["sel_made"], t)
                for k in range(SUB):
                    if maps and k + 1 < SUB:
                        turn(t, p, k + 1)
                    if summing:
                        sums(t - 1, 1 - p, k)
                    if maps:
                        linear(t, p, k)

            rolled(pe, T, [(hidden, 0), (weights, 1), (map_and_sum, 2, 1)])

        @block.scalar
        def _(act):
            def silu(t, p):
                reach(act, sig["hidden"], t + 1)
                reach(act, sig["weights"], t - 1)
                act.activation(hid[p][:, :], hid_ps[0:NS, :], ACT.Silu).then_inc(sig["silu_done"], 1)

            def copies(t, p):
                rows = ec.rows_in[0][p]
                ec.gathered(act, t, p)
                act.activation(rows[:, :, D:D + 2 * NV], rows[:, :, NS:NS + 2 * NV], ACT.Copy).then_inc(sig["rows_doubled"], 1)

            def take(t, p, k):
                reach(act, sig["turned"], SUB * t + k + 1)
                reach(act, sig["linear"], SUB * t + k - 1)
                act.activation(turned[k % 2][:, :], turn_ps[k % 2][:, 0:tp.blocks * P], ACT.Copy).then_inc(sig["turn_taken"], 1)

            def take_both(t, p):
                for k in range(-1, SUB):
                    if present(t, T) and k + 1 < SUB:
                        take(t, p, k + 1)
                    if present(t - 1, T) and k >= 0:
                        ec.take_out(act, t - 1, 1 - p, k)

            def take_scalars(t, p):
                reach(act, sig["linear"], SUB * t + SUB)
                reach(act, sig["summed"], SUB * t - SUB)
                for col, n, to in s_columns:
                    ins = act.activation(mapped[p][:, :, to:to + n], m_ps[:, :, col:col + n], ACT.Copy)
                ins.then_inc(sig["scalars_taken"], 1)

            act.wait_ge(sig["out_zeroed"], 2)
            act.wait_ge(sig["constants_set"], 4)
            rolled(act, T, [(silu, 0)] + [(copies, 1)] * cross + [
                (take_both, 2, 1), (lambda t, p: ec.load_dst(act, t, p), 1), (take_scalars, 2)])

        @block.vector
        def _(dve):
            w_scale(dve)
            dve.wait_ge(sig["constants_set"], 4)

            def messages(t, p):
                ec.gathered(dve, t, p)
                if cross:
                    reach(dve, sig["rows_doubled"], t + 1)
                reach(dve, sig["turned"], SUB * t - SUB)
                reach(dve, sig["messages"], t)
                reach(dve, sig["weights"], t + 1)
                tp.emit(dve, t, p, ec.rows_in[0][p], w_ps, "messages")

            def combine(t, p):
                ec.make_sel(dve, t, p)
                reach(dve, sig["scalars_taken"], t + 1)
                e4 = pr.edge4[:, bass.ds(t * (SUB * 6), SUB * 6)].rearrange("p (j k) -> p j k", j=SUB)
                dve.tensor_tensor(e_s[:, :, :, :], m_ps[:, :, e_col:e_col + NV].unsqueeze(2).to_broadcast([P, SUB, 3, NV]),
                                  e4[:, :, 1:4].unsqueeze(3).to_broadcast([P, SUB, 3, NV]), ALU.mult).then_inc(sig["e_s"], 1)
                reach(dve, sig["e_s"], t + 1)
                dve.tensor_tensor(mapped[p][:, :, v_col:width].rearrange("p j (i c) -> p j i c", i=3),
                                  m_ps[:, :, x_col:e_col].rearrange("p j (i c) -> p j i c", i=3), e_s[:, :, :, :],
                                  ALU.add).then_inc(sig["combined"], 1)

            rolled(dve, T, [(messages, 1), (combine, 2)])

    finish_pass(nc, sig)


def edges_layer1(pr):
    nc, T, pr.name = pr.nc, pr.T, "l1"
    with ExitStack() as ctx:
        sig = Signals(nc, ctx)
        sb = lambda n, shape, dt=F32: ctx.enter_context(nc.sbuf_tensor(f"l1_{n}", shape, dt))
        ps = lambda n, shape: ctx.enter_context(nc.psum_tensor(f"l1_{n}", shape, F32))
        ec = EdgeCommon(pr, ctx, sig, [(pr.table_x, 0)], D, "products")
        feat = [sb(f"feat{p}", [17, STEP]) for p in range(2)]
        prod = [sb(f"prod{p}", [P, SUB, 2 * P]) for p in range(2)]
        ve, dot, e_s = sb("ve", [P, SUB, 3, NV]), sb("dot", [P, SUB, NV]), sb("e_s", [P, SUB, 3, NV])
        pT = [sb(f"pT{k}", [P, 2 * P]) for k in range(2)]
        rad = [sb(f"rad{p}", [P, SUB, D]) for p in range(2)]
        msg = [sb(f"msg{p}", [P, SUB, D]) for p in range(2)]
        rad_ps, m_ps = ps("rad_ps", [P, SUB, 256]), ps("m_ps", [P, SUB, 256])
        pT_ps = [ps(f"pT_ps{k}", [P, 512]) for k in range(2)]
        r2, r3 = 2.0 ** -0.5, 3.0 ** -0.5
        c0, c1, cr = 0, 96, 192
        W_vs, f_vs = pr.d["L1_gnn_W_vs"], r3 * NV ** -0.5 * r2
        w, w_zero, w_load, w_scale, w_n = weight_tile(pr, ctx, sig, "l1_w", cr + D, [
            (0, c0, pr.d["L1_gnn_W_ss"], NS ** -0.5 * r2), (NS, c0, pr.d["L1_gnn_W_vv"], r3 * NV ** -0.5 * r2),
            (96, c0 + NS, W_vs, f_vs), (0, c1, W_vs, f_vs), (NV, c1 + NV, W_vs, f_vs),
            (NS, c1 + NS, pr.d["L1_gnn_W_sv"], r3 * NS ** -0.5 * r2), (0, cr, pr.d["L1_rad"], 1.0)])
        block = ctx.enter_context(nc.Block())

        @block.sync
        def _(sp):
            w_load(sp)
            sp.wait_ge(sig["ones_set"], 2)

            def load(t, p):
                reach(sp, sig["radial"], t - 1)
                sp.dma_start(feat[p][0:16, :], pr.d["edge_attr_16"][:, bass.ds(t * STEP, STEP)]).then_inc(
                    sig[f"feat_loaded{p}"], 16)

            rolled(sp, T, [(load, 0), (lambda t, p: ec.load_dst(sp, t, p), 0)])

        @block.gpsimd
        def _(pool):
            w_zero(pool)
            ec.start_out(pool)
            for p in range(2):
                pool.memset(feat[p][:, :], 1.0).then_inc(sig["ones_set"], 1)
            rolled(pool, T, [(lambda t, p: ec.gather(pool, t, p), 0), (lambda t, p: ec.scatter(pool, t, p), 2)])
            ec.all_scattered(pool)

        @block.tensor
        def _(pe):
            pe.wait_ge(sig["weights_ready"], w_n)
            pe.wait_ge(sig["out_zeroed"], 2)

            def radial(t, p):
                reach(pe, sig[f"feat_loaded{p}"], dma_count(t, p, 16))
                reach(pe, sig["sigmoid_done"], t)
                for j in range(SUB):
                    mm = pe.matmul(rad_ps[:, j, 0:D], feat[p][:, j * P:(j + 1) * P], w[0:17, cr:cr + D],
                                   start=True, stop=True)
                mm.then_inc(sig["radial"], 1)

            def turn(t, p, k):
                j = SUB - 1 - k
                reach(pe, sig["pT_taken"], SUB * t + k - 1)
                for q in range(2):
                    mm = pe.transpose(pT_ps[k % 2][:, q * P:(q + 1) * P], prod[p][:, j, q * P:(q + 1) * P], pr.ident[:, :])
                mm.then_inc(sig["pT"], 1)

            def linear(t, p, k):
                j, a = SUB - 1 - k, pT[k % 2]
                reach(pe, sig["pT_taken"], SUB * t + k + 1)
                pe.matmul(m_ps[:, j, 0:96], a[:, 0:P], w[:, c0:c0 + 96], start=True, stop=True)
                mm = pe.matmul(m_ps[:, j, 96:192], a[:, P:2 * P], w[:, c1:c1 + 96], start=True, stop=True)
                mm.then_inc(sig["linear"], 1)

            def sums(t, p, k):
                j = SUB - 1 - k
                reach(pe, sig["out_ready"], SUB * t + k - 1)
                pe.matmul(ec.o_ps[k % 2][:, 0:D], ec.sel[p][:, j, :], msg[p][:, j, :], start=True, stop=False)
                ec.carry(pe, t, p, k).then_inc(sig["summed"], 1)

            def map_and_sum(t, p):
                maps, summing = present(t, T), present(t - 1, T)
                if maps:
                    reach(pe, sig["products"], t + 1)
                    turn(t, p, 0)
                reach(pe, sig["scaled"], t)
                reach(pe, sig["sel_made"], t)
                for k in range(SUB):
                    if maps and k + 1 < SUB:
                        turn(t, p, k + 1)
                    if summing:
                        sums(t - 1, 1 - p, k)
                    if maps:
                        linear(t, p, k)

            rolled(pe, T, [(map_and_sum, 1, 1), (radial, 0)])

        @block.scalar
        def _(act):
            def sigmoid(t, p):
                reach(act, sig["radial"], t + 1)
                reach(act, sig["scaled"], t - 1)
                act.activation(rad[p][:, :, :], rad_ps[:, :, 0:D], ACT.Sigmoid).then_inc(sig["sigmoid_done"], 1)

            def take(t, p, k):
                reach(act, sig["pT"], SUB * t + k + 1)
                reach(act, sig["linear"], SUB * t + k - 1)
                act.activation(pT[k % 2][:, :], pT_ps[k % 2][:, 0:2 * P], ACT.Copy).then_inc(sig["pT_taken"], 1)

            def take_both(t, p):
                for k in range(-1, SUB):
                    if present(t, T) and k + 1 < SUB:
                        take(t, p, k + 1)
                    if present(t - 1, T) and k >= 0:
                        ec.take_out(act, t - 1, 1 - p, k)

            act.wait_ge(sig["out_zeroed"], 2)
            rolled(act, T, [(take_both, 1, 1), (sigmoid, 0)])

        @block.vector
        def _(dve):
            w_scale(dve)

            def products(t, p):
                e4 = pr.edge4[:, bass.ds(t * (SUB * 6), SUB * 6)].rearrange("p (j k) -> p j k", j=SUB)
                rows = ec.rows_in[0][p]
                v = rows[:, :, NS:D].rearrange("p j (i c) -> p j i c", i=3)
                ec.gathered(dve, t, p)
                reach(dve, sig["pT"], SUB * t - SUB)
                reach(dve, sig["products"], t)
                dve.tensor_tensor(ve[:, :, :, :], v, e4[:, :, 1:4].unsqueeze(3).to_broadcast([P, SUB, 3, NV]),
                                  ALU.mult).then_inc(sig["ve"], 1)
                dve.tensor_tensor(prod[p][:, :, 0:NS], rows[:, :, 0:NS], e4[:, :, 0:1].to_broadcast([P, SUB, NS]), ALU.mult)
                dve.tensor_copy(prod[p][:, :, 192:2 * P], rows[:, :, 0:NS])
                dve.wait_ge(sig["ve"], t + 1)
                dve.tensor_tensor(dot[:, :, :], ve[:, :, 0, :], ve[:, :, 1, :], ALU.add).then_inc(sig["dot"], 1)
                dve.tensor_tensor(prod[p][:, :, 96:192].rearrange("p j (i c) -> p j i c", i=3), v,
                                  e4[:, :, 0:1].unsqueeze(3).to_broadcast([P, SUB, 3, NV]), ALU.mult)
                dve.wait_ge(sig["dot"], t + 1)
                dve.tensor_tensor(prod[p][:, :, NS:96], dot[:, :, :], ve[:, :, 2, :], ALU.add).then_inc(sig["products"], 1)

            def scale(t, p):
                ec.make_sel(dve, t, p)
                reach(dve, sig["sigmoid_done"], t + 1)
                reach(dve, sig["linear"], SUB * t + SUB)
                e4 = pr.edge4[:, bass.ds(t * (SUB * 6), SUB * 6)].rearrange("p (j k) -> p j k", j=SUB)
                dve.tensor_tensor(e_s[:, :, :, :], m_ps[:, :, D:192].unsqueeze(2).to_broadcast([P, SUB, 3, NV]),
                                  e4[:, :, 1:4].unsqueeze(3).to_broadcast([P, SUB, 3, NV]), ALU.mult).then_inc(sig["e_s"], 1)
                dve.tensor_tensor(msg[p][:, :, 0:NS], m_ps[:, :, 0:NS], rad[p][:, :, 0:NS], ALU.mult)
                reach(dve, sig["e_s"], 2 * t + 1)
                dve.tensor_tensor(e_s[:, :, :, :], m_ps[:, :, NS:D].rearrange("p j (i c) -> p j i c", i=3), e_s[:, :, :, :],
                                  ALU.add).then_inc(sig["e_s"], 1)
                reach(dve, sig["e_s"], 2 * t + 2)
                dve.tensor_tensor(msg[p][:, :, NS:D].rearrange("p j (i c) -> p j i c", i=3), e_s[:, :, :, :],
                                  rad[p][:, :, NS:D].rearrange("p j (i c) -> p j i c", i=3), ALU.mult).then_inc(sig["scaled"], 1)

            rolled(dve, T, [(products, 0), (scale, 1)])

    finish_pass(nc, sig)


class Norm:

    def __init__(self, pr, ctx, sig, name, parts):
        nc = pr.nc
        self.sig, self.name, self.parts = sig, name, parts
        sb = lambda n, shape: ctx.enter_context(nc.sbuf_tensor(f"{pr.name}_{name}_{n}", shape, F32))
        n = len(parts)
        self.stats = sb("stats", [P, n, SUB, 6])
        self.mean = [sb(f"mean{p}", [P, n, SUB, 2]) for p in range(2)]
        self.var = [sb(f"var{p}", [P, n, SUB]) for p in range(2)]
        self.rstd = [sb(f"rstd{p}", [P, n, SUB]) for p in range(2)]
        self.half = sb("half", [P, n, SUB])
        self.minus_mean = [sb(f"minus_mean{p}", [P, n, SUB]) for p in range(2)]
        self.bias = [sb(f"bias{p}", [P, n, SUB]) for p in range(2)]

    def start(self, pool):
        pool.memset(self.half[:, :, :], -0.5).then_inc(self.sig[f"{self.name}_half"], 1)
        pool.wait_ge(self.sig[f"{self.name}_half"], 1)

    def statistics(self, dve, t, p, z, root_mean_square=False, on_scalar=False):
        sig, n = self.sig, self.name
        for k, (c, width) in enumerate(self.parts):
            for j in range(SUB):
                ins = dve.bn_stats(self.stats[:, k, j, :], z[:, j, c:c + width])
        ins.then_inc(sig[f"{n}_stats"], 1)
        reach_gate(dve, sig[f"{n}_stats"], t + 1, sig["dve_gate"])
        for k in range(len(self.parts)):
            for j in range(SUB):
                ins = dve.bn_aggr(self.mean[p][:, k, j, :], self.stats[:, k, j, :])
        ins.then_inc(sig[f"{n}_mean"], 1)
        dve.wait_ge(sig[f"{n}_mean"], t + 1)
        if root_mean_square:
            m = self.mean[p]
            dve.tensor_tensor(self.var[p][:, 1, :], m[:, 1, :, 0], m[:, 1, :, 0], ALU.mult).then_inc(sig[f"{n}_ms"], 1)
            dve.wait_ge(sig[f"{n}_ms"], 2 * t + 1)
            dve.tensor_tensor(self.var[p][:, 1, :], self.var[p][:, 1, :], m[:, 1, :, 1], ALU.add).then_inc(sig[f"{n}_ms"], 1)
            dve.wait_ge(sig[f"{n}_ms"], 2 * t + 2)
            dve.tensor_scalar(self.var[p][:, 1, :], self.var[p][:, 1, :], 3.0, EPS, ALU.mult, ALU.add)
            dve.tensor_scalar(self.var[p][:, 0, :], m[:, 0, :, 1], EPS, None, ALU.add).then_inc(sig[f"{n}_var"], 1)
        else:
            if on_scalar:
                reach(dve, sig[f"{n}_bias"], t - 1)
                dve.tensor_scalar(self.minus_mean[p][:, :, :], self.mean[p][:, :, :, 0], -1.0, None, ALU.mult)
            dve.tensor_scalar(self.var[p][:, :, :], self.mean[p][:, :, :, 1], EPS, None, ALU.add).then_inc(
                sig[f"{n}_var"], 1)

    def power(self, pool, t, p, on_scalar=False):
        sig, n = self.sig, self.name
        reach_gate(pool, sig[f"{n}_var"], t + 1, sig["pool_gate"])
        reach_gate(pool, sig[f"{n}_applied"], t - 1, sig["pool_gate"])
        pool.tensor_tensor(self.rstd[p][:, :, :], self.var[p][:, :, :], self.half[:, :, :], ALU.pow).then_inc(
            sig[f"{n}_rstd"], 1)
        if on_scalar:
            reach_gate(pool, sig[f"{n}_rstd"], t + 1, sig["pool_gate"])
            pool.tensor_tensor(self.bias[p][:, :, :], self.minus_mean[p][:, :, :], self.rstd[p][:, :, :], ALU.mult).then_inc(
                sig[f"{n}_bias"], 1)

    def apply_on_scalar(self, act, t, p, out, z):
        sig, n = self.sig, self.name
        reach(act, sig[f"{n}_bias"], t + 1)
        for j in range(SUB):
            ins = act.activation(out[:, j, :], z[:, j, :], ACT.Identity, bias=self.bias[p][:, 0, j:j + 1],
                                 scale=self.rstd[p][:, 0, j:j + 1])
        ins.then_inc(sig[f"{n}_applied"], 1)

    def apply(self, dve, t, p, out, z, root_mean_square=False):
        sig, n = self.sig, self.name
        reach(dve, sig[f"{n}_rstd"], t + 1)
        for k, (c, width) in enumerate(self.parts):
            for j in range(SUB):
                to, of, r = out[:, j, c:c + width], z[:, j, c:c + width], self.rstd[p][:, k, j:j + 1]
                if root_mean_square and k == 1:
                    ins = dve.tensor_scalar(to, of, r, None, ALU.mult)
                else:
                    ins = dve.tensor_scalar(to, of, self.mean[p][:, k, j, 0:1], r, ALU.subtract, ALU.mult)
        return ins.then_inc(sig[f"{n}_applied"], 1)


class Turn:

    def __init__(self, pr, ctx, sig, name):
        nc = pr.nc
        self.pr, self.sig, self.name = pr, sig, name
        self.ps = ctx.enter_context(nc.psum_tensor(f"{pr.name}_{name}_ps", [P, SUB, 2 * P], F32))
        self.s = ctx.enter_context(nc.sbuf_tensor(f"{pr.name}_{name}_s", [NS, SUB, P], F32))
        self.v = ctx.enter_context(nc.sbuf_tensor(f"{pr.name}_{name}_v", [3 * NV, SUB, P], F32))

    def turn(self, pe, t, rows):
        for j in range(SUB):
            pe.transpose(self.ps[0:NS, j, 0:P], rows[:, j, 0:NS], self.pr.ident[:, :])
            mm = pe.transpose(self.ps[0:3 * NV, j, P:2 * P], rows[:, j, NS:D], self.pr.ident[:, :])
        mm.then_inc(self.sig[f"{self.name}_turned"], 1)

    def take(self, act, t, used):
        reach(act, self.sig[f"{self.name}_turned"], t + 1)
        reach(act, self.sig[used], t)
        act.activation(self.s[:, :, :], self.ps[0:NS, :, 0:P], ACT.Copy)
        act.activation(self.v[:, :, :], self.ps[0:3 * NV, :, P:2 * P], ACT.Copy).then_inc(
            self.sig[f"{self.name}_taken"], 1)

    def product(self, pe, t, out, w, col, maps, done, tiles=range(SUB)):
        reach(pe, self.sig[f"{self.name}_taken"], t + 1)
        weights = w[:, col:col + maps * D].rearrange("p (k c) -> p k c", k=maps)
        for j in tiles:
            rows = out[:, j - tiles[0], 0:maps * D].rearrange("p (k c) -> p k c", k=maps)
            pe.matmul(rows[:, :, 0:NS], self.s[:, j, :], weights[0:NS, :, 0:NS], start=True, stop=True)
            mm = pe.matmul(rows[:, :, NS:D], self.v[:, j, :], weights[0:3 * NV, :, NS:D], start=True, stop=True)
        mm.then_inc(self.sig[done], 1)


def nodes_layer0(pr):
    nc, T, pr.name = pr.nc, pr.T, "n0"
    with ExitStack() as ctx:
        sig = Signals(nc, ctx)
        two = lambda n, shape: [ctx.enter_context(nc.sbuf_tensor(f"n0_{n}{p}", shape, F32)) for p in range(2)]
        xs, xv, x, agg = two("xs", [NS, STEP]), two("xv", [3 * NV, STEP]), two("x", [P, SUB, D]), two("agg", [P, SUB, AGG_W])
        pre, gate, z, x1 = two("pre", [P, SUB, 192]), two("gate", [P, SUB, 96]), two("z", [P, SUB, D]), two("x1", [P, SUB, D])
        acc = [ctx.enter_context(nc.psum_tensor(f"n0_acc{p}", [P, SUB, 256], F32)) for p in range(2)]
        norm = Norm(pr, ctx, sig, "norm", [(0, D)])
        w, w_zero, w_load, w_scale, w_n = weight_tile(pr, ctx, sig, "n0_w", 192, [
            (0, 0, pr.d["L0_gnn_sc_ws"], NS ** -0.5)] + block_diagonal(96, pr.d["L0_gnn_sc_wv"], NV ** -0.5))
        block = ctx.enter_context(nc.Block())

        @block.sync
        def _(sp):
            w_load(sp)

            def load(t, p):
                reach(sp, sig["self_product"], t - 1)
                sp.dma_start(xs[p][:, :], pr.d["xT"][0:NS, bass.ds(t * STEP, STEP)]).then_inc(sig[f"loaded{p}"], 16)
                sp.dma_start(xv[p][:, :], pr.d["xT"][NS:D, bass.ds(t * STEP, STEP)]).then_inc(sig[f"loaded{p}"], 16)
                reach(sp, sig["summed_up"], t - 1)
                sp.dma_start(agg[p][:, :, :].rearrange("p j c -> p (j c)"), pr.rows(pr.agg, t)).then_inc(sig[f"loaded{p}"], 16)

            def load_x(t, p):
                reach(sp, sig["z"], t - 1)
                sp.dma_start(x[p][:, :, :].rearrange("p j c -> p (j c)"), pr.rows(pr.d["x"], t)).then_inc(sig[f"x_loaded{p}"], 16)

            rolled(sp, T, [(load, 0), (load_x, 1)])

        @block.gpsimd
        def _(pool):
            w_zero(pool)
            norm.start(pool)
            rolled(pool, T, [(lambda t, p: norm.power(pool, t, p, on_scalar=True), 0)])

        @block.tensor
        def _(pe):
            pe.wait_ge(sig["weights_ready"], w_n)

            def product(t, p):
                reach(pe, sig[f"loaded{p}"], dma_count(t, p, 48))
                reach_gate(pe, sig["summed_up"], t - 1, sig["pe_gate"])
                for j in range(SUB):
                    cols = slice(j * P, (j + 1) * P)
                    pe.matmul(acc[p][:, j, 0:96], xs[p][:, cols], w[0:NS, 0:96], start=True, stop=True)
                    mm = pe.matmul(acc[p][:, j, 96:192], xv[p][:, cols], w[0:3 * NV, 96:192], start=True, stop=True)
                mm.then_inc(sig["self_product"], 1)

            rolled(pe, T, [(product, 0)])

        @block.scalar
        def _(act):
            def gates(t, p):
                reach(act, sig["pre"], t + 1)
                reach(act, sig["z"], t - 1)
                act.activation(gate[p][:, :, :], pre[p][:, :, 0:96], ACT.Sigmoid).then_inc(sig["gates"], 1)

            def normalise(t, p):
                reach(act, sig[f"stored{p}"], dma_count(t - 2, p, 16))
                norm.apply_on_scalar(act, t, p, x1[p], z[p])

            def store(t, p):
                reach(act, sig["norm_applied"], t + 1)
                act.dma_start(pr.rows(pr.table_x, t), x1[p][:, :, :].rearrange("p j c -> p (j c)")).then_inc(
                    sig[f"stored{p}"], 16)

            rolled(act, T, [(normalise, 2), (store, 2), (gates, 0)])
            for p in range(2):
                act.wait_ge(sig[f"stored{p}"], 16 * (T // 2))

        @block.vector
        def _(dve):
            w_scale(dve)

            def add_up(t, p):
                reach(dve, sig[f"loaded{p}"], dma_count(t, p, 48))
                reach(dve, sig["self_product"], t + 1)
                dve.tensor_tensor(pre[p][:, :, :], acc[p][:, :, 0:192], agg[p][:, :, :], ALU.add).then_inc(sig["summed_up"], 1)
                reach(dve, sig["summed_up"], t + 1)
                dve.tensor_tensor(pre[p][:, :, :], pre[p][:, :, :],
                                  pr.attr[:, bass.ds(t * SUB, SUB)].unsqueeze(2).to_broadcast([P, SUB, 192]),
                                  ALU.mult).then_inc(sig["pre"], 1)

            def gated(t, p):
                reach(dve, sig["norm_applied"], t - 1)
                reach(dve, sig["gates"], t + 1)
                dve.tensor_tensor(pre[p][:, :, 0:NS], pre[p][:, :, 0:NS], gate[p][:, :, 0:NS], ALU.mult).then_inc(sig["gated"], 1)
                vec = pre[p][:, :, 96:192].rearrange("p j (i c) -> p j i c", i=3)
                dve.tensor_tensor(vec, vec, gate[p][:, :, NS:96].unsqueeze(2).to_broadcast([P, SUB, 3, NV]),
                                  ALU.mult).then_inc(sig["gated"], 1)
                reach(dve, sig["gated"], 2 * t + 2)
                reach(dve, sig[f"x_loaded{p}"], dma_count(t, p, 16))
                dve.tensor_tensor(z[p][:, :, 0:NS], pre[p][:, :, 0:NS], x[p][:, :, 0:NS], ALU.add)
                dve.tensor_tensor(z[p][:, :, NS:D], pre[p][:, :, 96:192], x[p][:, :, NS:D], ALU.add).then_inc(sig["z"], 1)
                reach(dve, sig["z"], t + 1)
                norm.statistics(dve, t, p, z[p], on_scalar=True)

            rolled(dve, T, [(gated, 1), (add_up, 0)])

    finish_pass(nc, sig)


def nodes_layer1(pr):
    nc, T, pr.name = pr.nc, pr.T, "n1"
    with ExitStack() as ctx:
        sig = Signals(nc, ctx)
        two = lambda n, shape: [ctx.enter_context(nc.sbuf_tensor(f"n1_{n}{p}", shape, F32)) for p in range(2)]
        x, agg, h, z, x2 = (two(n, [P, SUB, D]) for n in ("x", "agg", "h", "z", "x2"))
        f = two("f", [P, SUB, 2 * D])
        y_ps = ctx.enter_context(nc.psum_tensor("n1_y", [P, SUB, 256], F32))
        f_ps = ctx.enter_context(nc.psum_tensor("n1_f", [P, 2, 512], F32))
        h_turn = Turn(pr, ctx, sig, "h_turn")
        x_turn = Turn(pr, ctx, sig, "x_turn")
        norm = Norm(pr, ctx, sig, "norm", [(0, D)])
        d, ks, kv = pr.d, NS ** -0.5, NV ** -0.5
        w, w_zero, w_load, w_scale, w_n = weight_tile(
            pr, ctx, sig, "n1_w", 3 * D, [(0, 0, d["L1_gnn_L_s"], ks), (0, D, d["L2_gnn_Wl1_0"], ks), (0, 2 * D, d["L2_gnn_Wsc0"], ks)]
            + block_diagonal(NS, d["L1_gnn_L_v"], kv) + block_diagonal(D + NS, d["L2_gnn_Wl1_1"], kv)
            + block_diagonal(2 * D + NS, d["L2_gnn_Wsc1"], kv))
        block = ctx.enter_context(nc.Block())

        @block.sync
        def _(sp):
            w_load(sp)

            def load(t, p):
                reach(sp, sig["z"], t - 1)
                sp.dma_start(x[p][:, :, :].rearrange("p j c -> p (j c)"), pr.rows(pr.table_x, t)).then_inc(sig[f"loaded{p}"], 16)
                sp.dma_start(agg[p][:, :, :], pr.agg.rearrange("(t p j) c -> t p j c", p=P, j=SUB)[bass.ds(t, 1), :, :, 0:D]
                             .rearrange("a p j c -> (a p) j c")).then_inc(sig[f"loaded{p}"], 16)

            rolled(sp, T, [(load, 0)])

        @block.gpsimd
        def _(pool):
            w_zero(pool)
            norm.start(pool)
            rolled(pool, T, [(lambda t, p: norm.power(pool, t, p), 0)])

        @block.tensor
        def _(pe):
            pe.wait_ge(sig["weights_ready"], w_n)

            def turn_h(t, p):
                reach(pe, sig["h"], t + 1)
                reach_gate(pe, sig["h_turn_taken"], t, sig["pe_gate"])
                h_turn.turn(pe, t, h[p])

            def product_y(t, p):
                reach(pe, sig["z"], t)
                h_turn.product(pe, t, y_ps, w, 0, 1, "y")

            def turn_x(t, p):
                reach(pe, sig["norm_applied"], t + 1)
                reach_gate(pe, sig["x_turn_taken"], t, sig["pe_gate"])
                x_turn.turn(pe, t, x2[p])

            def product_f0(t, p):
                reach(pe, sig["f1_read"], t)
                x_turn.product(pe, t, f_ps, w, D, 2, "f0_product", range(2))

            def product_f1(t, p):
                reach(pe, sig["f0_read"], t + 1)
                x_turn.product(pe, t, f_ps, w, D, 2, "f1_product", range(2, SUB))

            rolled(pe, T, [(turn_h, 1), (product_f1, 3), (product_y, 1), (turn_x, 2), (product_f0, 2)])

        @block.scalar
        def _(act):
            def store(t, p):
                reach(act, sig["tables"], t + 1)
                for k, table in enumerate((pr.table_a, pr.table_b)):
                    act.dma_start(pr.rows(table, t).rearrange("p (j c) -> p j c", j=SUB), f[p][:, :, k * D:(k + 1) * D]).then_inc(
                        sig[f"stored{p}"], 16)

            rolled(act, T, [(lambda t, p: h_turn.take(act, t, "y"), 1), (store, 4),
                            (lambda t, p: x_turn.take(act, t, "f1_product"), 2)])
            for p in range(2):
                act.wait_ge(sig[f"stored{p}"], 32 * (T // 2))

        @block.vector
        def _(dve):
            w_scale(dve)

            def add(t, p):
                reach(dve, sig[f"loaded{p}"], dma_count(t, p, 32))
                reach(dve, sig["h_turn_turned"], t - 1)
                dve.tensor_tensor(h[p][:, :, :], x[p][:, :, :], agg[p][:, :, :], ALU.add).then_inc(sig["h"], 1)

            def residual(t, p):
                reach(dve, sig["norm_applied"], t - 1)
                reach(dve, sig["y"], t + 1)
                dve.tensor_tensor(z[p][:, :, :], y_ps[:, :, 0:D], x[p][:, :, :], ALU.add).then_inc(sig["z"], 1)
                reach(dve, sig["z"], t + 1)
                norm.statistics(dve, t, p, z[p])

            def normalise(t, p):
                reach(dve, sig["x_turn_turned"], t - 1)
                norm.apply(dve, t, p, x2[p], z[p])

            def take_half(t, p, half):
                reach(dve, sig[f"f{half}_product"], t + 1)
                js = slice(2 * half, 2 * half + 2)
                dve.tensor_tensor(f[p][:, js, :], f_ps[:, :, 0:2 * D],
                                  pr.attr[:, bass.ds(t * SUB + 2 * half, 2)].unsqueeze(2).to_broadcast([P, 2, 2 * D]),
                                  ALU.mult).then_inc(sig[f"f{half}_read"], 1)

            def take_f0(t, p):
                reach(dve, sig[f"stored{p}"], dma_count(t - 2, p, 32))
                take_half(t, p, 0)

            def take_f1(t, p):
                take_half(t, p, 1)
                reach(dve, sig["f1_read"], t + 1)
                dve.tensor_tensor(f[p][:, :, D:2 * D], f[p][:, :, D:2 * D], x2[p][:, :, :], ALU.add).then_inc(sig["tables"], 1)

            rolled(dve, T, [(normalise, 2), (take_f0, 3), (add, 0), (take_f1, 3), (residual, 1)])

    finish_pass(nc, sig)


def nodes_layer2(pr):
    nc, T, d, pr.name = pr.nc, pr.T, pr.d, "n2"
    with ExitStack() as ctx:
        sig = Signals(nc, ctx)
        two = lambda n, shape: [ctx.enter_context(nc.sbuf_tensor(f"n2_{n}{p}", shape, F32)) for p in range(2)]
        base, z, x3, hat = (two(n, [P, SUB, D]) for n in ("base", "z", "x3", "hat"))
        agg = two("agg", [P, SUB, AGG_W])
        fa, fb = two("fa", [P, SUB, D]), two("fb", [P, SUB, D])
        share = ctx.enter_context(nc.sbuf_tensor("n2_share", [P, 3, SUB], F32))
        gamma = ctx.enter_context(nc.sbuf_tensor("n2_gamma", [P, D], F32))
        beta = ctx.enter_context(nc.sbuf_tensor("n2_beta", [P, NS], F32))
        f_ps = ctx.enter_context(nc.psum_tensor("n2_f", [P, SUB, 512], F32))
        turn = Turn(pr, ctx, sig, "turn")
        norm = Norm(pr, ctx, sig, "norm", [(0, D)])
        equi = Norm(pr, ctx, sig, "equi", [(0, NS), (NS, 3 * NV)])
        w, w_zero, w_load, w_scale, w_n = weight_tile(
            pr, ctx, sig, "n2_w", 2 * D, [(0, 0, d["L3_gnn_Ws_src"], 1.0), (0, D, d["L3_gnn_Ws_dst"], 1.0)]
            + block_diagonal(NS, d["L3_gnn_Wv_src"], 1.0) + block_diagonal(D + NS, d["L3_gnn_Wv_dst"], 1.0))
        block = ctx.enter_context(nc.Block())

        @block.sync
        def _(sp):
            w_load(sp)
            sp.dma_start(gamma[:, 0:NS], d["L3_gnn_gamma_s"].to_broadcast([P, NS])).then_inc(sig["affine_loaded"], 16)
            sp.dma_start(beta[:, :], d["L3_gnn_beta_s"].to_broadcast([P, NS])).then_inc(sig["affine_loaded"], 16)
            for i in range(3):
                sp.dma_start(gamma[:, NS + NV * i:NS + NV * (i + 1)], d["L3_gnn_gamma_v"].to_broadcast([P, NV])).then_inc(
                    sig["affine_loaded"], 16)

            def load(t, p):
                reach(sp, sig["z"], t - 1)
                sp.dma_start(base[p][:, :, :].rearrange("p j c -> p (j c)"), pr.rows(pr.table_b, t)).then_inc(sig[f"loaded{p}"], 16)
                sp.dma_start(agg[p][:, :, :].rearrange("p j c -> p (j c)"), pr.rows(pr.agg, t)).then_inc(sig[f"loaded{p}"], 16)

            rolled(sp, T, [(load, 0)])

        @block.gpsimd
        def _(pool):
            w_zero(pool)
            norm.start(pool)
            equi.start(pool)
            rolled(pool, T, [(lambda t, p: equi.power(pool, t, p), 1), (lambda t, p: norm.power(pool, t, p), 0)])

        @block.tensor
        def _(pe):
            pe.wait_ge(sig["weights_ready"], w_n)

            def product(t, p):
                reach(pe, sig["hat"], t + 1)
                reach_gate(pe, sig["turn_taken"], t, sig["pe_gate"])
                turn.turn(pe, t, hat[p])
                reach(pe, sig["f_taken"], t)
                turn.product(pe, t, f_ps, w, 0, 2, "f")

            rolled(pe, T, [(product, 2)])

        @block.scalar
        def _(act):
            def take(t, p):
                turn.take(act, t, "f")
                reach(act, sig["f"], t + 1)
                reach(act, sig[f"stored{p}"], dma_count(t - 2, p, 32))
                act.activation(fa[p][:, :, :], f_ps[:, :, 0:D], ACT.Copy)
                act.activation(fb[p][:, :, :], f_ps[:, :, D:2 * D], ACT.Copy).then_inc(sig["f_taken"], 1)

            def store(t, p):
                reach(act, sig["f_taken"], t + 1)
                for table, rows in ((pr.table_a, fa[p]), (pr.table_c, fb[p])):
                    act.dma_start(pr.rows(table, t), rows[:, :, :].rearrange("p j c -> p (j c)")).then_inc(sig[f"stored{p}"], 16)

            def store_x3(t, p):
                reach(act, sig["norm_applied"], t + 1)
                act.dma_start(pr.rows(pr.table_x, t), x3[p][:, :, :].rearrange("p j c -> p (j c)")).then_inc(
                    sig[f"x3_stored{p}"], 16)

            rolled(act, T, [(take, 2), (store_x3, 1), (store, 2)])
            for p in range(2):
                act.wait_ge(sig[f"stored{p}"], 32 * (T // 2))
                act.wait_ge(sig[f"x3_stored{p}"], 16 * (T // 2))

        @block.vector
        def _(dve):
            w_scale(dve)
            dve.wait_ge(sig["affine_loaded"], 16 * 5)

            def residual(t, p):
                s = agg[p]
                reach(dve, sig[f"loaded{p}"], dma_count(t, p, 32))
                dve.tensor_scalar(share[:, 0, :], s[:, :, 1], 1.0, None, ALU.max).then_inc(sig["count"], 1)
                reach(dve, sig["count"], t + 1)
                dve.reciprocal(share[:, 1, :], share[:, 0, :]).then_inc(sig["inverse"], 1)
                reach(dve, sig["inverse"], t + 1)
                dve.tensor_tensor(share[:, 0, :], share[:, 1, :], pr.attr[:, bass.ds(t * SUB, SUB)], ALU.mult).then_inc(sig["share"], 1)
                reach(dve, sig["share"], 3 * t + 1)
                dve.tensor_tensor(share[:, 1, :], share[:, 0, :], share[:, 0, :], ALU.mult).then_inc(sig["share"], 1)
                reach(dve, sig["share"], 3 * t + 2)
                dve.tensor_tensor(share[:, 2, :], share[:, 1, :], s[:, :, 0], ALU.mult).then_inc(sig["share"], 1)
                reach(dve, sig["share"], 3 * t + 3)
                for j in range(SUB):
                    ins = dve.scalar_tensor_tensor(out=z[p][:, j, :], in0=s[:, j, 2:2 + D], scalar=share[:, 2, j:j + 1],
                                                   in1=base[p][:, j, :], op0=ALU.mult, op1=ALU.add)
                ins.then_inc(sig["z"], 1)
                reach(dve, sig["z"], t + 1)
                norm.statistics(dve, t, p, z[p])

            def normalise(t, p):
                reach(dve, sig[f"x3_stored{p}"], dma_count(t - 2, p, 16))
                norm.apply(dve, t, p, x3[p], z[p])
                reach(dve, sig["norm_applied"], t + 1)
                equi.statistics(dve, t, p, x3[p], True)

            def second_norm(t, p):
                reach(dve, sig["turn_turned"], t - 1)
                equi.apply(dve, t, p, hat[p], x3[p], True)
                reach(dve, sig["equi_applied"], t + 1)
                dve.tensor_tensor(hat[p][:, :, :], hat[p][:, :, :], gamma[:, :].unsqueeze(1).to_broadcast([P, SUB, D]),
                                  ALU.mult).then_inc(sig["gamma"], 1)
                reach(dve, sig["gamma"], t + 1)
                dve.tensor_tensor(hat[p][:, :, 0:NS], hat[p][:, :, 0:NS], beta[:, :].unsqueeze(1).to_broadcast([P, SUB, NS]),
                                  ALU.add).then_inc(sig["hat"], 1)

            rolled(dve, T, [(second_norm, 2), (normalise, 1), (residual, 0)])

    finish_pass(nc, sig)


def nodes_layer3(pr):
    nc, T, d, pr.name = pr.nc, pr.T, pr.d, "n3"
    with ExitStack() as ctx:
        sig = Signals(nc, ctx)
        two = lambda n, shape: [ctx.enter_context(nc.sbuf_tensor(f"n3_{n}{p}", shape, F32)) for p in range(2)]
        x, att, z, o = (two(n, [P, SUB, D]) for n in ("x", "att", "z", "o"))
        agg = two("agg", [P, SUB, AGG_W])
        den = ctx.enter_context(nc.sbuf_tensor("n3_den", [P, 2, SUB, HEADS], F32))
        y_ps = ctx.enter_context(nc.psum_tensor("n3_y", [P, SUB, 256], F32))
        turn = Turn(pr, ctx, sig, "turn")
        norm = Norm(pr, ctx, sig, "norm", [(0, D)])
        w, w_zero, w_load, w_scale, w_n = weight_tile(pr, ctx, sig, "n3_w", D, [(0, 0, d["L3_gnn_Wps"], 1.0)]
                                                      + block_diagonal(NS, d["L3_gnn_Wpv"], 1.0))
        block = ctx.enter_context(nc.Block())

        @block.sync
        def _(sp):
            w_load(sp)

            def load(t, p):
                reach(sp, sig["attended"], t - 1)
                sp.dma_start(agg[p][:, :, :].rearrange("p j c -> p (j c)"), pr.rows(pr.agg, t)).then_inc(sig[f"loaded{p}"], 16)

            def load_x(t, p):
                reach(sp, sig["z"], t - 1)
                sp.dma_start(x[p][:, :, :].rearrange("p j c -> p (j c)"), pr.rows(pr.table_x, t)).then_inc(sig[f"x_loaded{p}"], 16)

            rolled(sp, T, [(load, 0), (load_x, 1)])

        @block.gpsimd
        def _(pool):
            w_zero(pool)
            norm.start(pool)
            rolled(pool, T, [(lambda t, p: norm.power(pool, t, p, on_scalar=True), 0)])

        @block.tensor
        def _(pe):
            pe.wait_ge(sig["weights_ready"], w_n)

            def product(t, p):
                reach(pe, sig["attended"], t + 1)
                reach_gate(pe, sig["turn_taken"], t, sig["pe_gate"])
                turn.turn(pe, t, att[p])
                reach(pe, sig["z"], t)
                turn.product(pe, t, y_ps, w, 0, 1, "y")

            rolled(pe, T, [(product, 0)])

        @block.scalar
        def _(act):
            def normalise(t, p):
                reach(act, sig[f"stored{p}"], dma_count(t - 2, p, 16))
                norm.apply_on_scalar(act, t, p, o[p], z[p])

            def store(t, p):
                reach(act, sig["norm_applied"], t + 1)
                act.dma_start(pr.rows(pr.output, t), o[p][:, :, :].rearrange("p j c -> p (j c)")).then_inc(sig[f"stored{p}"], 16)

            rolled(act, T, [(lambda t, p: turn.take(act, t, "y"), 0), (normalise, 2), (store, 2)])
            for p in range(2):
                act.wait_ge(sig[f"stored{p}"], 16 * (T // 2))

        @block.vector
        def _(dve):
            w_scale(dve)

            def attend(t, p):
                reach(dve, sig[f"loaded{p}"], dma_count(t, p, 16))
                reach(dve, sig["turn_turned"], t - 1)
                dve.tensor_scalar(den[:, 0, :, :], agg[p][:, :, D:D + HEADS], 1e-16, None, ALU.add).then_inc(sig["den"], 1)
                reach(dve, sig["den"], t + 1)
                dve.reciprocal(den[:, 1, :, :], den[:, 0, :, :]).then_inc(sig["den_inverse"], 1)
                reach(dve, sig["den_inverse"], t + 1)
                share = den[:, 1, :, :].unsqueeze(3)
                for c, per_head in [(0, 16)] + [(NS + NV * i, 8) for i in range(3)]:
                    cols = slice(c, c + HEADS * per_head)
                    ins = dve.tensor_tensor(att[p][:, :, cols].rearrange("p j (h k) -> p j h k", h=HEADS),
                                            agg[p][:, :, cols].rearrange("p j (h k) -> p j h k", h=HEADS),
                                            share.to_broadcast([P, SUB, HEADS, per_head]), ALU.mult)
                ins.then_inc(sig["attended"], 1)

            def residual(t, p):
                reach(dve, sig["norm_applied"], t - 1)
                reach(dve, sig["y"], t + 1)
                reach(dve, sig[f"x_loaded{p}"], dma_count(t, p, 16))
                dve.scalar_tensor_tensor(out=z[p][:, :, :], in0=x[p][:, :, :], scalar=2.0, in1=y_ps[:, :, 0:D],
                                         op0=ALU.mult, op1=ALU.add).then_inc(sig["z"], 1)
                reach(dve, sig["z"], t + 1)
                norm.statistics(dve, t, p, z[p], on_scalar=True)

            rolled(dve, T, [(attend, 0), (residual, 1)])

    finish_pass(nc, sig)


def tiles_before_first(t):
    if isinstance(t, int):
        return -SUB if t < 0 else SUB * (t + max(t - 1, 0))
    return 2 * SUB * t - SUB


def tiles_before_second(t, T):
    if isinstance(t, int):
        return -SUB if t < 0 else SUB * (min(t + 2, T) + t)
    return 2 * SUB * t + 2 * SUB


def edges_layer3(pr):
    nc, T, d, pr.name = pr.nc, pr.T, pr.d, "l3"
    r3, r2 = 3.0 ** -0.5, 2.0 ** -0.5
    with ExitStack() as ctx:
        sig = Signals(nc, ctx)
        sb = lambda n, shape, dt=F32: ctx.enter_context(nc.sbuf_tensor(f"l3_{n}", shape, dt))
        ps = lambda n, shape: ctx.enter_context(nc.psum_tensor(f"l3_{n}", shape, F32))
        two = lambda n, shape: [sb(f"{n}{p}", shape) for p in range(2)]
        width = D + HEADS
        ec = EdgeCommon(pr, ctx, sig, [(pr.table_a, 0), (pr.table_c, 2)], width, "rows", banks=1)
        tp1 = TensorProduct(pr, ctx, sig, True, "tp1")
        tp2 = TensorProduct(pr, ctx, sig, True, "tp2")
        feat = two("feat", [16, STEP])
        rows = sb("rows", [P, SUB, D + 2 * NV])
        rows2 = sb("rows2", [P, SUB, D + 2 * NV])
        turned = [sb(f"turned{k}", [P, 3 * P]) for k in range(2)]
        leak, relu, logits = two("leak", [P, SUB, NS]), two("relu", [P, SUB, NS]), two("logits", [P, SUB, HEADS])
        leaky = sb("leaky", [P, SUB, NS])
        values, half_tanh, gates = two("values", [P, SUB, P]), two("half_tanh", [P, SUB, 96]), sb("gates", [P, SUB, NV])
        mask, running, top = two("mask", [HEADS, STEP + 1]), sb("running", [HEADS, STEP]), two("top", [HEADS, STEP])
        fall = two("fall", [HEADS, 1])
        below, ex, shrink = sb("below", [P, SUB, HEADS]), two("ex", [P, SUB, HEADS]), two("shrink", [1, HEADS])
        weighted, handed = two("weighted", [P, SUB, width]), two("handed", [1, width])
        e_s, e_h = sb("e_s", [P, SUB, 3, NV]), sb("e_h", [P, SUB, 3, NV])
        dots = sb("dots", [P, NS])
        scale_col = sb("scale_col", [P, 3])
        sval_t = sb("sval_t", [NS, 96])
        wh_ps = ps("wh_ps", [P, SUB, 256])
        a_ps = ps("a_ps", [P, SUB, 256])
        turn_ps = [ps(f"turn_ps{k}", [P, 4 * P]) for k in range(2)]
        tail_ps = ec.o_ps[0][:, 192:192 + SUB * 2 * NV].rearrange("p (j c) -> p j c", j=SUB)
        small_ps = ps("small_ps", [P, STEP])
        c_rbf, c_a, c_v, c_hs, c_hv, c_g = 0, 224, 384, 512, 576, 704
        w, w_zero, w_load, w_scale, w_n = weight_tile(pr, ctx, sig, "l3_w", 736, [
            (0, c_rbf, d["L3_gnn_W_rbf"], 1.0),
            (0, c_a, d["L3_gnn_W_alpha"][0:NS, :], 1.0), (NS, c_a, d["L3_gnn_W_alpha"][NS:96, :], r3),
            (0, c_a + 64, d["L3_gnn_Ws_val"][0:NS, :], 1.0), (NS, c_a + 64, d["L3_gnn_Ws_val"][NS:96, :], r3),
            (0, c_hs, d["L3_gnn_Ws_vlin"][0:NS, :], 1.0), (NS, c_hs, d["L3_gnn_Ws_vlin"][NS:96, :], r3),
            (0, c_g, d["L3_gnn_Wg"], 1.0)] + grouped(c_v, d["L3_gnn_Wv_val"], 1.0, 1.0, r2) + grouped(c_hv, d["L3_gnn_Wv_vlin"], 1.0, 1.0, r2))
        columns = [(0, 0, "w2_ss"), (NS, 0, "w2_vv0")] + [
            (r, c, n) for c in (1, 2) for r, n in ((0, "w2_vs"), (NV, "w2_vv1"))] + [
            (NS, 1, "w2_vs"), (NS + NV, 1, "w2_vv1"), (NS, 2, "w2_sv")]
        block = ctx.enter_context(nc.Block())

        @block.sync
        def _(sp):
            w_load(sp)
            for r, c, n in columns:
                v = d[f"L3_gnn_{n}"].rearrange("a c -> c a")
                sp.dma_start(scale_col[r:r + v.shape[0], c:c + 1], v).then_inc(sig["constants"], 16)
            sp.dma_start(dots[:, :], d["alpha_dot"].to_broadcast([P, NS])).then_inc(sig["constants"], 16)
            sp.dma_start(sval_t[:, :], d["Ws_val_T"]).then_inc(sig["constants"], 16)

            def load(t, p):
                reach(sp, sig["w"], t - 1)
                sp.dma_start(feat[p][:, :], d["edge_attr_16"][:, bass.ds(t * STEP, STEP)]).then_inc(sig[f"feat_loaded{p}"], 16)

            def load_mask(t, p):
                reach(sp, sig["fall"], t - 1)
                sp.dma_start(mask[p][:, :], pr.mask_rows[bass.ds(t, 1), :].to_broadcast([HEADS, STEP + 1])).then_inc(
                    sig[f"mask_loaded{p}"], 16)

            rolled(sp, T, [(load, 0), (load_mask, 2), (lambda t, p: ec.load_dst(sp, t, p), 3)])

        @block.gpsimd
        def _(pool):
            w_zero(pool)
            ec.start_out(pool)
            for tp in (tp1, tp2):
                for p in range(2):
                    pool.memset(tp.msg[p][:, :, :], 0.0).then_inc(sig["msg_zeroed"], 1)
            pool.memset(top[1][:, :], -BIG).then_inc(sig["msg_zeroed"], 1)
            rolled(pool, T, [(lambda t, p: ec.gather(pool, t, p), 0), (lambda t, p: ec.scatter(pool, t, p), 6)])
            ec.all_scattered(pool)

        @block.tensor
        def _(pe):
            pe.wait_ge(sig["weights_ready"], w_n)
            pe.wait_ge(sig["constants"], 16 * (len(columns) + 2))
            pe.wait_ge(sig["out_zeroed"], 2)
            pe.matmul(wh_ps[0:96, 0, 0:NV], sval_t[:, :], w[0:NS, c_g:c_g + NV], start=True, stop=True).then_inc(sig["gate_map"], 1)
            pe.wait_ge(sig["maps_made"], 5)

            def weights(t, p):
                reach(pe, sig[f"feat_loaded{p}"], dma_count(t, p, 16))
                reach(pe, sig["messages"], t)
                reach(pe, sig["weighted"], t - 2)
                for j in range(SUB):
                    mm = pe.matmul(wh_ps[:, j, 0:224], feat[p][:, j * P:(j + 1) * P], w[0:16, c_rbf:c_rbf + 224],
                                   start=True, stop=True)
                mm.then_inc(sig["w"], 1)

            def turn(t, k, msg, taken):
                j = SUB - 1 - k
                reach(pe, sig["turn_taken"], taken - 1)
                for q in range(3):
                    mm = pe.transpose(turn_ps[k % 2][:, q * P:(q + 1) * P], msg[:, j, q * P:(q + 1) * P], pr.ident[:, :])
                mm.then_inc(sig["turned"], 1)

            def logits_values(t, p):
                reach(pe, sig["messages"], t + 1)
                reach(pe, sig["values_taken"], t)
                reach(pe, sig["out_ready"], SUB * (t - 2))
                base = tiles_before_first(t)
                for k in range(SUB + 1):
                    if k < SUB:
                        turn(t, k, tp1.msg[p], base + k)
                    if k:
                        j, m = SUB - k, turned[(k - 1) % 2]
                        reach(pe, sig["turn_taken"], base + k)
                        pe.matmul(a_ps[:, j, 0:D], m[:, 0:P], w[:, c_a:c_a + D], start=True, stop=True)
                        pe.matmul(a_ps[:, j, D:D + NS], m[:, P:2 * P], w[:, c_v:c_v + NS], start=True, stop=True)
                        mm = pe.matmul(tail_ps[:, j, :], m[:, 2 * P:3 * P], w[:, c_v + NS:c_v + P], start=True, stop=True)
                        mm.then_inc(sig["mapped"], 1)

            def head_tile(t, k, base):
                j, m = SUB - 1 - k, turned[k % 2]
                reach(pe, sig["turn_taken"], base + k + 1)
                pe.matmul(wh_ps[:, j, 0:NS], m[:, 0:P], w[:, c_hs:c_hs + NS], start=True, stop=True)
                for q in range(2):
                    mm = pe.matmul(wh_ps[:, j, NS * (1 + q):NS * (2 + q)], m[:, (1 + q) * P:(2 + q) * P],
                                   w[:, c_hv + NS * q:c_hv + NS * (1 + q)], start=True, stop=True)
                mm.then_inc(sig["mapped"], 1)

            def sums(t, p, k):
                j = SUB - 1 - k
                reach(pe, sig["out_ready"], SUB * t + k)
                pe.matmul(ec.o_ps[k % 2][:, 0:width], ec.sel[p][:, j, :], weighted[p][:, j, :], start=True, stop=False)
                ec.carry(pe, t, p, k, handed[p][:, :]).then_inc(sig["summed"], 1)

            def heads_and_sums(t, p):
                heads, summing, base = present(t, T), present(t - 1, T), tiles_before_second(t, T)
                if heads:
                    reach(pe, sig["messages2"], t + 1)
                    reach(pe, sig["messages"], t + 3 if not isinstance(t, int) else min(t + 3, T))
                    turn(t, 0, tp2.msg[p], base)
                if summing:
                    reach(pe, sig["values_taken"], t + 2 if not isinstance(t, int) else min(t + 2, T))
                    reach(pe, sig["weighted"], t)
                    reach(pe, sig["handed"], t)
                    reach(pe, sig["sel_made"], t)
                for k in range(SUB):
                    if heads and k + 1 < SUB:
                        turn(t, k + 1, tp2.msg[p], base + k + 1)
                    if summing:
                        sums(t - 1, 1 - p, k)
                    if heads:
                        head_tile(t, k, base)

            def turn_logits(t, p):
                reach(pe, sig["logits"], t + 1)
                reach(pe, sig["below"], t)
                reach_gate(pe, sig["shrink"], t, sig["pe_gate"])
                for j in range(SUB):
                    mm = pe.transpose(small_ps[0:HEADS, j * P:(j + 1) * P], logits[p][:, j, :], pr.ident[:, :])
                mm.then_inc(sig["logits_turned"], 1)

            def turn_top(t, p):
                reach_gate(pe, sig["fall"], t + 1, sig["pe_gate"])
                for j in range(SUB):
                    pe.transpose(small_ps[:, HEADS * j:HEADS * (j + 1)], top[p][:, j * P:(j + 1) * P], pr.ident[0:HEADS, 0:HEADS])
                pe.transpose(small_ps[0:1, 32:36], fall[p][:, :], pr.ident[0:HEADS, 0:HEADS]).then_inc(sig["top_turned"], 1)

            rolled(pe, T, [(turn_top, 4), (heads_and_sums, 4, 1), (turn_logits, 3), (weights, 1), (logits_values, 2)])

        @block.scalar
        def _(act):
            def take(k, base):
                reach(act, sig["turned"], base + k + 1)
                reach(act, sig["mapped"], base + k - 1)
                act.activation(turned[k % 2][:, :], turn_ps[k % 2][:, 0:3 * P], ACT.Copy).then_inc(sig["turn_taken"], 1)

            def take_first(t, p):
                for k in range(SUB):
                    take(k, tiles_before_first(t))

            def take_second(t, p):
                for k in range(-1, SUB):
                    if present(t, T) and k + 1 < SUB:
                        take(k + 1, tiles_before_second(t, T))
                    if present(t - 1, T) and k >= 0:
                        ec.take_out(act, t - 1, 1 - p, k)

            def exponentials(t, p):
                reach(act, sig["below"], t + 1)
                reach(act, sig["weighted"], t - 1)
                act.activation(ex[p][:, :, :], below[:, :, :], ACT.Exp).then_inc(sig["ex"], 1)
                reach(act, sig["top_turned"], t + 1)
                reach(act, sig["handed"], t - 1)
                act.activation(shrink[p][:, :], small_ps[0:1, 32:36], ACT.Exp).then_inc(sig["shrink"], 1)

            def gate(t, p):
                reach(act, sig["mapped"], tiles_before_first(t) + SUB)
                reach(act, sig["values"], t - 1)
                act.activation(leak[p][:, :, :], a_ps[:, :, 0:NS], ACT.Copy, scale=0.2)
                act.activation(relu[p][:, :, :], a_ps[:, :, 0:NS], ACT.Relu, scale=0.8).then_inc(sig["relu"], 1)
                act.activation(half_tanh[p][:, :, :], a_ps[:, :, NS:D], ACT.Tanh, scale=0.5)
                act.activation(values[p][:, :, 0:NS], a_ps[:, :, D:D + NS], ACT.Copy)
                act.activation(values[p][:, :, NS:P], tail_ps[:, :, :], ACT.Copy).then_inc(sig["values_taken"], 1)

            act.wait_ge(sig["out_zeroed"], 2)
            rolled(act, T, [(exponentials, 4), (take_second, 4, 1), (take_first, 2), (gate, 2)])

        @block.vector
        def _(dve):
            w_scale(dve)
            dve.wait_ge(sig["constants"], 16 * (len(columns) + 2))
            dve.wait_ge(sig["gate_map"], 1)
            dve.wait_ge(sig["weights_ready"], w_n)
            dve.tensor_copy(w[0:NS, c_a + P:c_a + D], wh_ps[0:NS, 0, 0:NV]).then_inc(sig["maps_made"], 1)
            dve.tensor_scalar(w[NS:96, c_a + P:c_a + D], wh_ps[NS:96, 0, 0:NV], r3, None, ALU.mult).then_inc(sig["maps_made"], 1)
            dve.tensor_scalar(w[0:96, c_hs:c_hs + NS], w[0:96, c_hs:c_hs + NS], scale_col[0:96, 0:1], None, ALU.mult).then_inc(
                sig["maps_made"], 1)
            for q in range(2):
                half = w[:, c_hv + NS * q:c_hv + NS * (1 + q)]
                dve.tensor_scalar(half, half, scale_col[:, 1 + q:2 + q], None, ALU.mult).then_inc(sig["maps_made"], 1)
            dve.wait_ge(sig["msg_zeroed"], 5)

            def e_i(t):
                e4 = pr.edge4[:, bass.ds(t * (SUB * 6), SUB * 6)].rearrange("p (j k) -> p j k", j=SUB)
                return e4[:, :, 1:4].unsqueeze(3).to_broadcast([P, SUB, 3, NV])

            def subtract_top(t, p):
                reach(dve, sig["top_turned"], t + 1)
                reach(dve, sig["ex"], t)
                dve.tensor_tensor(below[:, :, :], logits[p][:, :, :],
                                  small_ps[:, 0:SUB * HEADS].rearrange("p (j h) -> p j h", j=SUB),
                                  ALU.subtract).then_inc(sig["below"], 1)

            def first_product(t, p):
                a, b = ec.rows_in[0][p], ec.rows_in[1][p]
                ec.gathered(dve, t, p)
                dve.tensor_tensor(rows[:, :, D:D + 2 * NV], a[:, :, NS:NS + 2 * NV], b[:, :, NS:NS + 2 * NV], ALU.add)
                dve.tensor_tensor(rows[:, :, 0:D], a[:, :, :], b[:, :, :], ALU.add).then_inc(sig["rows"], 1)
                reach(dve, sig["rows"], t + 1)
                reach(dve, sig["w"], t + 1)
                reach(dve, sig["mapped"], tiles_before_first(t - 2) + SUB)
                tp1.emit(dve, t, p, rows, wh_ps, "messages")

            def softmax_values(t, p):
                reach(dve, sig["relu"], t + 1)
                dve.tensor_tensor(leaky[:, :, :], leak[p][:, :, :], relu[p][:, :, :], ALU.add).then_inc(sig["leaky"], 1)
                reach(dve, sig["leaky"], t + 1)
                dve.tensor_tensor(leaky[:, :, :], leaky[:, :, :], dots[:, :].unsqueeze(1).to_broadcast([P, SUB, NS]),
                                  ALU.mult).then_inc(sig["dotted"], 1)
                reach(dve, sig["values_taken"], t + 1)
                dve.tensor_scalar(gates[:, :, :], half_tanh[p][:, :, NS:96], 0.5, 0.5, ALU.mult, ALU.add).then_inc(sig["gates"], 1)
                dve.tensor_tensor(e_s[:, :, :, :], values[p][:, :, 96:P].unsqueeze(2).to_broadcast([P, SUB, 3, NV]), e_i(t),
                                  ALU.mult).then_inc(sig["e_s"], 1)
                reach(dve, sig["dotted"], t + 1)
                dve.tensor_reduce(logits[p][:, :, :], leaky[:, :, :].rearrange("p j (h k) -> p j h k", h=HEADS), AXX,
                                  ALU.add).then_inc(sig["logits"], 1)
                reach(dve, sig["e_s"], 2 * t + 1)
                dve.tensor_tensor(e_s[:, :, :, :], values[p][:, :, 0:96].rearrange("p j (i c) -> p j i c", i=3), e_s[:, :, :, :],
                                  ALU.add).then_inc(sig["e_s"], 1)
                reach(dve, sig["mapped"], tiles_before_second(t - 2, T) + SUB)
                dve.tensor_scalar(tp2.scalars(p), half_tanh[p][:, :, 0:NS], 0.5, 0.5, ALU.mult, ALU.add)
                reach(dve, sig["gates"], t + 1)
                reach(dve, sig["e_s"], 2 * t + 2)
                v5 = rows2[:, :, NS:D + 2 * NV].rearrange("p j (i c) -> p j i c", i=5)
                g = gates[:, :, :].unsqueeze(2)
                dve.tensor_tensor(v5[:, :, 3:5, :], e_s[:, :, 0:2, :], g.to_broadcast([P, SUB, 2, NV]), ALU.mult)
                dve.tensor_tensor(v5[:, :, 0:3, :], e_s[:, :, :, :], g.to_broadcast([P, SUB, 3, NV]), ALU.mult).then_inc(
                    sig["values"], 1)
                reach(dve, sig["values"], t + 1)
                tp2.emit(dve, t, p, rows2, None, "messages2")

            def maxima(t, p):
                reach(dve, sig["logits_turned"], t + 1)
                reach(dve, sig[f"mask_loaded{p}"], dma_count(t, p, 16))
                reach(dve, sig["top"], t)
                dve.tensor_tensor_scan(out=running[:, ::-1], data0=mask[p][:, STEP:0:-1], data1=small_ps[0:HEADS, ::-1],
                                       initial=top[1 - p][:, 0:1], op0=ALU.min, op1=ALU.max).then_inc(sig["running"], 1)
                reach(dve, sig["running"], t + 1)
                reach(dve, sig["top_turned"], t - 1)
                dve.tensor_tensor_scan(out=top[p][:, :], data0=mask[p][:, 0:STEP], data1=running[:, :], initial=-BIG,
                                       op0=ALU.min, op1=ALU.max).then_inc(sig["top"], 1)
                reach(dve, sig["top"], t + 1)
                dve.tensor_scalar(fall[p][:, :], top[1 - p][:, 0:1], top[p][:, STEP - 1:STEP], 0.0, ALU.subtract,
                                  ALU.min).then_inc(sig["fall"], 1)

            def weigh(t, p):
                reach(dve, sig["ex"], t + 1)
                reach(dve, sig["mapped"], tiles_before_second(t, T) + SUB)
                by_head = lambda x: x.rearrange("p j (h k) -> p j h k", h=HEADS)
                e = ex[p][:, :, :].unsqueeze(3)
                dve.tensor_tensor(e_h[:, :, :, :], wh_ps[:, :, D:192].unsqueeze(2).to_broadcast([P, SUB, 3, NV]), e_i(t),
                                  ALU.mult).then_inc(sig["e_h"], 1)
                dve.tensor_tensor(by_head(weighted[p][:, :, 0:NS]), by_head(wh_ps[:, :, 0:NS]),
                                  e.to_broadcast([P, SUB, HEADS, 16]), ALU.mult)
                reach(dve, sig["e_h"], 2 * t + 1)
                dve.tensor_tensor(e_h[:, :, :, :], wh_ps[:, :, NS:D].rearrange("p j (i c) -> p j i c", i=3), e_h[:, :, :, :],
                                  ALU.add).then_inc(sig["e_h"], 1)
                reach(dve, sig["e_h"], 2 * t + 2)
                for i in range(3):
                    dve.tensor_tensor(by_head(weighted[p][:, :, NS + NV * i:NS + NV * (i + 1)]), by_head(e_h[:, :, i, :]),
                                      e.to_broadcast([P, SUB, HEADS, 8]), ALU.mult)
                dve.tensor_copy(weighted[p][:, :, D:width], ex[p][:, :, :]).then_inc(sig["weighted"], 1)

            def hand_down(t, p):
                reach(dve, sig["shrink"], t + 1)
                reach(dve, sig["out_ready"], SUB * t)
                above = ec.out[1 - p][0:1, 0, :]
                f = shrink[p][:, :].unsqueeze(2)
                for c, per_head in [(0, 16)] + [(NS + NV * i, 8) for i in range(3)] + [(D, 1)]:
                    cols = slice(c, c + HEADS * per_head)
                    ins = dve.tensor_tensor(handed[p][:, cols].rearrange("p (h k) -> p h k", h=HEADS),
                                            above[:, cols].rearrange("p (h k) -> p h k", h=HEADS),
                                            f.to_broadcast([1, HEADS, per_head]), ALU.mult)
                ins.then_inc(sig["handed"], 1)

            rolled(dve, T, [(lambda t, p: ec.make_sel(dve, t, p), 4), (subtract_top, 4), (softmax_values, 3),
                            (weigh, 4), (maxima, 3), (hand_down, 4), (first_product, 1)])

    finish_pass(nc, sig)


def build(nc, d, out, T):
    with ExitStack() as ctx:
        pr = Program(nc, d, T, out, ctx)
        n = T * STEP
        pr.table_a = nc.dram_tensor("table_a", (n, D), F32, kind="Internal").ap()
        pr.table_b = nc.dram_tensor("table_b", (n, D), F32, kind="Internal").ap()
        pr.table_c = nc.dram_tensor("table_c", (n, D), F32, kind="Internal").ap()
        pr.table_x = nc.dram_tensor("table_x", (n, D), F32, kind="Internal").ap()
        pr.cont_rows = nc.dram_tensor("cont_rows", (T, STEP), F32, kind="Internal").ap()
        pr.mask_rows = nc.dram_tensor("mask_rows", (T, STEP + 1), F32, kind="Internal").ap()
        pr.agg = nc.dram_tensor("agg", (n, AGG_W), F32, kind="Internal").ap()
        pr.rows = lambda table, t: table.rearrange("(t p j) c -> t p (j c)", p=P, j=SUB)[bass.ds(t, 1)].rearrange("a p c -> (a p) c")
        pr.ident = ctx.enter_context(nc.sbuf_tensor("ident", [P, P], F32))
        pr.index = ctx.enter_context(nc.sbuf_tensor("index", [P, T * 3 * SUB], I32))
        pr.dst_f = ctx.enter_context(nc.sbuf_tensor("dst_f", [P, T * SUB], F32))
        pr.edge4 = ctx.enter_context(nc.sbuf_tensor("edge4", [P, T * SUB * 6], F32))
        pr.attr = ctx.enter_context(nc.sbuf_tensor("attr", [P, T * SUB], F32))
        prepare(pr)
        r3, r2 = 3.0 ** -0.5, 2.0 ** -0.5
        k_s, k_v = 0.25 * 96 ** -0.5, 0.25 * 128 ** -0.5
        l2s, l2v = d["L0_gnn_lin2_ws"], d["L0_gnn_lin2_wv"]
        edges_conv(pr, "l0", d["L0_gnn_fc_w1"], d["L0_gnn_fc_w2"], NS, d["edge_attr_64"], True,
                   [(0, 0, l2s[0:NS, :], k_s), (NS, 0, l2s[NS:96, :], k_s * r3)],
                   l2v, (k_v, k_v, k_v * r2), 96, [(0, 96, 0)], 96)
        nodes_layer0(pr)
        edges_layer1(pr)
        nodes_layer1(pr)
        k_m = 96 ** -0.5
        wa, ws, wv = d["L2_gnn_Wa"], d["L2_gnn_Wl2_s"], d["L2_gnn_Wl2_v"]
        edges_conv(pr, "l2", d["L2_gnn_Wfc1"], d["L2_gnn_Wfc2"], 16, d["edge_attr_16"], False,
                   [(0, 0, wa[0:NS, :], k_m), (NS, 0, wa[NS:96, :], k_m * r3), (0, 1, ws[0:NS, :], k_m),
                    (NS, 1, ws[NS:96, :], k_m * r3)],
                   wv, (k_m, k_m, 0.0), NS + 1, [(0, 1, 0), (1, NS, 2)], NS + 2)
        nodes_layer2(pr)
        edges_layer3(pr)
        nodes_layer3(pr)


WEIGHTS = """
L0_gnn_lin1_ws L0_gnn_lin1_wv L0_gnn_fc_w1 L0_gnn_fc_w2 L0_gnn_sc_ws L0_gnn_sc_wv L0_gnn_lin2_ws
L0_gnn_lin2_wv L1_gnn_W_ss L1_gnn_W_sv L1_gnn_W_vs L1_gnn_W_vv L1_gnn_L_s L1_gnn_L_v L2_gnn_Wfc1 L2_gnn_Wfc2
L2_gnn_Wsc0 L2_gnn_Wsc1 L2_gnn_Wl1_0 L2_gnn_Wl1_1 L2_gnn_Wl2_s L2_gnn_Wl2_v L2_gnn_Wa L3_gnn_gamma_s
L3_gnn_beta_s L3_gnn_gamma_v L3_gnn_Ws_src L3_gnn_Wv_src L3_gnn_Ws_dst L3_gnn_Wv_dst L3_gnn_W_rbf
L3_gnn_W_alpha L3_gnn_alpha_dot L3_gnn_Ws_val L3_gnn_Wv_val L3_gnn_Wg L3_gnn_w2_ss L3_gnn_w2_sv L3_gnn_w2_vs
L3_gnn_w2_vv0 L3_gnn_w2_vv1 L3_gnn_Ws_vlin L3_gnn_Wv_vlin L3_gnn_Wps L3_gnn_Wpv
""".split()


def kernel(**inputs):
    import concourse.bacc as bacc
    from concourse.bass_utils import run_bass_kernel_spmd

    a = {k: np.asarray(v) for k, v in inputs.items()}
    n, e = a["x"].shape[0], a["src"].shape[0]
    steps = -(-max(n, e) // STEP)
    steps += steps % 2
    size = steps * STEP

    def padded(v, fill=0):
        return np.concatenate([v, np.full((size - v.shape[0],) + v.shape[1:], fill, v.dtype)])

    def by_component(v):
        vec = v[..., NS:].reshape(v.shape[:-1] + (NV, 3))
        return np.concatenate([v[..., :NS], np.swapaxes(vec, -1, -2).reshape(v.shape[:-1] + (3 * NV,))], -1)

    def steps_down(v):
        v = v.reshape((steps, SUB, P) + v.shape[1:])[::-1]
        return np.moveaxis(v, 2, 0)

    def columns_down(v):
        c = v.shape[1]
        return np.ascontiguousarray(v.reshape(steps, STEP, c)[::-1].reshape(size, c).T)

    src, dst = padded(a["src"]), padded(a["dst"], n)
    before = np.concatenate([np.full(1, -1, dst.dtype), dst[:-1]])
    index = np.stack([steps_down(src), steps_down(before), steps_down(dst)], 2)
    around = np.concatenate([np.full(1, -1, dst.dtype), dst, np.full(1, -2, dst.dtype)])
    e4 = steps_down(padded(a["edge_attr_4"]))
    x = padded(by_component(a["x"]))
    d = {
        "x": x,
        "xT": np.ascontiguousarray(x.reshape(steps, P, SUB, D).transpose(3, 0, 2, 1).reshape(D, size)),
        "node_attr": np.ascontiguousarray(padded(a["node_vec1"]).reshape(steps, P, SUB).transpose(1, 0, 2).reshape(P, -1)),
        "edge_index": np.ascontiguousarray(index.reshape(P, -1)),
        "dst_rows": np.ascontiguousarray(np.stack([around[t * STEP:(t + 1) * STEP + 2] for t in range(steps)])[::-1]),
        "edge_attr_4": np.ascontiguousarray(np.concatenate([e4, e4[..., 1:3]], -1).reshape(P, -1)),
        "edge_attr_16": columns_down(padded(a["edge_attr_16"])),
        "edge_attr_64": columns_down(padded(a["edge_attr_64"])),
        "identity": np.eye(P, dtype=np.float32),
        "one": np.ones((1, 1), np.float32),
        "alpha_dot": a["L3_gnn_alpha_dot"].reshape(1, NS),
        "Ws_val_T": np.ascontiguousarray(a["L3_gnn_Ws_val"].T),
        "L1_rad": np.concatenate([by_component(a["L1_gnn_W_rad"].T), by_component(a["L1_gnn_b_rad"][None])]),
    }
    for k in WEIGHTS:
        d[k] = a[k].reshape(-1, a[k].shape[-1])
    nc = bacc.Bacc("TRN2", target_bir_lowering=False, num_devices=1)
    aps = {k: nc.dram_tensor(f"in_{k}", v.shape, mybir.dt.from_np(v.dtype), kind="ExternalInput").ap() for k, v in d.items()}
    out = nc.dram_tensor("out", (size, D), F32, kind="ExternalOutput").ap()
    build(nc, aps, out, steps)
    got = run_bass_kernel_spmd(nc, [{f"in_{k}": v for k, v in d.items()}], core_ids=[0]).results[0]["out"][:n]
    vec = got[:, NS:].reshape(n, 3, NV)
    return np.concatenate([got[:, :NS], np.swapaxes(vec, 1, 2).reshape(n, 3 * NV)], 1)
```
